# Optimizing a Trainium2 kernel written in Bass

```python
import numpy as np
import jax
import jax.numpy as jnp

def _softmax(x, axis=-1):
    return jax.nn.softmax(x, axis=axis)

def _gelu(x):
    return jax.nn.gelu(x, approximate=True)

def _silu(x):
    return jax.nn.silu(x)

def _sigmoid(x):
    return jax.nn.sigmoid(x)

def _layernorm(x, axis=-1, eps=1e-05):
    m = jnp.mean(x, axis=axis, keepdims=True)
    v = jnp.var(x, axis=axis, keepdims=True)
    return (x - m) / jnp.sqrt(v + eps)

def _scatter_add(tgt, idx, src, axis=0):
    return tgt.at[idx].add(src)

def _segment_sum(src, seg, n):
    return jax.ops.segment_sum(src, seg, n)
kernel_name = 'mk_decoder_postln_d1_seqx_r4_af434f'

def setup_inputs(seed: int=0):
    np.random.seed(seed)
    _w = jnp.asarray

    def _rec_inputs():
        import jax
        import jax.numpy as jnp
        _rk = jax.random.key(seed)
        x = 7.22e-05 + 1 * jax.random.normal(jax.random.fold_in(_rk, 1), (8, 256, 512), jnp.float32)
        _lenS = 256 - jax.random.randint(jax.random.fold_in(_rk, 7), (8,), 0, max(1, 256 // 4) + 1, jnp.int32)
        _lenS2 = 256 - jax.random.randint(jax.random.fold_in(_rk, 8), (8,), 0, max(1, 256 // 4) + 1, jnp.int32)
        _ctx_512P = jax.random.normal(jax.random.fold_in(_rk, 11), (8, 16, 128), jnp.float32)
        _ctx_512c = jax.random.dirichlet(jax.random.fold_in(_rk, 511), 0.3 * jnp.ones((16,), jnp.float32), (8, 256))
        _ctx_512t = jnp.einsum('bsk,bkd->bsd', _ctx_512c, _ctx_512P)
        _ctx_512t = _ctx_512t * jax.lax.rsqrt(jnp.mean(jnp.square(_ctx_512t)) + 1e-12) * 0.953939
        ctx_512 = -0.000514642 + 1.00011 * (_ctx_512t + 0.3 * jax.random.normal(jax.random.fold_in(_rk, 611), (8, 256, 128), jnp.float32))
        return (x, ctx_512)
    x, ctx_512 = _rec_inputs()

    def _L0_attn_setup():
        import jax, jax.numpy as jnp
        import numpy as np
        from jax import lax
        B, T, D_MODEL = (4, 512, 512)
        EXPAND, D_CONV = (2, 4)
        D_INNER = D_MODEL * EXPAND

        def _forward(x, w_in, w_out, conv_w, conv_b, D):
            x_proj = jnp.einsum('btc,dc->btd', x, w_in)
            xi, gate = jnp.split(x_proj, 2, axis=-1)
            xc = jnp.transpose(xi, (0, 2, 1))
            xc = lax.conv_general_dilated(xc, conv_w, window_strides=(1,), padding=[(D_CONV - 1, 0)], dimension_numbers=('NCH', 'OIH', 'NCH'), feature_group_count=D_INNER) + conv_b[None, :, None]
            xc = jnp.transpose(xc, (0, 2, 1))
            h = jax.nn.silu(xc) * D[None, None, :] * jax.nn.silu(gate)
            return jnp.einsum('btd,cd->btc', h, w_out)
        key = jax.random.key(seed)
        ks = jax.random.split(key, 5)
        x = jax.random.normal(ks[0], (B, T, D_MODEL), dtype=jnp.float32)
        w_in = jax.random.normal(ks[1], (2 * D_INNER, D_MODEL), dtype=jnp.float32) * D_MODEL ** (-0.5)
        w_out = jax.random.normal(ks[2], (D_MODEL, D_INNER), dtype=jnp.float32) * D_INNER ** (-0.5)
        conv_w = jax.random.normal(ks[3], (D_INNER, 1, D_CONV), dtype=jnp.float32) * D_CONV ** (-0.5)
        conv_b = jax.random.normal(ks[4], (D_INNER,), dtype=jnp.float32) * 0.02
        D = jnp.ones((D_INNER,), dtype=jnp.float32)
        return {'x': x, 'w_in': w_in, 'w_out': w_out, 'conv_w': conv_w, 'conv_b': conv_b, 'D': D}
    _L0_attn_all = _L0_attn_setup()
    _L0_attn_in = {k: v for k, v in _L0_attn_all.items() if k in ('w_in', 'w_out', 'conv_w', 'conv_b', 'D')}
    del _L0_attn_all

    def _L0_xattn_setup():
        import jax, jax.numpy as jnp
        import numpy as np
        B, S, H, NH, L = (2, 512, 512, 16, 128)
        HD = H // NH
        key = jax.random.key(seed)
        k1, k2, k3, k4, k5 = jax.random.split(key, 5)
        scale = 0.02
        return {'q': jax.random.normal(k1, (B, S, H), dtype=jnp.float32), 'latent_kv': jax.random.normal(k2, (B, S, L), dtype=jnp.float32), 'Wq': jax.random.normal(k3, (H, H), dtype=jnp.float32) * scale, 'Wkv_expand': jax.random.normal(k4, (2 * H, L), dtype=jnp.float32) * scale, 'Wout': jax.random.normal(k5, (H, H), dtype=jnp.float32) * scale}
    _L0_xattn_all = _L0_xattn_setup()
    _L0_xattn_in = {k: v for k, v in _L0_xattn_all.items() if k in ('Wq', 'Wkv_expand', 'Wout')}
    del _L0_xattn_all

    def _L0_ffn_setup():
        import jax, jax.numpy as jnp
        import numpy as np
        E = 8
        TOP_K = 2
        D = 512
        DE = 352
        DS = 704
        B, S = (2, 512)
        key = jax.random.key(seed)
        ks = jax.random.split(key, 8)
        std = 0.02
        return {'x': jax.random.normal(ks[0], (B, S, D), jnp.float32), 'W_router': jax.random.normal(ks[1], (D, E), jnp.float32) * std, 'We_gate': jax.random.normal(ks[2], (E, D, DE), jnp.float32) * std, 'We_up': jax.random.normal(ks[3], (E, D, DE), jnp.float32) * std, 'We_down': jax.random.normal(ks[4], (E, DE, D), jnp.float32) * std, 'Ws_gate': jax.random.normal(ks[5], (D, DS), jnp.float32) * std, 'Ws_up': jax.random.normal(ks[6], (D, DS), jnp.float32) * std, 'Ws_down': jax.random.normal(ks[7], (DS, D), jnp.float32) * std}
    _L0_ffn_all = _L0_ffn_setup()
    _L0_ffn_in = {k: v for k, v in _L0_ffn_all.items() if k in ('W_router', 'We_gate', 'We_up', 'We_down', 'Ws_gate', 'Ws_up', 'Ws_down')}
    del _L0_ffn_all
    return {'x': x, 'ctx_512': ctx_512, 'L0_attn_w_in': _L0_attn_in['w_in'], 'L0_attn_w_out': _L0_attn_in['w_out'], 'L0_attn_conv_w': _L0_attn_in['conv_w'], 'L0_attn_conv_b': _L0_attn_in['conv_b'], 'L0_attn_D': _L0_attn_in['D'], 'L0_xattn_Wq': _L0_xattn_in['Wq'], 'L0_xattn_Wkv_expand': _L0_xattn_in['Wkv_expand'], 'L0_xattn_Wout': _L0_xattn_in['Wout'], 'L0_ffn_W_router': _L0_ffn_in['W_router'], 'L0_ffn_We_gate': _L0_ffn_in['We_gate'], 'L0_ffn_We_up': _L0_ffn_in['We_up'], 'L0_ffn_We_down': _L0_ffn_in['We_down'], 'L0_ffn_Ws_gate': _L0_ffn_in['Ws_gate'], 'L0_ffn_Ws_up': _L0_ffn_in['Ws_up'], 'L0_ffn_Ws_down': _L0_ffn_in['Ws_down']}

def reference(x, ctx_512, L0_attn_w_in, L0_attn_w_out, L0_attn_conv_w, L0_attn_conv_b, L0_attn_D, L0_xattn_Wq, L0_xattn_Wkv_expand, L0_xattn_Wout, L0_ffn_W_router, L0_ffn_We_gate, L0_ffn_We_up, L0_ffn_We_down, L0_ffn_Ws_gate, L0_ffn_Ws_up, L0_ffn_Ws_down):
    import jax
    import jax.numpy as jnp

    def _L0_attn_ref(x, w_in, w_out, conv_w, conv_b, D):
        import jax, jax.numpy as jnp
        import numpy as np
        from jax import lax
        B, T, D_MODEL = (4, 512, 512)
        EXPAND, D_CONV = (2, 4)
        D_INNER = D_MODEL * EXPAND

        def _forward(x, w_in, w_out, conv_w, conv_b, D):
            x_proj = jnp.einsum('btc,dc->btd', x, w_in)
            xi, gate = jnp.split(x_proj, 2, axis=-1)
            xc = jnp.transpose(xi, (0, 2, 1))
            xc = lax.conv_general_dilated(xc, conv_w, window_strides=(1,), padding=[(D_CONV - 1, 0)], dimension_numbers=('NCH', 'OIH', 'NCH'), feature_group_count=D_INNER) + conv_b[None, :, None]
            xc = jnp.transpose(xc, (0, 2, 1))
            h = jax.nn.silu(xc) * D[None, None, :] * jax.nn.silu(gate)
            return jnp.einsum('btd,cd->btc', h, w_out)
        return _forward(x, w_in, w_out, conv_w, conv_b, D)

    def _L0_xattn_ref(q, latent_kv, Wq, Wkv_expand, Wout):
        import jax, jax.numpy as jnp
        import numpy as np
        B, S, H, NH, L = (2, 512, 512, 16, 128)
        HD = H // NH
        b, sq, _ = q.shape
        sk = latent_kv.shape[1]
        qp = q @ Wq.T
        kv = latent_kv @ Wkv_expand.T
        k, v = jnp.split(kv, 2, axis=-1)
        qh = qp.reshape(b, sq, NH, HD).transpose(0, 2, 1, 3)
        kh = k.reshape(b, sk, NH, HD).transpose(0, 2, 1, 3)
        vh = v.reshape(b, sk, NH, HD).transpose(0, 2, 1, 3)
        inv_sqrt_d = 1.0 / jnp.sqrt(jnp.float32(HD))
        scores = jnp.einsum('bhqd,bhkd->bhqk', qh, kh) * inv_sqrt_d
        causal = jnp.tril(jnp.ones((sq, sk), dtype=bool))
        scores = jnp.where(causal, scores, jnp.finfo(scores.dtype).min)
        attn = jax.nn.softmax(scores, axis=-1)
        out = jnp.einsum('bhqk,bhkd->bhqd', attn, vh)
        out = out.transpose(0, 2, 1, 3).reshape(b, sq, H)
        return out @ Wout.T

    def _L0_ffn_ref(x, W_router, We_gate, We_up, We_down, Ws_gate, Ws_up, Ws_down):
        import jax, jax.numpy as jnp
        import numpy as np
        E = 8
        TOP_K = 2
        D = 512
        DE = 352
        DS = 704
        B, S = (2, 512)
        b, s, d = x.shape
        shared = jax.nn.silu(x @ Ws_gate) * (x @ Ws_up) @ Ws_down
        scores = jax.nn.softmax(x @ W_router, axis=-1)
        topk_vals, topk_idx = jax.lax.top_k(scores, TOP_K)
        onehot = jax.nn.one_hot(topk_idx, E, dtype=x.dtype)
        combine = jnp.einsum('bsk,bske->bse', topk_vals, onehot)
        combine = combine.reshape(b * s, E)
        xf = x.reshape(b * s, d)
        h = jax.nn.silu(jnp.einsum('td,edh->eth', xf, We_gate)) * jnp.einsum('td,edh->eth', xf, We_up)
        y_all = jnp.einsum('eth,ehd->etd', h, We_down)
        routed = jnp.einsum('etd,te->td', y_all, combine)
        return routed.reshape(b, s, d) + shared
    x = _layernorm(x + _L0_attn_ref(x, L0_attn_w_in, L0_attn_w_out, L0_attn_conv_w, L0_attn_conv_b, L0_attn_D), axis=-1)
    x = _layernorm(x + _L0_xattn_ref(x, ctx_512, L0_xattn_Wq, L0_xattn_Wkv_expand, L0_xattn_Wout), axis=-1)
    x = _layernorm(x + _L0_ffn_ref(x, L0_ffn_W_router, L0_ffn_We_gate, L0_ffn_We_up, L0_ffn_We_down, L0_ffn_Ws_gate, L0_ffn_Ws_up, L0_ffn_Ws_down), axis=-1)
    return x

_drawn_inputs = setup_inputs


def setup_inputs(seed=0):
    import zlib

    import numpy as np

    out = dict(_drawn_inputs(seed))
    spreads = {'L0_attn_D': (1.0, 0.2)}
    factors = {'L0_attn_conv_b': 6.907,
     'L0_xattn_Wq': 8.0,
     'L0_ffn_W_router': 5.604,
     'L0_ffn_We_gate': 4.957,
     'L0_ffn_We_up': 4.862,
     'L0_ffn_We_down': 4.851,
     'L0_ffn_Ws_gate': 3.872,
     'L0_ffn_Ws_up': 3.792,
     'L0_ffn_Ws_down': 3.797}
    for name, (base, spread) in spreads.items():
        noise = np.random.default_rng([zlib.crc32(name.encode()), seed]).standard_normal(out[name].shape)
        drawn = base * np.exp(spread * noise) if base else spread * noise
        out[name] = jnp.asarray(drawn.astype(out[name].dtype))
    for name, factor in factors.items():
        out[name] = (out[name] * factor).astype(out[name].dtype)
    return out
```

```python
from contextlib import ExitStack

import concourse.bass as bass
from concourse import mybir

F32 = mybir.dt.float32
F32R = mybir.dt.float32r
BF16 = mybir.dt.bfloat16
I32 = mybir.dt.int32
U32 = mybir.dt.uint32
ALU = mybir.AluOpType
ACT = mybir.ActivationFunctionType
AX_X = mybir.AxisListType.X

P = 128
B, S, D = 8, 256, 512
T = B * S
GT = 512
GROUPS = T // GT
GB = GT // S
TILES = GT // P
DC = D // P
DI = 1024
JC = DI // P
TAPS = 4
EPS = 1e-5


def three_pass(pe, out, a_hi, a_lo, b_hi, b_lo, first, last):
    pe.matmul(out, a_hi, b_lo, start=first, stop=False)
    pe.matmul(out, a_lo, b_hi, start=False, stop=False)
    return pe.matmul(out, a_hi, b_hi, start=False, stop=last)


class Moments:

    def __init__(self, sb, name, n):
        self.n = n
        self.stats = sb(name + "_ln_stats", [P, n, 6])
        self.sum = sb(name + "_ln_sum", [P, n])
        self.diff = sb(name + "_ln_diff", [P, n])
        self.sq = sb(name + "_ln_sq", [P, n])
        self.mean = sb(name + "_ln_mean", [P, n])
        self.sq_eps = sb(name + "_ln_sq_eps", [P, n])
        self.diff_sq = sb(name + "_ln_diff_sq", [P, n])
        self.var = sb(name + "_ln_var", [P, n])
        self.power = sb(name + "_ln_power", [P, n])
        self.rstd = sb(name + "_ln_rstd", [P, n])


def moments(dve, x, ln, step, base, var_done):
    n, s = ln.n, ln.stats
    for t in range(n):
        dve.bn_stats(s[:, t], x[:, t]).then_inc(step, 1)
    dve.wait_ge(step, base + n)
    dve.tensor_tensor(ln.sum[:], s[:, :, 1], s[:, :, 4], ALU.add).then_inc(step, 1)
    dve.tensor_tensor(ln.diff[:], s[:, :, 1], s[:, :, 4], ALU.subtract).then_inc(step, 1)
    dve.tensor_tensor(ln.sq[:], s[:, :, 2], s[:, :, 5], ALU.add).then_inc(step, 1)
    dve.wait_ge(step, base + n + 3)
    dve.tensor_scalar(ln.mean[:], ln.sum[:], 0.5, None, ALU.mult).then_inc(step, 1)
    dve.tensor_scalar(ln.sq_eps[:], ln.sq[:], 1.0 / D, EPS, ALU.mult, ALU.add).then_inc(step, 1)
    dve.scalar_tensor_tensor(ln.diff_sq[:], ln.diff[:], 0.25, ln.diff[:], ALU.mult, ALU.mult).then_inc(step, 1)
    dve.wait_ge(step, base + n + 6)
    dve.tensor_tensor(ln.var[:], ln.sq_eps[:], ln.diff_sq[:], ALU.add).then_inc(var_done, 1)


def gated_conv(nc, x_t, x_tok, w_in, w_out, conv_w, conv_b, gain, x1_dram, arena, following):
    with ExitStack() as ctx:
        def sb(name, shape, dt=F32):
            return ctx.enter_context(nc.sbuf_tensor(name, shape, dt))

        def sem(name):
            return ctx.enter_context(nc.semaphore(name))

        w_raw = sb("a_w_raw", [P, 2, 1024])
        half = JC * DC * 2 * P
        wi_hi = arena[:, 0:half].rearrange("p (j c s m) -> p j c s m", j=JC, c=DC, s=2)
        wi_lo = arena[:, half:2 * half].rearrange("p (j c s m) -> p j c s m", j=JC, c=DC, s=2)
        wo_hi = sb("a_wo_hi", [P, JC, D], F32R)
        wo_lo = sb("a_wo_lo", [P, JC, D], F32R)
        taps = sb("a_taps", [P, JC, TAPS])
        bias = sb("a_bias", [P, JC])
        dgain = sb("a_dgain", [P, JC])
        x_raw = sb("a_x_raw", [P, DC, GT])
        x_hi = sb("a_x_hi", [P, DC, GT], F32R)
        x_lo = sb("a_x_lo", [P, DC, GT], F32R)
        xc = sb("a_xc", [P, 2, GB, S])
        sg = sb("a_sg", [P, 2, GT])
        hf = sb("a_hf", [P, 2, GT])
        h_hi = sb("a_h_hi", [P, JC, GT], F32R)
        h_lo = sb("a_h_lo", [P, JC, GT], F32R)
        xt = sb("a_xt", [P, TILES, D])
        x1 = sb("a_x1", [P, TILES, D])
        ln = Moments(sb, "a", TILES)
        ps_proj = ctx.enter_context(nc.psum_tensor("a_ps_proj", [P, 2, 2, GT], F32))
        ps_out = ctx.enter_context(nc.psum_tensor("a_ps_out", [P, TILES, D], F32))

        w_loaded = [sem("a_w_loaded_even"), sem("a_w_loaded_odd")]
        w_hi_done = sem("a_w_hi_done")
        w_lo_done = sem("a_w_lo_done")
        consts_loaded = sem("a_consts_loaded")
        x_loaded = sem("a_x_loaded")
        xt_loaded = sem("a_xt_loaded")
        x_hi_done = sem("a_x_hi_done")
        x_lo_done = sem("a_x_lo_done")
        proj_done = sem("a_proj_done")
        gate_free = sem("a_gate_free")
        tap_last = sem("a_tap_last")
        tap_step = sem("a_tap_step")
        conv_done = sem("a_conv_done")
        silu_done = sem("a_silu_done")
        h_done = sem("a_h_done")
        h_hi_done = sem("a_h_hi_done")
        h_lo_done = sem("a_h_lo_done")
        out_done = sem("a_out_done")
        out_free = sem("a_out_free")
        ln_step = sem("a_ln_step")
        ln_const = sem("a_ln_const")
        var_done = sem("a_var_done")
        rstd_done = sem("a_rstd_done")
        x1_ready = sem("a_x1_ready")
        x1_stored = sem("a_x1_stored")

        BANKS = 2
        W_UNITS = JC + JC // 2
        W_AHEAD = 3
        ALL_UNITS = W_UNITS + len(following)

        def w_unit(u, hi):
            if u >= W_UNITS:
                return following[u - W_UNITS][1 if hi else 2]
            if u < JC:
                return (wi_hi if hi else wi_lo)[:, u].rearrange("p c s m -> p (c s m)")
            c = 2 * (u - JC)
            return (wo_hi if hi else wo_lo)[:, c:c + 2].rearrange("p c n -> p (c n)")

        block = ctx.enter_context(nc.Block())

        @block.sync
        def _(sp):
            sp.dma_start(x_raw[:], x_t[0]).then_inc(x_loaded, 16)
            sp.dma_start(taps[:], conv_w).then_inc(consts_loaded, 16)
            sp.dma_start(bias[:], conv_b).then_inc(consts_loaded, 16)
            sp.dma_start(dgain[:], gain).then_inc(consts_loaded, 16)
            for u in range(W_UNITS):
                if u >= 2:
                    sp.wait_ge(w_lo_done, u - 1)
                src = w_in[u] if u < JC else w_out[u - JC]
                sp.dma_start(w_raw[:, u % 2], src).then_inc(w_loaded[u % 2], 16)
            with sp.Fori(0, GROUPS - 1) as g:
                sp.wait_ge(x1_ready, TILES * g)
                sp.dma_start(xt[:], x_tok[bass.ds(g, 1)].rearrange("o p t d -> p (o t) d")).then_inc(xt_loaded, 16)
                sp.wait_ge(x_lo_done, g + 1)
                sp.dma_start(x_raw[:], x_t[bass.ds(g + 1, 1)].rearrange("o p c t -> p (o c) t")).then_inc(x_loaded, 16)
            sp.wait_ge(x1_ready, TILES * (GROUPS - 1))
            sp.dma_start(xt[:], x_tok[GROUPS - 1]).then_inc(xt_loaded, 16)
            for u in range(W_UNITS, ALL_UNITS):
                sp.wait_ge(w_lo_done, u - 1)
                sp.dma_start(w_raw[:, u % 2], following[u - W_UNITS][0]).then_inc(w_loaded[u % 2], 16)

        @block.gpsimd
        def _(pool):
            def split_x(g):
                pool.wait_ge(x_hi_done, g + 1)
                pool.tensor_tensor(x_lo[:], x_raw[:], x_hi[:].bitcast(F32), ALU.subtract).then_inc(x_lo_done, 1)

            def root(g):
                pool.wait_ge(ln_const, 1)
                pool.wait_ge(var_done, g + 1)
                pool.tensor_tensor(ln.rstd[:], ln.var[:], ln.power[:], ALU.pow).then_inc(rstd_done, 1)

            pool.memset(ln.power[:], -0.5).then_inc(ln_const, 1)
            def split_w(u):
                pool.wait_ge(w_hi_done, u + 1)
                pool.tensor_tensor(w_unit(u, False), w_raw[:, u % 2], w_unit(u, True).bitcast(F32),
                                   ALU.subtract).then_inc(w_lo_done, 1)

            split_x(0)
            for u in range(W_UNITS):
                split_w(u)
            with pool.Fori(0, GROUPS - 1) as g:
                split_x(g + 1)
                root(g)
                pool.wait_ge(x1_ready, TILES * g + TILES)
                pool.dma_start(x1_dram[bass.ds(g, 1)].rearrange("o p t d -> p (o t) d"), x1[:]).then_inc(x1_stored, 16)
            for u in range(W_UNITS, ALL_UNITS):
                split_w(u)
            root(GROUPS - 1)
            pool.wait_ge(x1_ready, TILES * GROUPS)
            pool.dma_start(x1_dram[GROUPS - 1], x1[:]).then_inc(x1_stored, 16)
            pool.wait_ge(x1_stored, 16 * GROUPS)

        @block.scalar
        def _(act):
            act.preload_act_table_set("silu_and_others")

            def split_x(g):
                act.wait_ge(x_loaded, 16 * g + 16)
                act.wait_ge(proj_done, JC * g)
                act.activation(x_hi[:], x_raw[:], ACT.Copy).then_inc(x_hi_done, 1)

            def h_round(g, j):
                act.wait_ge(h_done, JC * g + j + 1)
                if j == 0:
                    act.wait_ge(out_done, TILES * g)
                act.activation(h_hi[:, j], hf[:, j % 2], ACT.Copy).then_inc(h_hi_done, 1)

            def split_w(u):
                act.wait_ge(w_loaded[u % 2], 16 * (u // 2) + 16)
                act.activation(w_unit(u, True), w_raw[:, u % 2], ACT.Copy).then_inc(w_hi_done, 1)

            split_x(0)
            act.sem_inc(gate_free, BANKS)
            for u in range(W_AHEAD):
                split_w(u)
            act.wait_ge(consts_loaded, 48)

            def group(g):
                for j in range(JC):
                    xcj = xc[:, j % 2].rearrange("p b s -> p (b s)")
                    act.wait_ge(proj_done, JC * g + j + 1)
                    act.activation(xcj, ps_proj[:, j % 2, 0], ACT.Identity,
                                   scale=taps[:, j, TAPS - 1:TAPS], bias=bias[:, j:j + 1]).then_inc(tap_last, 1)
                    act.activation(sg[:, j % 2], ps_proj[:, j % 2, 1], ACT.Silu).then_inc(gate_free, 1)
                    if isinstance(g, int) and g == 0:
                        for u in range(W_AHEAD + 2 * j, min(W_AHEAD + 2 * j + 2, W_UNITS)):
                            split_w(u)
                    if j:
                        h_round(g, j - 1)
                    act.wait_ge(conv_done, BANKS + JC * g + j + 1)
                    act.activation(xcj, xcj, ACT.Silu).then_inc(silu_done, 1)
                h_round(g, JC - 1)

            group(0)
            split_x(1)
            with act.Fori(1, GROUPS - 1) as g:
                group(g)
                split_x(g + 1)
            group(GROUPS - 1)
            for u in range(W_UNITS, ALL_UNITS):
                split_w(u)

        @block.vector
        def _(dve):
            dve.sem_inc(conv_done, BANKS)
            dve.wait_ge(consts_loaded, 48)

            def h_rest(g, j):
                dve.wait_ge(h_hi_done, JC * g + j + 1)
                dve.tensor_tensor(h_lo[:, j], hf[:, j % 2], h_hi[:, j].bitcast(F32), ALU.subtract).then_inc(h_lo_done, 1)

            with dve.Fori(0, GROUPS) as g:
                for j in range(JC):
                    dve.wait_ge(tap_last, JC * g + j + 1)
                    xi = ps_proj[:, j % 2, 0].rearrange("p (b s) -> p b s", b=GB)
                    for s in range(1, TAPS):
                        if s > 1:
                            dve.wait_ge(tap_step, (TAPS - 2) * (JC * g + j) + s - 1)
                        ins = dve.scalar_tensor_tensor(xc[:, j % 2, :, s:S], xi[:, :, 0:S - s],
                                                       taps[:, j, TAPS - 1 - s:TAPS - s], xc[:, j % 2, :, s:S],
                                                       ALU.mult, ALU.add)
                        ins.then_inc(tap_step if s < TAPS - 1 else conv_done, 1)
                    if j:
                        h_rest(g, j - 1)
                    dve.wait_ge(silu_done, JC * g + j + 1)
                    dve.scalar_tensor_tensor(hf[:, j % 2], xc[:, j % 2].rearrange("p b s -> p (b s)"),
                                             dgain[:, j:j + 1], sg[:, j % 2], ALU.mult, ALU.mult).then_inc(h_done, 1)
                h_rest(g, JC - 1)
                dve.wait_ge(xt_loaded, 16 * g + 16)
                for t in range(TILES):
                    dve.wait_ge(out_done, TILES * g + t + 1)
                    dve.tensor_tensor(xt[:, t], ps_out[:, t], xt[:, t], ALU.add).then_inc(out_free, 1)
                dve.wait_ge(out_free, TILES * g + TILES)
                moments(dve, xt, ln, ln_step, (TILES + 6) * g, var_done)
                dve.wait_ge(rstd_done, g + 1)
                dve.wait_ge(x1_stored, 16 * g)
                for t in range(TILES):
                    dve.tensor_scalar(x1[:, t], xt[:, t], ln.mean[:, t:t + 1], ln.rstd[:, t:t + 1],
                                      ALU.subtract, ALU.mult).then_inc(x1_ready, 1)

        @block.tensor
        def _(pe):
            with pe.Fori(0, GROUPS) as g:
                pe.wait_ge(x_lo_done, g + 1)
                for j in range(JC):
                    pe.wait_ge(w_lo_done, j + 1)
                    for side, free in ((0, conv_done), (1, gate_free)):
                        pe.wait_ge(free, JC * g + j + 1)
                        for c in range(DC):
                            mm = three_pass(pe, ps_proj[:, j % 2, side], wi_hi[:, j, c, side], wi_lo[:, j, c, side],
                                            x_hi[:, c], x_lo[:, c], c == 0, c == DC - 1)
                    mm.then_inc(proj_done, 1)
                pe.wait_ge(w_lo_done, W_UNITS)
                pe.wait_ge(out_free, TILES * g)
                for j in range(JC):
                    pe.wait_ge(h_lo_done, JC * g + j + 1)
                    for t in range(TILES):
                        mm = three_pass(pe, ps_out[:, t], h_hi[:, j, t * P:(t + 1) * P], h_lo[:, j, t * P:(t + 1) * P],
                                        wo_hi[:, j], wo_lo[:, j], j == 0, j == JC - 1)
                        if j == JC - 1:
                            mm.then_inc(out_done, 1)


HEADS = 16
HD = D // HEADS
HC = P // HD
L = 128
SCALE = 1.0 / float(HD) ** 0.5
MASKED = -1e30


class CrossWeights:

    def __init__(self, arena, w_q, w_kv, w_o):
        n = DC * D
        at = [arena[:, k:k + size] for k, size in ((0, n), (n, n), (2 * n, n), (3 * n, n), (4 * n, n // 2), (9 * n // 2, n // 2))]
        self.q_hi, self.q_lo, self.o_hi, self.o_lo, self.kv_hi, self.kv_lo = (
            w.rearrange("p (c n) -> p c n", n=D) for w in at)
        h = n // 2
        self.units = [(w_q[0], at[0][:, 0:h], at[1][:, 0:h]), (w_q[1], at[0][:, h:n], at[1][:, h:n]),
                      (w_kv, at[4], at[5]),
                      (w_o[0], at[2][:, 0:h], at[3][:, 0:h]), (w_o[1], at[2][:, h:n], at[3][:, h:n])]


def cross_attention(nc, x1_dram, ctx_t, weights, x2_dram):
    with ExitStack() as ctx:
        def sb(name, shape, dt=F32):
            return ctx.enter_context(nc.sbuf_tensor("b_" + name, shape, dt))

        def sem(name):
            return ctx.enter_context(nc.semaphore("b_" + name))

        GH = GB * HEADS
        wq_hi, wq_lo, wkv_hi, wkv_lo = weights.q_hi, weights.q_lo, weights.kv_hi, weights.kv_lo
        wo_hi, wo_lo = weights.o_hi, weights.o_lo
        ident = sb("ident", [P, P])
        mask = sb("mask", [P, 3 * P])
        xt = sb("xt", [P, TILES, D])
        x_hi = sb("x_hi", [P, DC, GT], F32R)
        x_lo = sb("x_lo", [P, DC, GT], F32R)
        c_raw = sb("c_raw", [P, GT])
        c_hi = sb("c_hi", [P, GT], F32R)
        c_lo = sb("c_lo", [P, GT], F32R)
        q = sb("q", [P, DC, GT])
        k = sb("k", [P, DC, HC, GT])
        v = sb("v", [P, TILES, DC, HC, P])
        carrier = sb("carrier", [P, GH])
        pr = sb("pr", [P, 4, 3 * P])
        bmax = sb("bmax", [P, 4, 2])
        rsum = sb("rsum", [P, 4, 2])
        rinv = sb("rinv", [P, 4, 2])
        pt = sb("pt", [P, 2, 3 * P])
        a_hi = sb("a_hi", [P, DC, GT], F32R)
        a_lo = sb("a_lo", [P, DC, GT], F32R)
        res = sb("res", [P, TILES, D])
        ln = Moments(sb, "b", TILES)
        ps_pj = ctx.enter_context(nc.psum_tensor("b_ps_pj", [P, 2, 512], F32))
        ps_s = ctx.enter_context(nc.psum_tensor("b_ps_s", [P, 2, 512], F32))
        ps_t = ctx.enter_context(nc.psum_tensor("b_ps_t", [P, 2, 512], F32))
        ps_o = ctx.enter_context(nc.psum_tensor("b_ps_o", [P, 2, 512], F32))

        consts = sem("consts")
        zeros = sem("zeros")
        xt_loaded = sem("xt_loaded")
        c_loaded = sem("c_loaded")
        res_loaded = sem("res_loaded")
        c_hi_done = sem("c_hi_done")
        c_lo_done = sem("c_lo_done")
        pj_ready = sem("pj_ready")
        x_hi_done = sem("x_hi_done")
        k_done = sem("k_done")
        pj_free = sem("pj_free")
        s_ready = sem("s_ready")
        max_done = sem("max_done")
        exp_done = sem("exp_done")
        rinv_done = sem("rinv_done")
        norm_done = sem("norm_done")
        pt_ready = sem("pt_ready")
        pt_free = sem("pt_free")
        pv_done = sem("pv_done")
        o_hi_done = sem("o_hi_done")
        o_free = sem("o_free")
        ln_step = sem("ln_step")
        var_done = sem("var_done")
        rstd_done = sem("rstd_done")
        x2_ready = sem("x2_ready")
        x2_stored = sem("x2_stored")

        CONSTS = 7
        BANKS = 2
        USES = 4 * DC + TILES
        FREES = USES - DC
        GC = GB * DC
        AHEAD = 3
        STEPS = GH + AHEAD + 3

        def seq(n):
            return n // HEADS, n % HEADS // HC, n % HC

        block = ctx.enter_context(nc.Block())

        @block.sync
        def _(sp):
            sp.dma_start(xt[:], x1_dram[0]).then_inc(xt_loaded, 16)
            sp.dma_start(c_raw[:], ctx_t[0]).then_inc(c_loaded, 16)
            with sp.Fori(0, GROUPS - 1) as g:
                sp.wait_ge(x2_stored, 16 * g)
                sp.dma_start(res[:], x1_dram[bass.ds(g, 1)].rearrange("o p t d -> p (o t) d")).then_inc(res_loaded, 16)
                sp.wait_ge(pj_ready, USES * g + DC)
                sp.dma_start(xt[:], x1_dram[bass.ds(g + 1, 1)].rearrange("o p t d -> p (o t) d")).then_inc(xt_loaded, 16)
                sp.wait_ge(c_lo_done, g + 1)
                sp.dma_start(c_raw[:], ctx_t[bass.ds(g + 1, 1)].rearrange("o p t -> p (o t)")).then_inc(c_loaded, 16)
            sp.wait_ge(x2_stored, 16 * (GROUPS - 1))
            sp.dma_start(res[:], x1_dram[GROUPS - 1]).then_inc(res_loaded, 16)

        @block.gpsimd
        def _(pool):
            pool.memset(ident[:], 0.0).then_inc(consts, 1)
            pool.memset(mask[:], 0.0).then_inc(consts, 1)
            pool.memset(ln.power[:], -0.5).then_inc(consts, 1)
            pool.wait_ge(consts, 3)
            pool.affine_select(out=ident[:], in_=ident[:], compare_op=ALU.not_equal, fill=1.0, base=0,
                               pattern=[[-1, P]], channel_multiplier=1).then_inc(consts, 1)
            for c in (0, 2):
                pool.affine_select(out=mask[:, c * P:(c + 1) * P], in_=mask[:, c * P:(c + 1) * P], compare_op=ALU.is_ge,
                                   fill=MASKED, base=0, pattern=[[-1, P]], channel_multiplier=1).then_inc(consts, 1)
            pool.memset(k[:], 0.0).then_inc(consts, 1)

            def top(g):
                pool.wait_ge(c_hi_done, g + 1)
                pool.tensor_tensor(c_lo[:], c_raw[:], c_hi[:].bitcast(F32), ALU.subtract).then_inc(c_lo_done, 1)

            def attend(g):
                for n in range(GH):
                    pool.wait_ge(rinv_done, GH * g + n + 1)
                    for a, b, r in ((0, P, 0), (P, 3 * P, 1)):
                        ins = pool.tensor_tensor(pr[:, n % 4, a:b], pr[:, n % 4, a:b],
                                                 rinv[:, n % 4, r:r + 1].broadcast_to([P, b - a]), ALU.mult)
                    ins.then_inc(norm_done, 1)

            def normalize(g):
                pool.wait_ge(var_done, g + 1)
                pool.tensor_tensor(ln.rstd[:], ln.var[:], ln.power[:], ALU.pow).then_inc(rstd_done, 1)
                pool.wait_ge(x2_ready, TILES * g + TILES)
                if isinstance(g, int):
                    dst = x2_dram[g]
                else:
                    dst = x2_dram[bass.ds(g, 1)].rearrange("o p t d -> p (o t) d")
                pool.dma_start(dst, res[:]).then_inc(x2_stored, 16)

            top(0)
            attend(0)
            with pool.Fori(1, GROUPS) as g:
                top(g)
                normalize(g - 1)
                attend(g)
            normalize(GROUPS - 1)
            pool.wait_ge(x2_stored, 16 * GROUPS)

        @block.scalar
        def _(act):
            act.preload_act_table_set("exp_and_others")
            with act.Fori(0, GROUPS) as g:
                act.wait_ge(c_loaded, 16 * g + 16)
                act.activation(c_hi[:], c_raw[:], ACT.Copy).then_inc(c_hi_done, 1)
                for c in range(DC):
                    act.wait_ge(pj_ready, USES * g + c + 1)
                    act.activation(x_hi[:, c], ps_pj[:, c % 2], ACT.Copy).then_inc(x_hi_done, 1)
                act.wait_ge(consts, CONSTS)
                for c in range(DC):
                    act.wait_ge(pj_ready, USES * g + 2 * DC + c + 1)
                    for h in range(HC):
                        rows = slice(h * HD, (h + 1) * HD)
                        ins = act.activation(k[rows, c, h], ps_pj[rows, c % 2], ACT.Copy)
                    ins.then_inc(k_done, 1)
                for n in range(STEPS):
                    if n < GH:
                        act.wait_ge(max_done, BANKS + GH * g + n + 1)
                        for a, b, r in ((0, P, 0), (P, 3 * P, 1)):
                            ins = act.activation(pr[:, n % 4, a:b], pr[:, n % 4, a:b], ACT.Exp, scale=-1.0,
                                                 bias=bmax[:, n % 4, r:r + 1], accum_out=rsum[:, n % 4, r:r + 1])
                        ins.then_inc(exp_done, 1)
                    m = n - AHEAD - 2
                    if 0 <= m < GH and m % HC == HC - 1:
                        b, c, _ = seq(m)
                        act.wait_ge(pv_done, BANKS + GH * g + m + 1)
                        act.activation(a_hi[:, c, b * S:(b + 1) * S], ps_o[:, m // HC % 2, 0:S], ACT.Copy)\
                            .then_inc(o_hi_done, 1)

        @block.vector
        def _(dve):
            dve.sem_inc(pj_free, BANKS)
            dve.sem_inc(max_done, BANKS)
            dve.sem_inc(pt_free, BANKS)
            dve.sem_inc(o_free, BANKS)
            dve.memset(v[:], 0.0).then_inc(zeros, 1)

            def top(g):
                for i in range(4 * DC):
                    if i // DC == 2:
                        continue
                    src, c = ps_pj[:, i % 2], i % DC
                    if i < DC:
                        dve.wait_ge(x_hi_done, DC * g + i + 1)
                        dve.tensor_tensor(x_lo[:, c], src, x_hi[:, c].bitcast(F32), ALU.subtract).then_inc(pj_free, 1)
                        continue
                    dve.wait_ge(pj_ready, USES * g + i + 1)
                    if i < 2 * DC:
                        dve.tensor_copy(q[:, c], src).then_inc(pj_free, 1)
                        continue
                    vs = src.rearrange("p (c h d) -> p c h d", c=DC, h=HC)
                    for h in range(HC):
                        ins = dve.tensor_copy(v[:, c, :, h, h * HD:(h + 1) * HD], vs[:, :, h])
                    ins.then_inc(pj_free, 1)

            def normalize(g):
                moments(dve, res, ln, ln_step, (TILES + 6) * g, var_done)
                dve.wait_ge(rstd_done, g + 1)
                for t in range(TILES):
                    dve.tensor_scalar(res[:, t], res[:, t], ln.mean[:, t:t + 1], ln.rstd[:, t:t + 1],
                                      ALU.subtract, ALU.mult).then_inc(x2_ready, 1)

            def attend(g):
                for n in range(STEPS):
                    if n < GH:
                        dve.wait_ge(s_ready, GH * g + n + 1)
                        dve.memset(carrier[:, n:n + 1], 0.0)
                        for a, b, r in ((0, P, 0), (P, 3 * P, 1)):
                            ins = dve.tensor_tensor_reduce(pr[:, n % 4, a:b], ps_s[:, n % 2, a:b], mask[:, a:b], -SCALE, 3e38,
                                                           ALU.add, ALU.min, bmax[:, n % 4, r:r + 1])
                        ins.then_inc(max_done, 1)
                    m = n - 1
                    if 0 <= m < GH:
                        dve.wait_ge(exp_done, GH * g + m + 1)
                        dve.reciprocal(rinv[:, m % 4], rsum[:, m % 4]).then_inc(rinv_done, 1)
                    m = n - AHEAD
                    if 0 <= m < GH:
                        dve.wait_ge(pv_done, GH * g + m + 1)
                        dve.wait_ge(pt_ready, GH * g + m + 1)
                        dve.tensor_copy(pt[:, m % 2], ps_t[:, m % 2, 0:3 * P]).then_inc(pt_free, 1)
                    m = n - AHEAD - 2
                    if 0 <= m < GH and m % HC == HC - 1:
                        b, c, _ = seq(m)
                        dve.wait_ge(o_hi_done, GC * g + m // HC + 1)
                        dve.tensor_tensor(a_lo[:, c, b * S:(b + 1) * S], ps_o[:, m // HC % 2, 0:S],
                                          a_hi[:, c, b * S:(b + 1) * S].bitcast(F32), ALU.subtract).then_inc(o_free, 1)
                dve.wait_ge(res_loaded, 16 * g + 16)
                for t in range(TILES):
                    i = 4 * DC + t
                    dve.wait_ge(pj_ready, USES * g + i + 1)
                    dve.tensor_tensor(res[:, t], ps_pj[:, i % 2], res[:, t], ALU.add).then_inc(pj_free, 1)
                dve.wait_ge(pj_free, BANKS + FREES * g + FREES)

            dve.wait_ge(zeros, 1)
            dve.wait_ge(consts, CONSTS)
            top(0)
            attend(0)
            with dve.Fori(1, GROUPS) as g:
                top(g)
                normalize(g - 1)
                attend(g)
            normalize(GROUPS - 1)

        @block.tensor
        def _(pe):
            pe.wait_ge(consts, CONSTS - 3)
            pe.sem_inc(pv_done, BANKS)

            def wait_read(g, i):
                if i // DC == 2:
                    pe.wait_ge(k_done, DC * g + i - 2 * DC + 1)
                else:
                    pe.wait_ge(pj_free, BANKS + FREES * g + (i if i < 2 * DC else i - DC) + 1)

            with pe.Fori(0, GROUPS) as g:
                pe.wait_ge(xt_loaded, 16 * g + 16)
                for i in range(4 * DC):
                    c = i % DC
                    out = ps_pj[:, i % 2]
                    wait_read(g, i - BANKS)
                    if i < DC:
                        for t in range(TILES):
                            mm = pe.transpose(out[:, t * P:(t + 1) * P], xt[:, t, c * P:(c + 1) * P], ident[:])
                    elif i < 2 * DC:
                        if c == 0:
                            wait_read(g, DC - 1)
                        for j in range(DC):
                            mm = three_pass(pe, out, wq_hi[:, j, c * P:(c + 1) * P], wq_lo[:, j, c * P:(c + 1) * P],
                                            x_hi[:, j], x_lo[:, j], j == 0, j == DC - 1)
                    elif i < 3 * DC:
                        pe.wait_ge(c_lo_done, g + 1)
                        mm = three_pass(pe, out, wkv_hi[:, 0, c * P:(c + 1) * P], wkv_lo[:, 0, c * P:(c + 1) * P],
                                        c_hi[:], c_lo[:], True, True)
                    else:
                        mm = three_pass(pe, out, c_hi[:, c * P:(c + 1) * P], c_lo[:, c * P:(c + 1) * P],
                                        wkv_hi[:, 1], wkv_lo[:, 1], True, True)
                    mm.then_inc(pj_ready, 1)
                wait_read(g, 3 * DC - 1)
                wait_read(g, 4 * DC - 1)
                for n in range(STEPS):
                    if n < GH:
                        b, c, h = seq(n)
                        pe.wait_ge(max_done, GH * g + n + 1)
                        for u in range(2):
                            qs = slice(b * S + u * P, b * S + (u + 1) * P)
                            ks = slice(b * S, b * S + (u + 1) * P)
                            mm = pe.matmul(ps_s[:, n % 2, u * P:(1 + 2 * u) * P], q[:, c, qs], k[:, c, h, ks],
                                           start=True, stop=True)
                        mm.then_inc(s_ready, 1)
                    m = n - AHEAD
                    if 0 <= m < GH:
                        pe.wait_ge(norm_done, GH * g + m + 1)
                        pe.wait_ge(pt_free, GH * g + m + 1)
                        for u in range(3):
                            mm = pe.transpose(ps_t[:, m % 2, u * P:(u + 1) * P], pr[:, m % 4, u * P:(u + 1) * P], ident[:])
                        mm.then_inc(pt_ready, 1)
                    m = n - AHEAD - 1
                    if 0 <= m < GH:
                        b, c, h = seq(m)
                        pe.wait_ge(pt_free, BANKS + GH * g + m + 1)
                        if h == 0:
                            pe.wait_ge(o_free, GC * g + m // HC + 1)
                        o = ps_o[:, m // HC % 2]
                        for u, out, keys in ((0, o[:, 0:S], slice(0, S)), (1, o[:, P:S], slice(S, 3 * P))):
                            mm = pe.matmul(out, v[:, b * GB + u, c, h], pt[:, m % 2, keys],
                                           start=h == 0 and u == 0, stop=h == HC - 1 and u == 1)
                        mm.then_inc(pv_done, 1)
                pe.wait_ge(o_free, BANKS + GC * g + GC)
                for t in range(TILES):
                    i = 4 * DC + t
                    wait_read(g, i - BANKS)
                    for c in range(DC):
                        mm = three_pass(pe, ps_pj[:, i % 2], a_hi[:, c, t * P:(t + 1) * P], a_lo[:, c, t * P:(t + 1) * P],
                                        wo_hi[:, c], wo_lo[:, c], c == 0, c == DC - 1)
                    mm.then_inc(pj_ready, 1)


E_N = 8
DE = 352
DS = 704
E_UNITS = (P, P, DE - 2 * P)
S_UNITS = (P, P, P, P, (DS - 4 * P) // 2, (DS - 4 * P) // 2)
SLOTS = 512
E_TILES = (2 * T + E_N * (SLOTS - 1)) // SLOTS
BLOCKS = SLOTS // P
NB = E_TILES * BLOCKS
NT = T // P
F16 = mybir.dt.float16


class Routing:

    def __init__(self, sb):
        self.token_of = sb("token_of", [P, NB], I32)
        self.slot = sb("slot", [P, 2, NT], I32)
        self.weight = sb("weight", [P, 2, NT])
        self.expert_of = sb("expert_of", [P, E_TILES], I32)


def route(nc, x2_dram, w_router, xt_hi, xt_lo, rt):
    with ExitStack() as ctx:
        def sb(name, shape, dt=F32):
            return ctx.enter_context(nc.sbuf_tensor("r_" + name, shape, dt))

        def sem(name):
            return ctx.enter_context(nc.semaphore("r_" + name))

        xt = sb("xt", [P, 2, TILES, D])
        ident = sb("ident", [P, P])
        before = sb("before", [P, P])
        ones = sb("ones", [P, P])
        w_raw = sb("w_raw", [P, DC, E_N])
        w_hi = sb("w_hi", [P, DC, P], F32R)
        w_lo = sb("w_lo", [P, DC, P], F32R)
        lg_t = sb("lg_t", [E_N, T])
        int_a = sb("int_a", [P, P], I32)
        rank8 = sb("rank8", [P, NT, E_N])
        col128 = sb("col128", [P, P])
        col_nb = sb("col_nb", [P, NB])
        token = sb("token", [P, NT])
        tile_no = sb("tile_no", [P, E_TILES, E_N])
        keep = sb("keep", [P, E_N, NT])
        unit = sb("unit", [P, E_N])
        lg = sb("lg", [P, NT, E_N])
        pr = sb("pr", [P, NT, E_N])
        top = sb("top", [P, NT])
        rsum = sb("rsum", [P, NT])
        cand = sb("cand", [P, NT, E_N])
        best = sb("best", [P, NT])
        pick = sb("pick", [P, 2, NT, E_N])
        both = sb("both", [P, NT, E_N])
        tot = sb("tot", [P, E_N, NT])
        run = sb("run", [P, E_N, NT])
        tiles_f = sb("tiles_f", [P, E_N])
        tiles_i = sb("tiles_i", [P, E_N], I32)
        ends = sb("ends", [P, E_N])
        base = sb("base", [P, E_N])
        pos = sb("pos", [P, NT, E_N])
        cmp = sb("cmp", [P, E_TILES, E_N])
        ex_f = sb("ex_f", [P, E_TILES])
        slot_f = sb("slot_f", [P, 2, NT])
        part_i = sb("part_i", [P, 2, 2, NT], I32)
        part_f = sb("part_f", [P, 2, 2, NT])
        hot_lo = sb("hot_lo", [P, 2 * NT, P], F16)
        hot_hi = sb("hot_hi", [P, 2 * NT, NB], F16)
        ps_x = ctx.enter_context(nc.psum_tensor("r_ps_x", [P, 2, 512], F32))
        ps_l = ctx.enter_context(nc.psum_tensor("r_ps_l", [P, 2, 512], F32))
        ps_r = ctx.enter_context(nc.psum_tensor("r_ps_r", [P, 4, 512], F32))

        consts = sem("consts")
        iotas = sem("iotas")
        loaded = [sem("loaded_even"), sem("loaded_odd")]
        w_loaded = sem("w_loaded")
        w_hi_done = sem("w_hi_done")
        w_lo_done = sem("w_lo_done")
        x_ready = sem("x_ready")
        x_hi_done = sem("x_hi_done")
        x_lo_done = sem("x_lo_done")
        lg_ready = sem("lg_ready")
        lg_read = sem("lg_read")
        turned = sem("turned")
        sub_done = sem("sub_done")
        exp_done = sem("exp_done")
        both_done = sem("both_done")
        counted = sem("counted")
        hot_done = sem("hot_done")
        placed = sem("placed")
        step = sem("step")

        block = ctx.enter_context(nc.Block())

        @block.sync
        def _(sp):
            sp.dma_start(w_raw[:], w_router).then_inc(w_loaded, 16)
            for g in range(GROUPS):
                if g >= 2:
                    sp.wait_ge(x_ready, DC * (g - 1))
                sp.dma_start(xt[:, g % 2], x2_dram[g]).then_inc(loaded[g % 2], 16)

        @block.gpsimd
        def _(pool):
            pool.memset(ident[:], 0.0).then_inc(consts, 1)
            pool.memset(before[:], 1.0).then_inc(consts, 1)
            pool.memset(ones[:], 1.0).then_inc(consts, 1)
            pool.memset(w_hi[:].bitcast(F32), 0.0).then_inc(consts, 1)
            pool.memset(w_lo[:].bitcast(F32), 0.0).then_inc(consts, 1)
            pool.memset(keep[:], 1.0).then_inc(consts, 1)
            pool.memset(unit[:], 1.0).then_inc(consts, 1)
            pool.wait_ge(consts, 7)
            pool.affine_select(out=ident[:], in_=ident[:], compare_op=ALU.not_equal, fill=1.0, base=0,
                               pattern=[[-1, P]], channel_multiplier=1).then_inc(consts, 1)
            pool.affine_select(out=before[:], in_=before[:], compare_op=ALU.is_gt, fill=0.0, base=0,
                               pattern=[[1, P]], channel_multiplier=-1).then_inc(consts, 1)
            pool.memset(keep[:, :, 0:1], 0.0).then_inc(consts, 1)
            n = 0
            for out, pattern, start, mult in (
                (rank8[:], [[0, NT], [-1, E_N]], E_N, 0),
                (col128[:], [[1, P]], 0, 0),
                (col_nb[:], [[1, NB]], 0, 0),
                (token[:], [[P, NT]], 0, 1),
                (tile_no[:], [[1, E_TILES], [0, E_N]], 0, 0),
            ):
                size = 1
                for _, k in pattern:
                    size *= k
                if n:
                    pool.wait_ge(iotas, n)
                pool.iota(int_a[:, 0:size], pattern=pattern, base=start, channel_multiplier=mult).then_inc(iotas, 1)
                pool.wait_ge(iotas, n + 1)
                flat = out if len(out.shape) == 2 else out.rearrange("p a b -> p (a b)")
                pool.tensor_copy(flat, int_a[:, 0:size]).then_inc(iotas, 1)
                n += 2

        @block.scalar
        def _(act):
            act.preload_act_table_set("exp_and_others")
            act.wait_ge(w_loaded, 16)
            act.wait_ge(consts, 10)
            act.activation(w_hi[:, :, 0:E_N], w_raw[:], ACT.Copy).then_inc(w_hi_done, 1)
            with act.Fori(0, GROUPS) as g:
                for c in range(DC):
                    act.wait_ge(x_ready, DC * g + c + 1)
                    act.activation(xt_hi[:, c, bass.ds(g * GT, GT)], ps_x[:, c % 2], ACT.Copy).then_inc(x_hi_done, 1)
                act.wait_ge(lg_ready, g + 1)
                act.activation(lg_t[:, bass.ds(g * GT, GT)], ps_l[0:E_N, 0], ACT.Copy).then_inc(lg_read, 1)
            act.wait_ge(sub_done, 1)
            act.activation(pr[:], lg[:], ACT.Exp).then_inc(exp_done, 1)

        @block.vector
        def _(dve):
            steps = [0]

            def link(ins):
                steps[0] += 1
                ins.then_inc(step, 1)
                dve.wait_ge(step, steps[0])

            dve.sem_inc(x_lo_done, 2)
            dve.wait_ge(w_hi_done, 1)
            dve.tensor_tensor(w_lo[:, :, 0:E_N], w_raw[:], w_hi[:, :, 0:E_N].bitcast(F32), ALU.subtract)\
                .then_inc(w_lo_done, 1)
            with dve.Fori(0, GROUPS) as g:
                for c in range(DC):
                    dve.wait_ge(x_hi_done, DC * g + c + 1)
                    cols = bass.ds(g * GT, GT)
                    dve.tensor_tensor(xt_lo[:, c, cols], ps_x[:, c % 2], xt_hi[:, c, cols].bitcast(F32), ALU.subtract)\
                        .then_inc(x_lo_done, 1)

            def each(row):
                return row.rearrange("p (t o) -> p t o", o=1).broadcast_to([P, NT, E_N])

            dve.wait_ge(iotas, 10)
            dve.wait_ge(turned, 1)
            logits = ps_r[:, 0, 0:NT * E_N].rearrange("p (t e) -> p t e", e=E_N)
            link(dve.tensor_reduce(top[:], logits, AX_X, ALU.max))
            dve.tensor_tensor(lg[:], logits, each(top[:]), ALU.subtract).then_inc(sub_done, 1)
            dve.wait_ge(exp_done, 1)
            link(dve.tensor_reduce(rsum[:], pr[:], AX_X, ALU.add))
            link(dve.reciprocal(rsum[:], rsum[:]))
            link(dve.tensor_tensor(pr[:], pr[:], each(rsum[:]), ALU.mult))
            for k in range(2):
                w = rt.weight[:, k]
                link(dve.tensor_reduce(w, pr[:], AX_X, ALU.max))
                link(dve.tensor_tensor(cand[:], pr[:], each(w), ALU.is_equal))
                link(dve.tensor_tensor(cand[:], cand[:], rank8[:], ALU.mult))
                link(dve.tensor_reduce(best[:], cand[:], AX_X, ALU.max))
                link(dve.tensor_tensor(pick[:, k], cand[:], each(best[:]), ALU.is_equal))
                if k == 0:
                    link(dve.scalar_tensor_tensor(pr[:], pick[:, 0], -4.0, pr[:], ALU.mult, ALU.add))
            dve.tensor_tensor(both[:], pick[:, 0], pick[:, 1], ALU.add).then_inc(both_done, 1)
            dve.wait_ge(counted, 1)
            prior = ps_r[:, 1, 0:NT * E_N].rearrange("p (t e) -> p t e", e=E_N)
            total = ps_r[:, 2, 0:NT * E_N].rearrange("p (t e) -> p e t", e=E_N)
            link(dve.tensor_copy(tot[:], total))
            link(dve.tensor_tensor_scan(run[:].rearrange("p e t -> p (e t)"), keep[:].rearrange("p e t -> p (e t)"),
                                        tot[:].rearrange("p e t -> p (e t)"), 0.0, ALU.mult, ALU.add))
            link(dve.tensor_scalar(tiles_i[:], run[:, :, NT - 1], float(SLOTS - 1), None, ALU.add))
            link(dve.tensor_scalar(tiles_i[:], tiles_i[:], SLOTS.bit_length() - 1, None, ALU.logical_shift_right))
            link(dve.tensor_copy(tiles_f[:], tiles_i[:]))
            link(dve.tensor_tensor_scan(ends[:], unit[:], tiles_f[:], 0.0, ALU.mult, ALU.add))
            link(dve.tensor_tensor(base[:], ends[:], tiles_f[:], ALU.subtract))
            link(dve.tensor_scalar(base[:], base[:], float(SLOTS), None, ALU.mult))
            link(dve.tensor_tensor(cmp[:], tile_no[:],
                                   ends[:].rearrange("p (o e) -> p o e", o=1).broadcast_to([P, E_TILES, E_N]), ALU.is_ge))
            link(dve.tensor_reduce(ex_f[:], cmp[:], AX_X, ALU.add))
            link(dve.tensor_scalar(rt.expert_of[:], ex_f[:], float(E_N - 1), None, ALU.min))
            link(dve.tensor_tensor(tot[:], run[:], tot[:], ALU.subtract))
            link(dve.tensor_tensor(tot[:], tot[:], base[:].rearrange("p (e o) -> p e o", o=1).broadcast_to([P, E_N, NT]),
                                   ALU.add))
            link(dve.tensor_tensor(pos[:], prior, tot[:].rearrange("p e t -> p t e"), ALU.add))
            for k in range(2):
                link(dve.tensor_tensor(cand[:], pos[:], pick[:, k], ALU.mult))
                link(dve.tensor_reduce(slot_f[:, k], cand[:], AX_X, ALU.add))
            link(dve.tensor_copy(rt.slot[:], slot_f[:]))
            link(dve.tensor_scalar(part_i[:, 0], rt.slot[:], P.bit_length() - 1, None, ALU.logical_shift_right))
            link(dve.tensor_scalar(part_i[:, 1], rt.slot[:], P - 1, None, ALU.bitwise_and))
            link(dve.tensor_copy(part_f[:], part_i[:]))
            def spread(x, n):
                return x.rearrange("p k t -> p (k t)").rearrange("p (a o) -> p a o", o=1).broadcast_to([P, 2 * NT, n])

            def repeat(x, n):
                return x.rearrange("p (o n) -> p o n", o=1).broadcast_to([P, 2 * NT, n])

            link(dve.tensor_tensor(hot_lo[:], repeat(col128[:], P), spread(part_f[:, 1], P), ALU.is_equal))
            link(dve.tensor_tensor(hot_hi[:], repeat(col_nb[:], NB), spread(part_f[:, 0], NB), ALU.is_equal))
            for k in range(2):
                rows = hot_hi[:, k * NT:(k + 1) * NT]
                ins = dve.tensor_tensor(rows, rows, token[:].rearrange("p (t o) -> p t o", o=1).broadcast_to([P, NT, NB]),
                                        ALU.mult).then_inc(hot_done, 1)
            dve.wait_ge(placed, 1)
            link(dve.tensor_copy(rt.token_of[:], ps_r[:, 3, 0:NB]))

        @block.tensor
        def _(pe):
            pe.wait_ge(consts, 10)
            pe.wait_ge(w_lo_done, 1)
            with pe.Fori(0, GROUPS // 2) as h:
                for b in range(2):
                    g = 2 * h + b
                    pe.wait_ge(loaded[b], 16 * h + 16)
                    for c in range(DC):
                        pe.wait_ge(x_lo_done, DC * g + c + 1)
                        for t in range(TILES):
                            mm = pe.transpose(ps_x[:, c % 2, t * P:(t + 1) * P], xt[:, b, t, c * P:(c + 1) * P], ident[:])
                        mm.then_inc(x_ready, 1)
                    pe.wait_ge(x_lo_done, 2 + DC * g + DC)
                    pe.wait_ge(lg_read, g)
                    for c in range(DC):
                        cols = bass.ds(g * GT, GT)
                        mm = three_pass(pe, ps_l[:, 0], w_hi[:, c], w_lo[:, c], xt_hi[:, c, cols], xt_lo[:, c, cols],
                                        c == 0, c == DC - 1)
                    mm.then_inc(lg_ready, 1)
            pe.wait_ge(lg_read, GROUPS)
            for t in range(NT):
                mm = pe.transpose(ps_r[:, 0, t * E_N:(t + 1) * E_N], lg_t[:, t * P:(t + 1) * P], ident[0:E_N, 0:E_N])
            mm.then_inc(turned, 1)
            pe.wait_ge(both_done, 1)
            rows = both[:].rearrange("p t e -> p (t e)")
            pe.matmul(ps_r[:, 1, 0:NT * E_N], before[:], rows, start=True, stop=True)
            pe.matmul(ps_r[:, 2, 0:NT * E_N], ones[:], rows, start=True, stop=True).then_inc(counted, 1)
            pe.wait_ge(hot_done, 2)
            for n in range(2 * NT):
                mm = pe.matmul(ps_r[:, 3, 0:NB], hot_lo[:, n], hot_hi[:, n], start=n == 0, stop=n == 2 * NT - 1)
            mm.then_inc(placed, 1)


def experts(nc, x2_rows, w_gate_up, w_down, y_dram, rt):
    with ExitStack() as ctx:
        def sb(name, shape, dt=F32):
            return ctx.enter_context(nc.sbuf_tensor("e_" + name, shape, dt))

        def sem(name):
            return ctx.enter_context(nc.semaphore("e_" + name))

        U = len(E_UNITS)
        gu_raw = sb("gu_raw", [P, DC, 2 * DE])
        gu_hi = sb("gu_hi", [P, DC, 2 * DE], F32R)
        gu_lo = sb("gu_lo", [P, DC, 2 * DE], F32R)
        dn_raw = sb("dn_raw", [P, U, D])
        dn_hi = sb("dn_hi", [P, U, D], F32R)
        dn_lo = sb("dn_lo", [P, U, D], F32R)
        ident = sb("ident", [P, P])
        xg = sb("xg", [P, BLOCKS, D])
        index = sb("index", [P, BLOCKS], I32)
        carrier = sb("carrier", [P, 1])
        x_hi = sb("x_hi", [P, DC, SLOTS], F32R)
        x_lo = sb("x_lo", [P, DC, SLOTS], F32R)
        sg = sb("sg", [P, 2, SLOTS])
        hf = sb("hf", [P, 2, SLOTS])
        h_hi = sb("h_hi", [P, U, SLOTS], F32R)
        h_lo = sb("h_lo", [P, U, SLOTS], F32R)
        y = sb("y", [P, BLOCKS, D])
        ps_h = ctx.enter_context(nc.psum_tensor("e_ps_h", [P, 2, 2, SLOTS], F32))
        ps_x = ctx.enter_context(nc.psum_tensor("e_ps_x", [P, 2, 512], F32))
        ps_y = ctx.enter_context(nc.psum_tensor("e_ps_y", [P, 2, D], F32))

        consts = sem("consts")
        padded = sem("padded")
        gu_loaded = sem("gu_loaded")
        dn_loaded = sem("dn_loaded")
        gu_hi_done = sem("gu_hi_done")
        gu_lo_done = sem("gu_lo_done")
        dn_hi_done = sem("dn_hi_done")
        dn_lo_done = sem("dn_lo_done")
        indexed = sem("indexed")
        carried = sem("carried")
        x_gathered = sem("x_gathered")
        x_ready = sem("x_ready")
        x_hi_done = sem("x_hi_done")
        x_lo_done = sem("x_lo_done")
        h_ready = sem("h_ready")
        silu_done = sem("silu_done")
        h_done = sem("h_done")
        h_hi_done = sem("h_hi_done")
        h_lo_done = sem("h_lo_done")
        y_ready = sem("y_ready")
        y_read = sem("y_read")
        y_stored = sem("y_stored")

        BANKS = 2
        LAST = E_TILES - 1
        y_tiles = y_dram.rearrange("(i b p) d -> i p b d", b=BLOCKS, p=P)

        block = ctx.enter_context(nc.Block())

        @block.sync
        def _(sp):
            def load(i):
                e = sp.value_load(rt.expert_of[0:1, i:i + 1] if isinstance(i, int) else rt.expert_of[0:1, bass.ds(i, 1)],
                                  min_val=0, max_val=E_N - 1)
                sp.wait_ge(gu_lo_done, DC * i)
                sp.dma_start(gu_raw[:], w_gate_up[bass.ds(e, 1)].rearrange("o p c n -> p (o c) n")).then_inc(gu_loaded, 16)
                sp.wait_ge(dn_lo_done, i)
                rows = w_down[bass.ds(e, 1)].rearrange("o h n -> (o h) n")
                sp.dma_start(dn_raw[:, 0:2], rows[0:2 * P].rearrange("(u p) n -> p u n", p=P)).then_inc(dn_loaded, 16)
                sp.dma_start(dn_raw[0:E_UNITS[2], 2], rows[2 * P:DE]).then_inc(dn_loaded, 16)

            load(0)
            with sp.Fori(0, LAST) as i:
                load(i + 1)
                sp.wait_ge(y_read, BANKS + BLOCKS * i + BLOCKS)
                sp.dma_start(y_tiles[bass.ds(i, 1)].rearrange("o p b d -> p (o b) d"), y[:]).then_inc(y_stored, 16)
            sp.wait_ge(y_read, BANKS + BLOCKS * E_TILES)
            sp.dma_start(y_tiles[LAST], y[:]).then_inc(y_stored, 16)
            sp.wait_ge(y_stored, 16 * E_TILES)

        @block.gpsimd
        def _(pool):
            pool.memset(ident[:], 0.0).then_inc(consts, 1)
            pool.wait_ge(consts, 1)
            pool.affine_select(out=ident[:], in_=ident[:], compare_op=ALU.not_equal, fill=1.0, base=0,
                               pattern=[[-1, P]], channel_multiplier=1).then_inc(consts, 1)

            pool.memset(carrier[:], 0.0).then_inc(carried, 1)

            def gather(i):
                pool.wait_ge(x_ready, DC * i)
                pool.wait_ge(carried, 1 + i)
                pool.tensor_copy(index[:], rt.token_of[:, bass.ds(BLOCKS * i, BLOCKS)]).then_inc(indexed, 1)
                pool.wait_ge(indexed, i + 1)
                pool.tensor_tensor(carrier[:], carrier[:], carrier[:], ALU.add).then_inc(carried, 1)
                for b in range(BLOCKS):
                    pool.indirect_dma_start(xg[:, b], None, x2_rows,
                                            bass.IndirectOffsetOnAxis(ap=index[:, b:b + 1], axis=0)).then_inc(x_gathered, 16)

            def split_down(i):
                pool.wait_ge(dn_hi_done, i + 1)
                pool.tensor_tensor(dn_lo[:], dn_raw[:], dn_hi[:].bitcast(F32), ALU.subtract).then_inc(dn_lo_done, 1)

            gather(0)
            with pool.Fori(0, LAST) as i:
                gather(i + 1)
                split_down(i)
            split_down(LAST)

        @block.scalar
        def _(act):
            act.preload_act_table_set("silu_and_others")

            def split_x(i, c):
                act.wait_ge(x_ready, DC * i + c + 1)
                act.activation(x_hi[:, c], ps_x[:, c % 2], ACT.Copy).then_inc(x_hi_done, 1)

            def split_gate_up(i, c):
                if c == 0:
                    act.wait_ge(gu_loaded, 16 * i + 16)
                    act.wait_ge(h_ready, U * i)
                act.activation(gu_hi[:, c], gu_raw[:, c], ACT.Copy).then_inc(gu_hi_done, 1)

            def split_x_and_gate_up(i):
                split_x(i, 0)
                split_x(i, 1)
                split_gate_up(i, 0)
                split_x(i, 2)
                split_gate_up(i, 1)
                split_x(i, 3)
                split_gate_up(i, 2)
                split_gate_up(i, 3)

            def split_down(i):
                act.wait_ge(dn_loaded, 32 * i + 32)
                act.wait_ge(y_ready, BLOCKS * i)
                act.activation(dn_hi[:], dn_raw[:], ACT.Copy).then_inc(dn_hi_done, 1)

            def hidden(i):
                for u, n in enumerate(E_UNITS):
                    act.wait_ge(h_ready, U * i + u + 1)
                    act.activation(sg[0:n, u % 2], ps_h[0:n, u % 2, 0], ACT.Silu).then_inc(silu_done, 1)
                    if u == 0:
                        split_down(i)
                    act.wait_ge(h_done, U * i + u + 1)
                    act.activation(h_hi[0:n, u], hf[0:n, u % 2], ACT.Copy).then_inc(h_hi_done, 1)

            act.wait_ge(padded, 1)
            split_x_and_gate_up(0)
            with act.Fori(0, LAST) as i:
                hidden(i)
                split_x_and_gate_up(i + 1)
            hidden(LAST)

        @block.vector
        def _(dve):
            dve.memset(dn_raw[E_UNITS[2]:P, 2], 0.0).then_inc(padded, 1)
            dve.sem_inc(x_lo_done, BANKS)
            dve.sem_inc(y_read, BANKS)

            def split_x(i, c):
                dve.wait_ge(x_hi_done, DC * i + c + 1)
                dve.tensor_tensor(x_lo[:, c], ps_x[:, c % 2], x_hi[:, c].bitcast(F32), ALU.subtract)\
                    .then_inc(x_lo_done, 1)

            def split_gate_up(i, c):
                dve.wait_ge(gu_hi_done, DC * i + c + 1)
                dve.tensor_tensor(gu_lo[:, c], gu_raw[:, c], gu_hi[:, c].bitcast(F32), ALU.subtract)\
                    .then_inc(gu_lo_done, 1)

            def hidden(i):
                for u, n in enumerate(E_UNITS):
                    dve.wait_ge(silu_done, U * i + u + 1)
                    dve.wait_ge(h_lo_done, U * i + max(0, u - 1))
                    dve.tensor_tensor(hf[0:n, u % 2], ps_h[0:n, u % 2, 1], sg[0:n, u % 2], ALU.mult).then_inc(h_done, 1)
                    dve.wait_ge(h_hi_done, U * i + u + 1)
                    dve.tensor_tensor(h_lo[0:n, u], hf[0:n, u % 2], h_hi[0:n, u].bitcast(F32), ALU.subtract)\
                        .then_inc(h_lo_done, 1)

            def output(i, b):
                dve.wait_ge(y_ready, BLOCKS * i + b + 1)
                if b == 0:
                    dve.wait_ge(y_stored, 16 * i)
                dve.tensor_copy(y[:, b], ps_y[:, b % 2]).then_inc(y_read, 1)

            for c in range(DC):
                split_x(0, c)
            for c in range(DC):
                split_gate_up(0, c)
            with dve.Fori(0, LAST) as i:
                hidden(i)
                split_x(i + 1, 0)
                split_x(i + 1, 1)
                output(i, 0)
                output(i, 1)
                split_gate_up(i + 1, 0)
                split_x(i + 1, 2)
                split_gate_up(i + 1, 1)
                output(i, 2)
                split_x(i + 1, 3)
                split_gate_up(i + 1, 2)
                split_gate_up(i + 1, 3)
                output(i, 3)
            hidden(LAST)
            for b in range(BLOCKS):
                output(LAST, b)

        @block.tensor
        def _(pe):
            def turn(i, c):
                if c == 0:
                    pe.wait_ge(x_gathered, 16 * BLOCKS * i + 16 * BLOCKS)
                pe.wait_ge(x_lo_done, DC * i + c + 1)
                for b in range(BLOCKS):
                    mm = pe.transpose(ps_x[:, c % 2, b * P:(b + 1) * P], xg[:, b, c * P:(c + 1) * P], ident[:])
                mm.then_inc(x_ready, 1)

            def hidden(i, u):
                n = E_UNITS[u]
                pe.wait_ge(h_done, U * i + max(0, u - 1))
                for s in range(2):
                    at = slice(s * DE + u * P, s * DE + u * P + n)
                    for c in range(DC):
                        if u == 0 and s == 0:
                            pe.wait_ge(x_lo_done, BANKS + DC * i + c + 1)
                            pe.wait_ge(gu_lo_done, DC * i + c + 1)
                        mm = three_pass(pe, ps_h[0:n, u % 2, s], gu_hi[:, c, at], gu_lo[:, c, at], x_hi[:, c], x_lo[:, c],
                                        c == 0, c == DC - 1)
                mm.then_inc(h_ready, 1)

            def down(i, b, units):
                for u in units:
                    n = E_UNITS[u]
                    if b == 0:
                        if u == 0:
                            pe.wait_ge(dn_lo_done, i + 1)
                        pe.wait_ge(h_lo_done, U * i + u + 1)
                    if u == 0:
                        pe.wait_ge(y_read, BLOCKS * i + b + 1)
                    mm = three_pass(pe, ps_y[:, b % 2], h_hi[0:n, u, b * P:(b + 1) * P], h_lo[0:n, u, b * P:(b + 1) * P],
                                    dn_hi[0:n, u], dn_lo[0:n, u], u == 0, u == U - 1)
                    if u == U - 1:
                        mm.then_inc(y_ready, 1)

            def tile(i, more):
                hidden(i, 0)
                hidden(i, 1)
                if more:
                    turn(i + 1, 0)
                    turn(i + 1, 1)
                hidden(i, 2)
                down(i, 0, (0, 1))
                down(i, 1, (0, 1))
                down(i, 0, (2,))
                down(i, 1, (2,))
                if more:
                    turn(i + 1, 2)
                down(i, 2, range(U))
                if more:
                    turn(i + 1, 3)
                down(i, 3, range(U))

            pe.wait_ge(consts, 2)
            for c in range(DC):
                turn(0, c)
            with pe.Fori(0, LAST) as i:
                tile(i, True)
            tile(LAST, False)


def shared_and_combine(nc, w_gate_up, w_down, x2_tiles, y_dram, xt_hi, xt_lo, out_tiles, rt):
    with ExitStack() as ctx:
        def sb(name, shape, dt=F32):
            return ctx.enter_context(nc.sbuf_tensor("c_" + name, shape, dt))

        def sem(name):
            return ctx.enter_context(nc.semaphore("c_" + name))

        U = len(S_UNITS)
        w_raw = sb("w_raw", [P, 2, 2 * DS])
        gu_hi = sb("gu_hi", [P, DC, 2 * DS], F32R)
        gu_lo = sb("gu_lo", [P, DC, 2 * DS], F32R)
        dn_hi = sb("dn_hi", [P, U, D], F32R)
        dn_lo = sb("dn_lo", [P, U, D], F32R)
        sg = sb("sg", [P, 2, GT])
        hf = sb("hf", [P, 2, GT])
        h_hi = sb("h_hi", [P, U, GT], F32R)
        h_lo = sb("h_lo", [P, U, GT], F32R)
        res = sb("res", [P, TILES, D])
        y = sb("y", [P, 2, TILES, D])
        index = sb("index", [P, 2, TILES], I32)
        carrier = sb("carrier", [P, 1])
        ln = Moments(sb, "c", TILES)
        ps_h = ctx.enter_context(nc.psum_tensor("c_ps_h", [P, 2, 2, GT], F32))
        ps_out = ctx.enter_context(nc.psum_tensor("c_ps_out", [P, TILES, D], F32))

        w_loaded = [sem("w_loaded_even"), sem("w_loaded_odd")]
        w_hi_done = sem("w_hi_done")
        w_lo_done = sem("w_lo_done")
        ln_const = sem("ln_const")
        res_loaded = sem("res_loaded")
        indexed = sem("indexed")
        carried = sem("carried")
        y_gathered = sem("y_gathered")
        h_ready = sem("h_ready")
        silu_done = sem("silu_done")
        h_done = sem("h_done")
        h_hi_done = sem("h_hi_done")
        h_lo_done = sem("h_lo_done")
        out_done = sem("out_done")
        out_free = sem("out_free")
        add_step = sem("add_step")
        y_read = sem("y_read")
        ln_step = sem("ln_step")
        var_done = sem("var_done")
        rstd_done = sem("rstd_done")
        out_ready = sem("out_ready")
        out_stored = sem("out_stored")

        BANKS = 2
        LU = S_UNITS[-1]
        FULL = 4 * P
        parts = [(gu_hi[:, c], gu_lo[:, c], P, 2 * DS, w_gate_up[:, c]) for c in range(DC)]
        for u, n, rows in ((0, P, w_down[0:2 * P]), (2, P, w_down[2 * P:FULL]), (4, LU, w_down[FULL:DS])):
            parts.append((dn_hi[0:n, u:u + 2].rearrange("p u n -> p (u n)"), dn_lo[0:n, u:u + 2].rearrange("p u n -> p (u n)"),
                          n, 2 * D, rows.rearrange("(u p) n -> p u n", u=2)))

        block = ctx.enter_context(nc.Block())

        @block.sync
        def _(sp):
            for k, (_, _, n, cols, src) in enumerate(parts):
                if k >= 2:
                    sp.wait_ge(w_lo_done, k - 1)
                dst = w_raw[0:n, k % 2, 0:cols]
                if k >= DC:
                    dst = dst.rearrange("p (u n) -> p u n", u=2)
                sp.dma_start(dst, src).then_inc(w_loaded[k % 2], 16)
            with sp.Fori(0, GROUPS) as g:
                sp.wait_ge(out_stored, 16 * g)
                sp.dma_start(res[:], x2_tiles[bass.ds(g, 1)].rearrange("o p t d -> p (o t) d")).then_inc(res_loaded, 16)
                sp.wait_ge(out_ready, TILES * g + TILES)
                sp.dma_start(out_tiles[bass.ds(g, 1)].rearrange("o p t d -> p (o t) d"), res[:]).then_inc(out_stored, 16)
            sp.wait_ge(out_stored, 16 * GROUPS)

        @block.gpsimd
        def _(pool):
            pool.memset(ln.power[:], -0.5).then_inc(ln_const, 1)
            pool.memset(carrier[:], 0.0).then_inc(carried, 1)
            pool.wait_ge(ln_const, 1)
            with pool.Fori(0, GROUPS) as g:
                pool.wait_ge(y_read, TILES * g)
                pool.wait_ge(carried, 1 + g)
                pool.tensor_copy(index[:], rt.slot[:, :, bass.ds(TILES * g, TILES)]).then_inc(indexed, 1)
                pool.wait_ge(indexed, g + 1)
                pool.tensor_tensor(carrier[:], carrier[:], carrier[:], ALU.add).then_inc(carried, 1)
                for t in range(TILES):
                    for k in range(2):
                        pool.indirect_dma_start(y[:, k, t], None, y_dram,
                                                bass.IndirectOffsetOnAxis(ap=index[:, k, t:t + 1], axis=0))\
                            .then_inc(y_gathered, 16)
                pool.wait_ge(var_done, g + 1)
                pool.tensor_tensor(ln.rstd[:], ln.var[:], ln.power[:], ALU.pow).then_inc(rstd_done, 1)

        @block.scalar
        def _(act):
            for k, (hi, _, n, cols, _) in enumerate(parts):
                act.wait_ge(w_loaded[k % 2], 16 * (k // 2) + 16)
                act.activation(hi, w_raw[0:n, k % 2, 0:cols], ACT.Copy).then_inc(w_hi_done, 1)

            with act.Fori(0, GROUPS) as g:
                def rounded(u):
                    act.wait_ge(h_done, U * g + u + 1)
                    if u == 0:
                        act.wait_ge(out_done, TILES * g)
                    n = S_UNITS[u]
                    act.activation(h_hi[0:n, u], hf[0:n, u % 2], ACT.Copy).then_inc(h_hi_done, 1)

                for u, n in enumerate(S_UNITS):
                    act.wait_ge(h_ready, U * g + u + 1)
                    act.activation(sg[0:n, u % 2], ps_h[0:n, u % 2, 0], ACT.Silu).then_inc(silu_done, 1)
                    if u:
                        rounded(u - 1)
                rounded(U - 1)

        @block.vector
        def _(dve):
            for k, (hi, lo, n, cols, _) in enumerate(parts):
                dve.wait_ge(w_hi_done, k + 1)
                dve.tensor_tensor(lo, w_raw[0:n, k % 2, 0:cols], hi.bitcast(F32), ALU.subtract).then_inc(w_lo_done, 1)

            with dve.Fori(0, GROUPS) as g:
                def rest(u):
                    n = S_UNITS[u]
                    dve.wait_ge(h_hi_done, U * g + u + 1)
                    dve.tensor_tensor(h_lo[0:n, u], hf[0:n, u % 2], h_hi[0:n, u].bitcast(F32), ALU.subtract)\
                        .then_inc(h_lo_done, 1)

                for u, n in enumerate(S_UNITS):
                    dve.wait_ge(silu_done, U * g + u + 1)
                    dve.wait_ge(h_lo_done, U * g + u - 1 if u else U * g)
                    dve.tensor_tensor(hf[0:n, u % 2], ps_h[0:n, u % 2, 1], sg[0:n, u % 2], ALU.mult).then_inc(h_done, 1)
                    if u:
                        rest(u - 1)
                rest(U - 1)
                dve.wait_ge(res_loaded, 16 * g + 16)
                for t in range(TILES):
                    dve.wait_ge(out_done, TILES * g + t + 1)
                    dve.tensor_tensor(res[:, t], ps_out[:, t], res[:, t], ALU.add).then_inc(out_free, 1)
                dve.wait_ge(y_gathered, 2 * TILES * 16 * (g + 1))
                dve.wait_ge(out_free, TILES * g + TILES)
                for t in range(TILES):
                    w = rt.weight[:, 0, bass.ds(TILES * g + t, 1)]
                    dve.scalar_tensor_tensor(res[:, t], y[:, 0, t], w, res[:, t], ALU.mult, ALU.add).then_inc(add_step, 1)
                dve.wait_ge(add_step, TILES * g + TILES)
                for t in range(TILES):
                    w = rt.weight[:, 1, bass.ds(TILES * g + t, 1)]
                    dve.scalar_tensor_tensor(res[:, t], y[:, 1, t], w, res[:, t], ALU.mult, ALU.add).then_inc(y_read, 1)
                dve.wait_ge(y_read, TILES * g + TILES)
                moments(dve, res, ln, ln_step, (TILES + 6) * g, var_done)
                dve.wait_ge(rstd_done, g + 1)
                for t in range(TILES):
                    dve.tensor_scalar(res[:, t], res[:, t], ln.mean[:, t:t + 1], ln.rstd[:, t:t + 1],
                                      ALU.subtract, ALU.mult).then_inc(out_ready, 1)

        @block.tensor
        def _(pe):
            pe.wait_ge(w_lo_done, len(parts))
            with pe.Fori(0, GROUPS) as g:
                cols = bass.ds(g * GT, GT)
                for u, n in enumerate(S_UNITS):
                    pe.wait_ge(h_done, U * g + u - 1 if u else U * g)
                    row = sum(S_UNITS[:u])
                    for s in range(2):
                        at = slice(s * DS + row, s * DS + row + n)
                        for c in range(DC):
                            mm = three_pass(pe, ps_h[0:n, u % 2, s], gu_hi[:, c, at], gu_lo[:, c, at],
                                            xt_hi[:, c, cols], xt_lo[:, c, cols], c == 0, c == DC - 1)
                    mm.then_inc(h_ready, 1)
                pe.wait_ge(out_free, TILES * g)
                for u, n in enumerate(S_UNITS):
                    pe.wait_ge(h_lo_done, U * g + u + 1)
                    for t in range(TILES):
                        mm = three_pass(pe, ps_out[:, t], h_hi[0:n, u, t * P:(t + 1) * P], h_lo[0:n, u, t * P:(t + 1) * P],
                                        dn_hi[0:n, u], dn_lo[0:n, u], u == 0, u == U - 1)
                        if u == U - 1:
                            mm.then_inc(out_done, 1)


def program(nc, x_t, x_tok, w_in, w_out, conv_w, conv_b, gain, ctx_t, w_q, w_kv, w_o, w_router, we_gate_up, we_down,
            ws_gate_up, ws_down, out):
    x1 = nc.dram_tensor("x1", (GROUPS, P, TILES, D), F32, kind="Internal").ap()
    x2 = nc.dram_tensor("x2", (T, D), F32, kind="Internal").ap()
    y = nc.dram_tensor("y_slots", (E_TILES * SLOTS, D), F32, kind="Internal").ap()
    x2_tiles = x2.rearrange("(g t p) d -> g p t d", p=P, t=TILES)
    out_tiles = out.rearrange("(g b) (s p) d -> g p (b s) d", b=GB, p=P)
    with ExitStack() as ctx:
        arena = ctx.enter_context(nc.sbuf_tensor("arena", [P, 2 * JC * DC * 2 * P], F32R))[:]
        cross = CrossWeights(arena, w_q, w_kv, w_o)
        gated_conv(nc, x_t, x_tok, w_in, w_out, conv_w, conv_b, gain, x1, arena, cross.units)
        cross_attention(nc, x1, ctx_t, cross, x2_tiles)
    with ExitStack() as ctx:
        def sb(name, shape, dt=F32):
            return ctx.enter_context(nc.sbuf_tensor("f_" + name, shape, dt))

        rt = Routing(sb)
        xt_hi = sb("xt_hi", [P, DC, T], F32R)
        xt_lo = sb("xt_lo", [P, DC, T], F32R)
        route(nc, x2_tiles, w_router, xt_hi, xt_lo, rt)
        experts(nc, x2, we_gate_up, we_down, y, rt)
        shared_and_combine(nc, ws_gate_up, ws_down, x2_tiles, y, xt_hi, xt_lo, out_tiles, rt)


def layouts(inputs):
    import numpy as np

    def get(name):
        return np.asarray(inputs["L0_" + name])

    def square(name):
        return get(name).T.reshape(2, 2, P, D).transpose(0, 2, 1, 3).reshape(2, P, 2 * D)

    def gate_up(gate, up, width):
        both = np.stack([get(gate), get(up)], axis=-2)
        lead = both.shape[:-3]
        both = both.reshape(*lead, DC, P, 2 * width)
        return np.swapaxes(both, -3, -2)

    x = np.asarray(inputs["x"])
    ctx = np.asarray(inputs["ctx_512"])
    out = {
        "x_t": x.reshape(GROUPS, GT, DC, P).transpose(0, 3, 2, 1),
        "x_tok": x.reshape(GROUPS, TILES, P, D).transpose(0, 2, 1, 3),
        "w_in": get("attn_w_in").reshape(2, JC, P, DC, P).transpose(1, 4, 3, 0, 2).reshape(JC, P, 1024),
        "w_out": get("attn_w_out").reshape(D, JC // 2, 2, P).transpose(1, 3, 2, 0).reshape(JC // 2, P, 1024),
        "conv_w": get("attn_conv_w").reshape(JC, P, TAPS).transpose(1, 0, 2),
        "conv_b": get("attn_conv_b").reshape(JC, P).T,
        "gain": get("attn_D").reshape(JC, P).T,
        "ctx_t": ctx.reshape(GROUPS, GT, L).transpose(0, 2, 1),
        "w_q": square("xattn_Wq"),
        "w_kv": get("xattn_Wkv_expand").T,
        "w_o": square("xattn_Wout"),
        "w_router": get("ffn_W_router").reshape(DC, P, E_N).transpose(1, 0, 2),
        "we_gate_up": gate_up("ffn_We_gate", "ffn_We_up", DE),
        "we_down": get("ffn_We_down"),
        "ws_gate_up": gate_up("ffn_Ws_gate", "ffn_Ws_up", DS),
        "ws_down": get("ffn_Ws_down"),
    }
    return {k: np.ascontiguousarray(v) for k, v in out.items()}


def kernel(**inputs):
    import concourse.bacc as bacc
    import numpy as np
    from concourse.bass_utils import run_bass_kernel_spmd

    nc = bacc.Bacc("TRN2", target_bir_lowering=False, num_devices=1)
    arrays = layouts(inputs)
    args = [nc.dram_tensor(name, a.shape, mybir.dt.from_np(a.dtype), kind="ExternalInput").ap()
            for name, a in arrays.items()]
    out = nc.dram_tensor("out", (B, S, D), F32, kind="ExternalOutput").ap()
    program(nc, *args, out)
    result = run_bass_kernel_spmd(nc, [arrays], core_ids=[0])
    return np.asarray(result.results[0]["out"])
```

```python
from contextlib import ExitStack

import concourse.bass as bass
from concourse import mybir

F32 = mybir.dt.float32
F32R = mybir.dt.float32r
BF16 = mybir.dt.bfloat16
I32 = mybir.dt.int32
U32 = mybir.dt.uint32
ALU = mybir.AluOpType
ACT = mybir.ActivationFunctionType
AX_X = mybir.AxisListType.X

P = 128
B, S, D = 8, 256, 512
T = B * S
GT = 512
GROUPS = T // GT
GB = GT // S
TILES = GT // P
DC = D // P
DI = 1024
JC = DI // P
TAPS = 4
EPS = 1e-5


def three_pass(pe, out, a_hi, a_lo, b_hi, b_lo, first, last):
    pe.matmul(out, a_hi, b_lo, start=first, stop=False)
    pe.matmul(out, a_lo, b_hi, start=False, stop=False)
    return pe.matmul(out, a_hi, b_hi, start=False, stop=last)


class Moments:

    def __init__(self, sb, name, n):
        self.n = n
        self.stats = sb(name + "_ln_stats", [P, n, 6])
        self.sum = sb(name + "_ln_sum", [P, n])
        self.diff = sb(name + "_ln_diff", [P, n])
        self.sq = sb(name + "_ln_sq", [P, n])
        self.mean = sb(name + "_ln_mean", [P, n])
        self.sq_eps = sb(name + "_ln_sq_eps", [P, n])
        self.diff_sq = sb(name + "_ln_diff_sq", [P, n])
        self.var = sb(name + "_ln_var", [P, n])
        self.power = sb(name + "_ln_power", [P, n])
        self.rstd = sb(name + "_ln_rstd", [P, n])


def moments(dve, x, ln, step, base, var_done):
    n, s = ln.n, ln.stats
    for t in range(n):
        dve.bn_stats(s[:, t], x[:, t]).then_inc(step, 1)
    dve.wait_ge(step, base + n)
    dve.tensor_tensor(ln.sum[:], s[:, :, 1], s[:, :, 4], ALU.add).then_inc(step, 1)
    dve.tensor_tensor(ln.diff[:], s[:, :, 1], s[:, :, 4], ALU.subtract).then_inc(step, 1)
    dve.tensor_tensor(ln.sq[:], s[:, :, 2], s[:, :, 5], ALU.add).then_inc(step, 1)
    dve.wait_ge(step, base + n + 3)
    dve.tensor_scalar(ln.mean[:], ln.sum[:], 0.5, None, ALU.mult).then_inc(step, 1)
    dve.tensor_scalar(ln.sq_eps[:], ln.sq[:], 1.0 / D, EPS, ALU.mult, ALU.add).then_inc(step, 1)
    dve.scalar_tensor_tensor(ln.diff_sq[:], ln.diff[:], 0.25, ln.diff[:], ALU.mult, ALU.mult).then_inc(step, 1)
    dve.wait_ge(step, base + n + 6)
    dve.tensor_tensor(ln.var[:], ln.sq_eps[:], ln.diff_sq[:], ALU.add).then_inc(var_done, 1)


def gated_conv(nc, x_t, x_tok, w_in, w_out, conv_w, conv_b, gain, x1_dram, arena, following):
    with ExitStack() as ctx:
        def sb(name, shape, dt=F32):
            return ctx.enter_context(nc.sbuf_tensor(name, shape, dt))

        def sem(name):
            return ctx.enter_context(nc.semaphore(name))

        w_raw = sb("a_w_raw", [P, 2, 1024])
        half = JC * DC * 2 * P
        wi_hi = arena[:, 0:half].rearrange("p (j c s m) -> p j c s m", j=JC, c=DC, s=2)
        wi_lo = arena[:, half:2 * half].rearrange("p (j c s m) -> p j c s m", j=JC, c=DC, s=2)
        wo_hi = sb("a_wo_hi", [P, JC, D], F32R)
        wo_lo = sb("a_wo_lo", [P, JC, D], F32R)
        taps = sb("a_taps", [P, JC, TAPS])
        bias = sb("a_bias", [P, JC])
        dgain = sb("a_dgain", [P, JC])
        x_raw = sb("a_x_raw", [P, DC, GT])
        x_hi = sb("a_x_hi", [P, DC, GT], F32R)
        x_lo = sb("a_x_lo", [P, DC, GT], F32R)
        xc = sb("a_xc", [P, 2, GB, S])
        sg = sb("a_sg", [P, 2, GT])
        hf = sb("a_hf", [P, 2, GT])
        h_hi = sb("a_h_hi", [P, JC, GT], F32R)
        h_lo = sb("a_h_lo", [P, JC, GT], F32R)
        xt = sb("a_xt", [P, TILES, D])
        x1 = sb("a_x1", [P, TILES, D])
        ln = Moments(sb, "a", TILES)
        ps_proj = ctx.enter_context(nc.psum_tensor("a_ps_proj", [P, 2, 2, GT], F32))
        ps_out = ctx.enter_context(nc.psum_tensor("a_ps_out", [P, TILES, D], F32))

        w_loaded = [sem("a_w_loaded_even"), sem("a_w_loaded_odd")]
        w_hi_done = sem("a_w_hi_done")
        w_lo_done = sem("a_w_lo_done")
        consts_loaded = sem("a_consts_loaded")
        x_loaded = sem("a_x_loaded")
        xt_loaded = sem("a_xt_loaded")
        x_hi_done = sem("a_x_hi_done")
        x_lo_done = sem("a_x_lo_done")
        proj_done = sem("a_proj_done")
        gate_free = sem("a_gate_free")
        tap_last = sem("a_tap_last")
        tap_step = sem("a_tap_step")
        conv_done = sem("a_conv_done")
        silu_done = sem("a_silu_done")
        h_done = sem("a_h_done")
        h_hi_done = sem("a_h_hi_done")
        h_lo_done = sem("a_h_lo_done")
        out_done = sem("a_out_done")
        out_free = sem("a_out_free")
        ln_step = sem("a_ln_step")
        ln_const = sem("a_ln_const")
        var_done = sem("a_var_done")
        rstd_done = sem("a_rstd_done")
        x1_ready = sem("a_x1_ready")
        x1_stored = sem("a_x1_stored")

        BANKS = 2
        W_UNITS = JC + JC // 2
        W_AHEAD = 3
        ALL_UNITS = W_UNITS + len(following)

        def w_unit(u, hi):
            if u >= W_UNITS:
                return following[u - W_UNITS][1 if hi else 2]
            if u < JC:
                return (wi_hi if hi else wi_lo)[:, u].rearrange("p c s m -> p (c s m)")
            c = 2 * (u - JC)
            return (wo_hi if hi else wo_lo)[:, c:c + 2].rearrange("p c n -> p (c n)")

        block = ctx.enter_context(nc.Block())

        @block.sync
        def _(sp):
            sp.dma_start(x_raw[:], x_t[0]).then_inc(x_loaded, 16)
            sp.dma_start(taps[:], conv_w).then_inc(consts_loaded, 16)
            sp.dma_start(bias[:], conv_b).then_inc(consts_loaded, 16)
            sp.dma_start(dgain[:], gain).then_inc(consts_loaded, 16)
            for u in range(W_UNITS):
                if u >= 2:
                    sp.wait_ge(w_lo_done, u - 1)
                src = w_in[u] if u < JC else w_out[u - JC]
                sp.dma_start(w_raw[:, u % 2], src).then_inc(w_loaded[u % 2], 16)
            with sp.Fori(0, GROUPS - 1) as g:
                sp.wait_ge(x1_ready, TILES * g)
                sp.dma_start(xt[:], x_tok[bass.ds(g, 1)].rearrange("o p t d -> p (o t) d")).then_inc(xt_loaded, 16)
                sp.wait_ge(x_lo_done, g + 1)
                sp.dma_start(x_raw[:], x_t[bass.ds(g + 1, 1)].rearrange("o p c t -> p (o c) t")).then_inc(x_loaded, 16)
            sp.wait_ge(x1_ready, TILES * (GROUPS - 1))
            sp.dma_start(xt[:], x_tok[GROUPS - 1]).then_inc(xt_loaded, 16)
            for u in range(W_UNITS, ALL_UNITS):
                sp.wait_ge(w_lo_done, u - 1)
                sp.dma_start(w_raw[:, u % 2], following[u - W_UNITS][0]).then_inc(w_loaded[u % 2], 16)

        @block.gpsimd
        def _(pool):
            def split_x(g):
                pool.wait_ge(x_hi_done, g + 1)
                pool.tensor_tensor(x_lo[:], x_raw[:], x_hi[:].bitcast(F32), ALU.subtract).then_inc(x_lo_done, 1)

            def root(g):
                pool.wait_ge(ln_const, 1)
                pool.wait_ge(var_done, g + 1)
                pool.tensor_tensor(ln.rstd[:], ln.var[:], ln.power[:], ALU.pow).then_inc(rstd_done, 1)

            pool.memset(ln.power[:], -0.5).then_inc(ln_const, 1)
            def split_w(u):
                pool.wait_ge(w_hi_done, u + 1)
                pool.tensor_tensor(w_unit(u, False), w_raw[:, u % 2], w_unit(u, True).bitcast(F32),
                                   ALU.subtract).then_inc(w_lo_done, 1)

            split_x(0)
            for u in range(W_UNITS):
                split_w(u)
            with pool.Fori(0, GROUPS - 1) as g:
                split_x(g + 1)
                root(g)
                pool.wait_ge(x1_ready, TILES * g + TILES)
                pool.dma_start(x1_dram[bass.ds(g, 1)].rearrange("o p t d -> p (o t) d"), x1[:]).then_inc(x1_stored, 16)
            for u in range(W_UNITS, ALL_UNITS):
                split_w(u)
            root(GROUPS - 1)
            pool.wait_ge(x1_ready, TILES * GROUPS)
            pool.dma_start(x1_dram[GROUPS - 1], x1[:]).then_inc(x1_stored, 16)
            pool.wait_ge(x1_stored, 16 * GROUPS)

        @block.scalar
        def _(act):
            act.preload_act_table_set("silu_and_others")

            def split_x(g):
                act.wait_ge(x_loaded, 16 * g + 16)
                act.wait_ge(proj_done, JC * g)
                act.activation(x_hi[:], x_raw[:], ACT.Copy).then_inc(x_hi_done, 1)

            def h_round(g, j):
                act.wait_ge(h_done, JC * g + j + 1)
                if j == 0:
                    act.wait_ge(out_done, TILES * g)
                act.activation(h_hi[:, j], hf[:, j % 2], ACT.Copy).then_inc(h_hi_done, 1)

            def split_w(u):
                act.wait_ge(w_loaded[u % 2], 16 * (u // 2) + 16)
                act.activation(w_unit(u, True), w_raw[:, u % 2], ACT.Copy).then_inc(w_hi_done, 1)

            split_x(0)
            act.sem_inc(gate_free, BANKS)
            for u in range(W_AHEAD):
                split_w(u)
            act.wait_ge(consts_loaded, 48)

            def group(g):
                for j in range(JC):
                    xcj = xc[:, j % 2].rearrange("p b s -> p (b s)")
                    act.wait_ge(proj_done, JC * g + j + 1)
                    act.activation(xcj, ps_proj[:, j % 2, 0], ACT.Identity,
                                   scale=taps[:, j, TAPS - 1:TAPS], bias=bias[:, j:j + 1]).then_inc(tap_last, 1)
                    act.activation(sg[:, j % 2], ps_proj[:, j % 2, 1], ACT.Silu).then_inc(gate_free, 1)
                    if isinstance(g, int) and g == 0:
                        for u in range(W_AHEAD + 2 * j, min(W_AHEAD + 2 * j + 2, W_UNITS)):
                            split_w(u)
                    if j:
                        h_round(g, j - 1)
                    act.wait_ge(conv_done, BANKS + JC * g + j + 1)
                    act.activation(xcj, xcj, ACT.Silu).then_inc(silu_done, 1)
                h_round(g, JC - 1)

            group(0)
            split_x(1)
            with act.Fori(1, GROUPS - 1) as g:
                group(g)
                split_x(g + 1)
            group(GROUPS - 1)
            for u in range(W_UNITS, ALL_UNITS):
                split_w(u)

        @block.vector
        def _(dve):
            dve.sem_inc(conv_done, BANKS)
            dve.wait_ge(consts_loaded, 48)

            def h_rest(g, j):
                dve.wait_ge(h_hi_done, JC * g + j + 1)
                dve.tensor_tensor(h_lo[:, j], hf[:, j % 2], h_hi[:, j].bitcast(F32), ALU.subtract).then_inc(h_lo_done, 1)

            with dve.Fori(0, GROUPS) as g:
                for j in range(JC):
                    dve.wait_ge(tap_last, JC * g + j + 1)
                    xi = ps_proj[:, j % 2, 0].rearrange("p (b s) -> p b s", b=GB)
                    for s in range(1, TAPS):
                        if s > 1:
                            dve.wait_ge(tap_step, (TAPS - 2) * (JC * g + j) + s - 1)
                        ins = dve.scalar_tensor_tensor(xc[:, j % 2, :, s:S], xi[:, :, 0:S - s],
                                                       taps[:, j, TAPS - 1 - s:TAPS - s], xc[:, j % 2, :, s:S],
                                                       ALU.mult, ALU.add)
                        ins.then_inc(tap_step if s < TAPS - 1 else conv_done, 1)
                    if j:
                        h_rest(g, j - 1)
                    dve.wait_ge(silu_done, JC * g + j + 1)
                    dve.scalar_tensor_tensor(hf[:, j % 2], xc[:, j % 2].rearrange("p b s -> p (b s)"),
                                             dgain[:, j:j + 1], sg[:, j % 2], ALU.mult, ALU.mult).then_inc(h_done, 1)
                h_rest(g, JC - 1)
                dve.wait_ge(xt_loaded, 16 * g + 16)
                for t in range(TILES):
                    dve.wait_ge(out_done, TILES * g + t + 1)
                    dve.tensor_tensor(xt[:, t], ps_out[:, t], xt[:, t], ALU.add).then_inc(out_free, 1)
                dve.wait_ge(out_free, TILES * g + TILES)
                moments(dve, xt, ln, ln_step, (TILES + 6) * g, var_done)
                dve.wait_ge(rstd_done, g + 1)
                dve.wait_ge(x1_stored, 16 * g)
                for t in range(TILES):
                    dve.tensor_scalar(x1[:, t], xt[:, t], ln.mean[:, t:t + 1], ln.rstd[:, t:t + 1],
                                      ALU.subtract, ALU.mult).then_inc(x1_ready, 1)

        @block.tensor
        def _(pe):
            with pe.Fori(0, GROUPS) as g:
                pe.wait_ge(x_lo_done, g + 1)
                for j in range(JC):
                    pe.wait_ge(w_lo_done, j + 1)
                    for side, free in ((0, conv_done), (1, gate_free)):
                        pe.wait_ge(free, JC * g + j + 1)
                        for c in range(DC):
                            mm = three_pass(pe, ps_proj[:, j % 2, side], wi_hi[:, j, c, side], wi_lo[:, j, c, side],
                                            x_hi[:, c], x_lo[:, c], c == 0, c == DC - 1)
                    mm.then_inc(proj_done, 1)
                pe.wait_ge(w_lo_done, W_UNITS)
                pe.wait_ge(out_free, TILES * g)
                for j in range(JC):
                    pe.wait_ge(h_lo_done, JC * g + j + 1)
                    for t in range(TILES):
                        mm = three_pass(pe, ps_out[:, t], h_hi[:, j, t * P:(t + 1) * P], h_lo[:, j, t * P:(t + 1) * P],
                                        wo_hi[:, j], wo_lo[:, j], j == 0, j == JC - 1)
                        if j == JC - 1:
                            mm.then_inc(out_done, 1)


HEADS = 16
HD = D // HEADS
HC = P // HD
L = 128
SCALE = 1.0 / float(HD) ** 0.5
MASKED = -1e30


class CrossWeights:

    def __init__(self, arena, w_q, w_kv, w_o):
        n = DC * D
        at = [arena[:, k:k + size] for k, size in ((0, n), (n, n), (2 * n, n), (3 * n, n), (4 * n, n // 2), (9 * n // 2, n // 2))]
        self.q_hi, self.q_lo, self.o_hi, self.o_lo, self.kv_hi, self.kv_lo = (
            w.rearrange("p (c n) -> p c n", n=D) for w in at)
        h = n // 2
        self.units = [(w_q[0], at[0][:, 0:h], at[1][:, 0:h]), (w_q[1], at[0][:, h:n], at[1][:, h:n]),
                      (w_kv, at[4], at[5]),
                      (w_o[0], at[2][:, 0:h], at[3][:, 0:h]), (w_o[1], at[2][:, h:n], at[3][:, h:n])]


def cross_attention(nc, x1_dram, ctx_t, weights, x2_dram, ident, res, ln):
    with ExitStack() as ctx:
        def sb(name, shape, dt=F32):
            return ctx.enter_context(nc.sbuf_tensor("b_" + name, shape, dt))

        def sem(name):
            return ctx.enter_context(nc.semaphore("b_" + name))

        GH = GB * HEADS
        wq_hi, wq_lo, wkv_hi, wkv_lo = weights.q_hi, weights.q_lo, weights.kv_hi, weights.kv_lo
        wo_hi, wo_lo = weights.o_hi, weights.o_lo
        mask = sb("mask", [P, 3 * P])
        xt = sb("xt", [P, TILES, D])
        x_hi = sb("x_hi", [P, DC, GT], F32R)
        x_lo = sb("x_lo", [P, DC, GT], F32R)
        c_raw = sb("c_raw", [P, GT])
        c_hi = sb("c_hi", [P, GT], F32R)
        c_lo = sb("c_lo", [P, GT], F32R)
        q = sb("q", [P, DC, GT])
        k = sb("k", [P, DC, HC, GT])
        v = sb("v", [P, TILES, DC, HC, P])
        carrier = sb("carrier", [P, GH])
        pr = sb("pr", [P, 4, 3 * P])
        bmax = sb("bmax", [P, 4, 2])
        rsum = sb("rsum", [P, 4, 2])
        rinv = sb("rinv", [P, 4, 2])
        pt = sb("pt", [P, 2, 3 * P])
        a_hi = sb("a_hi", [P, DC, GT], F32R)
        a_lo = sb("a_lo", [P, DC, GT], F32R)
        ps_pj = ctx.enter_context(nc.psum_tensor("b_ps_pj", [P, 2, 512], F32))
        ps_s = ctx.enter_context(nc.psum_tensor("b_ps_s", [P, 2, 512], F32))
        ps_t = ctx.enter_context(nc.psum_tensor("b_ps_t", [P, 2, 512], F32))
        ps_o = ctx.enter_context(nc.psum_tensor("b_ps_o", [P, 2, 512], F32))

        consts = sem("consts")
        zeros = sem("zeros")
        xt_loaded = sem("xt_loaded")
        c_loaded = sem("c_loaded")
        res_loaded = sem("res_loaded")
        c_hi_done = sem("c_hi_done")
        c_lo_done = sem("c_lo_done")
        pj_ready = sem("pj_ready")
        x_hi_done = sem("x_hi_done")
        k_done = sem("k_done")
        pj_free = sem("pj_free")
        s_ready = sem("s_ready")
        max_done = sem("max_done")
        exp_done = sem("exp_done")
        rinv_done = sem("rinv_done")
        norm_done = sem("norm_done")
        pt_ready = sem("pt_ready")
        pt_free = sem("pt_free")
        pv_done = sem("pv_done")
        o_hi_done = sem("o_hi_done")
        o_free = sem("o_free")
        ln_step = sem("ln_step")
        var_done = sem("var_done")
        rstd_done = sem("rstd_done")
        x2_ready = sem("x2_ready")
        x2_stored = sem("x2_stored")

        CONSTS = 7
        BANKS = 2
        USES = 4 * DC + TILES
        FREES = USES - DC
        GC = GB * DC
        AHEAD = 3
        STEPS = GH + AHEAD + 3

        def seq(n):
            return n // HEADS, n % HEADS // HC, n % HC

        block = ctx.enter_context(nc.Block())

        @block.sync
        def _(sp):
            sp.dma_start(xt[:], x1_dram[0]).then_inc(xt_loaded, 16)
            sp.dma_start(c_raw[:], ctx_t[0]).then_inc(c_loaded, 16)
            with sp.Fori(0, GROUPS - 1) as g:
                sp.wait_ge(x2_stored, 16 * g)
                sp.dma_start(res[:], x1_dram[bass.ds(g, 1)].rearrange("o p t d -> p (o t) d")).then_inc(res_loaded, 16)
                sp.wait_ge(pj_ready, USES * g + DC)
                sp.dma_start(xt[:], x1_dram[bass.ds(g + 1, 1)].rearrange("o p t d -> p (o t) d")).then_inc(xt_loaded, 16)
                sp.wait_ge(c_lo_done, g + 1)
                sp.dma_start(c_raw[:], ctx_t[bass.ds(g + 1, 1)].rearrange("o p t -> p (o t)")).then_inc(c_loaded, 16)
            sp.wait_ge(x2_stored, 16 * (GROUPS - 1))
            sp.dma_start(res[:], x1_dram[GROUPS - 1]).then_inc(res_loaded, 16)

        @block.gpsimd
        def _(pool):
            pool.memset(ident[:], 0.0).then_inc(consts, 1)
            pool.memset(mask[:], 0.0).then_inc(consts, 1)
            pool.memset(ln.power[:], -0.5).then_inc(consts, 1)
            pool.wait_ge(consts, 3)
            pool.affine_select(out=ident[:], in_=ident[:], compare_op=ALU.not_equal, fill=1.0, base=0,
                               pattern=[[-1, P]], channel_multiplier=1).then_inc(consts, 1)
            for c in (0, 2):
                pool.affine_select(out=mask[:, c * P:(c + 1) * P], in_=mask[:, c * P:(c + 1) * P], compare_op=ALU.is_ge,
                                   fill=MASKED, base=0, pattern=[[-1, P]], channel_multiplier=1).then_inc(consts, 1)
            pool.memset(k[:], 0.0).then_inc(consts, 1)

            def top(g):
                pool.wait_ge(c_hi_done, g + 1)
                pool.tensor_tensor(c_lo[:], c_raw[:], c_hi[:].bitcast(F32), ALU.subtract).then_inc(c_lo_done, 1)

            def attend(g):
                for n in range(GH):
                    pool.wait_ge(rinv_done, GH * g + n + 1)
                    for a, b, r in ((0, P, 0), (P, 3 * P, 1)):
                        ins = pool.tensor_tensor(pr[:, n % 4, a:b], pr[:, n % 4, a:b],
                                                 rinv[:, n % 4, r:r + 1].broadcast_to([P, b - a]), ALU.mult)
                    ins.then_inc(norm_done, 1)

            def normalize(g):
                pool.wait_ge(var_done, g + 1)
                pool.tensor_tensor(ln.rstd[:], ln.var[:], ln.power[:], ALU.pow).then_inc(rstd_done, 1)
                pool.wait_ge(x2_ready, TILES * g + TILES)
                pool.dma_start(x2_dram[bass.ds(g, 1)].rearrange("o p t d -> p (o t) d"), res[:]).then_inc(x2_stored, 16)

            top(0)
            attend(0)
            with pool.Fori(1, GROUPS) as g:
                top(g)
                normalize(g - 1)
                attend(g)
            pool.wait_ge(x2_stored, 16 * (GROUPS - 1))

        @block.scalar
        def _(act):
            act.preload_act_table_set("exp_and_others")
            with act.Fori(0, GROUPS) as g:
                act.wait_ge(c_loaded, 16 * g + 16)
                act.activation(c_hi[:], c_raw[:], ACT.Copy).then_inc(c_hi_done, 1)
                for c in range(DC):
                    act.wait_ge(pj_ready, USES * g + c + 1)
                    act.activation(x_hi[:, c], ps_pj[:, c % 2], ACT.Copy).then_inc(x_hi_done, 1)
                act.wait_ge(consts, CONSTS)
                for c in range(DC):
                    act.wait_ge(pj_ready, USES * g + 2 * DC + c + 1)
                    for h in range(HC):
                        rows = slice(h * HD, (h + 1) * HD)
                        ins = act.activation(k[rows, c, h], ps_pj[rows, c % 2], ACT.Copy)
                    ins.then_inc(k_done, 1)
                for n in range(STEPS):
                    if n < GH:
                        act.wait_ge(max_done, BANKS + GH * g + n + 1)
                        for a, b, r in ((0, P, 0), (P, 3 * P, 1)):
                            ins = act.activation(pr[:, n % 4, a:b], pr[:, n % 4, a:b], ACT.Exp, scale=-1.0,
                                                 bias=bmax[:, n % 4, r:r + 1], accum_out=rsum[:, n % 4, r:r + 1])
                        ins.then_inc(exp_done, 1)
                    m = n - AHEAD - 2
                    if 0 <= m < GH and m % HC == HC - 1:
                        b, c, _ = seq(m)
                        act.wait_ge(pv_done, BANKS + GH * g + m + 1)
                        act.activation(a_hi[:, c, b * S:(b + 1) * S], ps_o[:, m // HC % 2, 0:S], ACT.Copy)\
                            .then_inc(o_hi_done, 1)

        @block.vector
        def _(dve):
            dve.sem_inc(pj_free, BANKS)
            dve.sem_inc(max_done, BANKS)
            dve.sem_inc(pt_free, BANKS)
            dve.sem_inc(o_free, BANKS)
            dve.memset(v[:], 0.0).then_inc(zeros, 1)

            def top(g):
                for i in range(4 * DC):
                    if i // DC == 2:
                        continue
                    src, c = ps_pj[:, i % 2], i % DC
                    if i < DC:
                        dve.wait_ge(x_hi_done, DC * g + i + 1)
                        dve.tensor_tensor(x_lo[:, c], src, x_hi[:, c].bitcast(F32), ALU.subtract).then_inc(pj_free, 1)
                        continue
                    dve.wait_ge(pj_ready, USES * g + i + 1)
                    if i < 2 * DC:
                        dve.tensor_copy(q[:, c], src).then_inc(pj_free, 1)
                        continue
                    vs = src.rearrange("p (c h d) -> p c h d", c=DC, h=HC)
                    for h in range(HC):
                        ins = dve.tensor_copy(v[:, c, :, h, h * HD:(h + 1) * HD], vs[:, :, h])
                    ins.then_inc(pj_free, 1)

            def normalize(g):
                moments(dve, res, ln, ln_step, (TILES + 6) * g, var_done)
                dve.wait_ge(rstd_done, g + 1)
                for t in range(TILES):
                    dve.tensor_scalar(res[:, t], res[:, t], ln.mean[:, t:t + 1], ln.rstd[:, t:t + 1],
                                      ALU.subtract, ALU.mult).then_inc(x2_ready, 1)

            def attend(g):
                for n in range(STEPS):
                    if n < GH:
                        dve.wait_ge(s_ready, GH * g + n + 1)
                        dve.memset(carrier[:, n:n + 1], 0.0)
                        for a, b, r in ((0, P, 0), (P, 3 * P, 1)):
                            ins = dve.tensor_tensor_reduce(pr[:, n % 4, a:b], ps_s[:, n % 2, a:b], mask[:, a:b], -SCALE, 3e38,
                                                           ALU.add, ALU.min, bmax[:, n % 4, r:r + 1])
                        ins.then_inc(max_done, 1)
                    m = n - 1
                    if 0 <= m < GH:
                        dve.wait_ge(exp_done, GH * g + m + 1)
                        dve.reciprocal(rinv[:, m % 4], rsum[:, m % 4]).then_inc(rinv_done, 1)
                    m = n - AHEAD
                    if 0 <= m < GH:
                        dve.wait_ge(pv_done, GH * g + m + 1)
                        dve.wait_ge(pt_ready, GH * g + m + 1)
                        dve.tensor_copy(pt[:, m % 2], ps_t[:, m % 2, 0:3 * P]).then_inc(pt_free, 1)
                    m = n - AHEAD - 2
                    if 0 <= m < GH and m % HC == HC - 1:
                        b, c, _ = seq(m)
                        dve.wait_ge(o_hi_done, GC * g + m // HC + 1)
                        dve.tensor_tensor(a_lo[:, c, b * S:(b + 1) * S], ps_o[:, m // HC % 2, 0:S],
                                          a_hi[:, c, b * S:(b + 1) * S].bitcast(F32), ALU.subtract).then_inc(o_free, 1)
                dve.wait_ge(res_loaded, 16 * g + 16)
                for t in range(TILES):
                    i = 4 * DC + t
                    dve.wait_ge(pj_ready, USES * g + i + 1)
                    dve.tensor_tensor(res[:, t], ps_pj[:, i % 2], res[:, t], ALU.add).then_inc(pj_free, 1)
                dve.wait_ge(pj_free, BANKS + FREES * g + FREES)

            dve.wait_ge(zeros, 1)
            dve.wait_ge(consts, CONSTS)
            top(0)
            attend(0)
            with dve.Fori(1, GROUPS) as g:
                top(g)
                normalize(g - 1)
                attend(g)

        @block.tensor
        def _(pe):
            pe.wait_ge(consts, CONSTS - 3)
            pe.sem_inc(pv_done, BANKS)

            def wait_read(g, i):
                if i // DC == 2:
                    pe.wait_ge(k_done, DC * g + i - 2 * DC + 1)
                else:
                    pe.wait_ge(pj_free, BANKS + FREES * g + (i if i < 2 * DC else i - DC) + 1)

            with pe.Fori(0, GROUPS) as g:
                pe.wait_ge(xt_loaded, 16 * g + 16)
                for i in range(4 * DC):
                    c = i % DC
                    out = ps_pj[:, i % 2]
                    wait_read(g, i - BANKS)
                    if i < DC:
                        for t in range(TILES):
                            mm = pe.transpose(out[:, t * P:(t + 1) * P], xt[:, t, c * P:(c + 1) * P], ident[:])
                    elif i < 2 * DC:
                        if c == 0:
                            wait_read(g, DC - 1)
                        for j in range(DC):
                            mm = three_pass(pe, out, wq_hi[:, j, c * P:(c + 1) * P], wq_lo[:, j, c * P:(c + 1) * P],
                                            x_hi[:, j], x_lo[:, j], j == 0, j == DC - 1)
                    elif i < 3 * DC:
                        pe.wait_ge(c_lo_done, g + 1)
                        mm = three_pass(pe, out, wkv_hi[:, 0, c * P:(c + 1) * P], wkv_lo[:, 0, c * P:(c + 1) * P],
                                        c_hi[:], c_lo[:], True, True)
                    else:
                        mm = three_pass(pe, out, c_hi[:, c * P:(c + 1) * P], c_lo[:, c * P:(c + 1) * P],
                                        wkv_hi[:, 1], wkv_lo[:, 1], True, True)
                    mm.then_inc(pj_ready, 1)
                wait_read(g, 3 * DC - 1)
                wait_read(g, 4 * DC - 1)
                for n in range(STEPS):
                    if n < GH:
                        b, c, h = seq(n)
                        pe.wait_ge(max_done, GH * g + n + 1)
                        for u in range(2):
                            qs = slice(b * S + u * P, b * S + (u + 1) * P)
                            ks = slice(b * S, b * S + (u + 1) * P)
                            mm = pe.matmul(ps_s[:, n % 2, u * P:(1 + 2 * u) * P], q[:, c, qs], k[:, c, h, ks],
                                           start=True, stop=True)
                        mm.then_inc(s_ready, 1)
                    m = n - AHEAD
                    if 0 <= m < GH:
                        pe.wait_ge(norm_done, GH * g + m + 1)
                        pe.wait_ge(pt_free, GH * g + m + 1)
                        for u in range(3):
                            mm = pe.transpose(ps_t[:, m % 2, u * P:(u + 1) * P], pr[:, m % 4, u * P:(u + 1) * P], ident[:])
                        mm.then_inc(pt_ready, 1)
                    m = n - AHEAD - 1
                    if 0 <= m < GH:
                        b, c, h = seq(m)
                        pe.wait_ge(pt_free, BANKS + GH * g + m + 1)
                        if h == 0:
                            pe.wait_ge(o_free, GC * g + m // HC + 1)
                        o = ps_o[:, m // HC % 2]
                        for u, out, keys in ((0, o[:, 0:S], slice(0, S)), (1, o[:, P:S], slice(S, 3 * P))):
                            mm = pe.matmul(out, v[:, b * GB + u, c, h], pt[:, m % 2, keys],
                                           start=h == 0 and u == 0, stop=h == HC - 1 and u == 1)
                        mm.then_inc(pv_done, 1)
                pe.wait_ge(o_free, BANKS + GC * g + GC)
                for t in range(TILES):
                    i = 4 * DC + t
                    wait_read(g, i - BANKS)
                    for c in range(DC):
                        mm = three_pass(pe, ps_pj[:, i % 2], a_hi[:, c, t * P:(t + 1) * P], a_lo[:, c, t * P:(t + 1) * P],
                                        wo_hi[:, c], wo_lo[:, c], c == 0, c == DC - 1)
                    mm.then_inc(pj_ready, 1)


E_N = 8
DE = 352
DS = 704
E_UNITS = (P, P, DE - 2 * P)
S_UNITS = (P, P, P, P, (DS - 4 * P) // 2, (DS - 4 * P) // 2)
SLOTS = 512
E_TILES = (2 * T + E_N * (SLOTS - 1)) // SLOTS
BLOCKS = SLOTS // P
NB = E_TILES * BLOCKS
NT = T // P
F16 = mybir.dt.float16


class Routing:

    def __init__(self, sb):
        self.token_of = sb("token_of", [P, NB], I32)
        self.slot = sb("slot", [P, 2, NT], I32)
        self.weight = sb("weight", [P, 2, NT])
        self.expert_of = sb("expert_of", [P, E_TILES], I32)


S_PARTS = DC + 3


class Shared:

    def __init__(self, sb):
        U = len(S_UNITS)
        self.gu_hi = sb("s_gu_hi", [P, DC, 2 * DS], F32R)
        self.gu_lo = sb("s_gu_lo", [P, DC, 2 * DS], F32R)
        self.dn_hi = sb("s_dn_hi", [P, U, D], F32R)
        self.dn_lo = sb("s_dn_lo", [P, U, D], F32R)

    def parts(self, w_gate_up, w_down):
        out = [(self.gu_hi[:, c], self.gu_lo[:, c], P, 2 * DS, w_gate_up[:, c]) for c in range(DC)]
        full = 4 * P
        for u, n, rows in ((0, P, w_down[0:2 * P]), (2, P, w_down[2 * P:full]), (4, S_UNITS[4], w_down[full:DS])):
            hi, lo = (w[0:n, u:u + 2].rearrange("p u n -> p (u n)") for w in (self.dn_hi, self.dn_lo))
            out.append((hi, lo, n, 2 * D, rows.rearrange("(u p) n -> p u n", u=2)))
        return out

    def block(self, sb, sem, psum):
        U = len(S_UNITS)
        self.x_hi = sb("s_x_hi", [P, DC, GT], F32R)
        self.x_lo = sb("s_x_lo", [P, DC, GT], F32R)
        self.sg = sb("s_sg", [P, 2, GT])
        self.hf = sb("s_hf", [P, 2, GT])
        self.h_hi = sb("s_h_hi", [P, U, GT], F32R)
        self.h_lo = sb("s_h_lo", [P, U, GT], F32R)
        self.ps_x = psum("s_ps_x", [P, 2, GT], F32)
        self.ps_h = psum("s_ps_h", [P, 2, 2, GT], F32)
        self.ps_out = psum("s_ps_out", [P, 2, D], F32)
        self.x_ready = sem("s_x_ready")
        self.x_hi_done = sem("s_x_hi_done")
        self.x_lo_done = sem("s_x_lo_done")
        self.h_ready = sem("s_h_ready")
        self.silu_done = sem("s_silu_done")
        self.h_done = sem("s_h_done")
        self.h_hi_done = sem("s_h_hi_done")
        self.h_lo_done = sem("s_h_lo_done")
        self.out_done = sem("s_out_done")
        self.out_free = sem("s_out_free")

    BANKS = 2
    U = len(S_UNITS)

    def begin(self, dve):
        dve.sem_inc(self.x_lo_done, self.BANKS)
        dve.sem_inc(self.out_free, self.BANKS)

    def turn(self, pe, xt, ident, n, c):
        pe.wait_ge(self.x_lo_done, DC * n + c + 1)
        for t in range(TILES):
            mm = pe.transpose(self.ps_x[:, c % 2, t * P:(t + 1) * P], xt[:, t, c * P:(c + 1) * P], ident[:])
        mm.then_inc(self.x_ready, 1)

    def x_round(self, act, n, c):
        act.wait_ge(self.x_ready, DC * n + c + 1)
        act.activation(self.x_hi[:, c], self.ps_x[:, c % 2], ACT.Copy).then_inc(self.x_hi_done, 1)

    def x_rest(self, dve, n, c):
        dve.wait_ge(self.x_hi_done, DC * n + c + 1)
        dve.tensor_tensor(self.x_lo[:, c], self.ps_x[:, c % 2], self.x_hi[:, c].bitcast(F32), ALU.subtract)\
            .then_inc(self.x_lo_done, 1)

    def hidden(self, pe, n, u):
        pe.wait_ge(self.h_done, self.U * n + max(0, u - 1))
        row, size = sum(S_UNITS[:u]), S_UNITS[u]
        for s in range(2):
            at = slice(s * DS + row, s * DS + row + size)
            for c in range(DC):
                mm = three_pass(pe, self.ps_h[0:size, u % 2, s], self.gu_hi[:, c, at], self.gu_lo[:, c, at],
                                self.x_hi[:, c], self.x_lo[:, c], c == 0, c == DC - 1)
        mm.then_inc(self.h_ready, 1)

    def gate(self, act, n, u):
        size = S_UNITS[u]
        act.wait_ge(self.h_ready, self.U * n + u + 1)
        act.activation(self.sg[0:size, u % 2], self.ps_h[0:size, u % 2, 0], ACT.Silu).then_inc(self.silu_done, 1)
        act.wait_ge(self.h_done, self.U * n + u + 1)
        if u == 0:
            act.wait_ge(self.out_done, TILES * n)
        act.activation(self.h_hi[0:size, u], self.hf[0:size, u % 2], ACT.Copy).then_inc(self.h_hi_done, 1)

    def up(self, dve, n, u):
        size = S_UNITS[u]
        dve.wait_ge(self.silu_done, self.U * n + u + 1)
        dve.wait_ge(self.h_lo_done, self.U * n + max(0, u - 1))
        dve.tensor_tensor(self.hf[0:size, u % 2], self.ps_h[0:size, u % 2, 1], self.sg[0:size, u % 2], ALU.mult)\
            .then_inc(self.h_done, 1)
        dve.wait_ge(self.h_hi_done, self.U * n + u + 1)
        dve.tensor_tensor(self.h_lo[0:size, u], self.hf[0:size, u % 2], self.h_hi[0:size, u].bitcast(F32), ALU.subtract)\
            .then_inc(self.h_lo_done, 1)

    def down(self, pe, n, t):
        pe.wait_ge(self.out_free, TILES * n + t + 1)
        for u, size in enumerate(S_UNITS):
            pe.wait_ge(self.h_lo_done, self.U * n + u + 1)
            mm = three_pass(pe, self.ps_out[:, t % 2], self.h_hi[0:size, u, t * P:(t + 1) * P],
                            self.h_lo[0:size, u, t * P:(t + 1) * P], self.dn_hi[0:size, u], self.dn_lo[0:size, u],
                            u == 0, u == self.U - 1)
        mm.then_inc(self.out_done, 1)

    def add(self, dve, res, n, t):
        dve.wait_ge(self.out_done, TILES * n + t + 1)
        dve.tensor_tensor(res[:, t], self.ps_out[:, t % 2], res[:, t], ALU.add).then_inc(self.out_free, 1)


def route(nc, x2_dram, w_router, sums, ln, ident, shared, w_gate_up, w_down, we_gate_up, we_down, raw, kept, rt):
    with ExitStack() as ctx:
        def sb(name, shape, dt=F32):
            return ctx.enter_context(nc.sbuf_tensor("r_" + name, shape, dt))

        def sem(name):
            return ctx.enter_context(nc.semaphore("r_" + name))

        xt = sb("xt", [P, 2, TILES, D])
        before = sb("before", [P, P])
        ones = sb("ones", [P, P])
        w_raw = sb("w_raw", [P, DC, E_N])
        w_hi = sb("w_hi", [P, DC, P], F32R)
        w_lo = sb("w_lo", [P, DC, P], F32R)
        lg_t = sb("lg_t", [E_N, T])
        int_a = sb("int_a", [P, P], I32)
        rank8 = sb("rank8", [P, NT, E_N])
        col128 = sb("col128", [P, P])
        col_nb = sb("col_nb", [P, NB])
        token = sb("token", [P, NT])
        tile_no = sb("tile_no", [P, E_TILES, E_N])
        keep = sb("keep", [P, E_N, NT])
        unit = sb("unit", [P, E_N])
        lg = sb("lg", [P, NT, E_N])
        pr = sb("pr", [P, NT, E_N])
        top = sb("top", [P, NT])
        rsum = sb("rsum", [P, NT])
        cand = sb("cand", [P, NT, E_N])
        best = sb("best", [P, NT])
        pick = sb("pick", [P, 2, NT, E_N])
        both = sb("both", [P, NT, E_N])
        tot = sb("tot", [P, E_N, NT])
        run = sb("run", [P, E_N, NT])
        tiles_f = sb("tiles_f", [P, E_N])
        tiles_i = sb("tiles_i", [P, E_N], I32)
        ends = sb("ends", [P, E_N])
        base = sb("base", [P, E_N])
        pos = sb("pos", [P, NT, E_N])
        cmp = sb("cmp", [P, E_TILES, E_N])
        ex_f = sb("ex_f", [P, E_TILES])
        slot_f = sb("slot_f", [P, 2, NT])
        part_i = sb("part_i", [P, 2, 2, NT], I32)
        part_f = sb("part_f", [P, 2, 2, NT])
        hot_lo = sb("hot_lo", [P, 2 * NT, P], F16)
        hot_hi = sb("hot_hi", [P, 2 * NT, NB], F16)
        shared.block(sb, sem, lambda name, shape, dt: ctx.enter_context(nc.psum_tensor("r_" + name, shape, dt)))
        ps_l = shared.ps_h[:, 0, 0]
        ps_r = shared.ps_x[:, 1]
        each_e = NT * E_N
        ps_logits, ps_prior, ps_total = (ps_r[:, k * each_e:(k + 1) * each_e] for k in range(3))
        ps_token = ps_r[:, 3 * each_e:3 * each_e + NB]
        parts = shared.parts(w_gate_up, w_down)
        w_part = raw[0].rearrange("p c n -> p (c n)").rearrange("p (b n) -> p b n", b=2)

        consts = sem("consts")
        iotas = sem("iotas")
        loaded = [sem("loaded_even"), sem("loaded_odd")]
        w_loaded = sem("w_loaded")
        w_hi_done = sem("w_hi_done")
        w_lo_done = sem("w_lo_done")
        part_loaded = [sem("part_loaded_even"), sem("part_loaded_odd")]
        part_hi_done = sem("part_hi_done")
        part_lo_done = sem("part_lo_done")
        ln_step = sem("ln_step")
        var_done = sem("var_done")
        rstd_done = sem("rstd_done")
        x2_ready = sem("x2_ready")
        x2_stored = sem("x2_stored")
        padded = sem("padded")
        expert_known = sem("expert_known")
        expert_loaded = sem("expert_loaded")
        lg_ready = sem("lg_ready")
        lg_read = sem("lg_read")
        turned = sem("turned")
        sub_done = sem("sub_done")
        exp_done = sem("exp_done")
        both_done = sem("both_done")
        counted = sem("counted")
        hot_done = sem("hot_done")
        placed = sem("placed")
        step = sem("step")

        CONSTS = 8
        LAST = GROUPS - 1

        block = ctx.enter_context(nc.Block())

        @block.sync
        def _(sp):
            def load(g):
                sp.dma_start(xt[:, g % 2], x2_dram[g]).then_inc(loaded[g % 2], 16)

            def load_part(k):
                if k >= 2:
                    sp.wait_ge(part_lo_done, k - 1)
                _, _, n, cols, src = parts[k]
                dst = w_part[0:n, k % 2, 0:cols]
                if k >= DC:
                    dst = dst.rearrange("p (u n) -> p u n", u=2)
                sp.dma_start(dst, src).then_inc(part_loaded[k % 2], 16)

            sp.dma_start(w_raw[:], w_router).then_inc(w_loaded, 16)
            load(0)
            load(1)
            load_part(0)
            load_part(1)
            sp.wait_ge(x2_ready, TILES)
            sp.dma_start(x2_dram[LAST], kept[:]).then_inc(x2_stored, 16)
            for g in range(2, GROUPS):
                sp.wait_ge(shared.x_ready, DC * (g - 1))
                if g == LAST:
                    sp.wait_ge(x2_stored, 16)
                load(g)
                load_part(2 * g - 2)
                load_part(2 * g - 1)
            load_part(S_PARTS - 1)
            sp.wait_ge(part_lo_done, S_PARTS)
            sp.wait_ge(padded, 1)
            sp.wait_ge(expert_known, 1)
            e = sp.value_load(rt.expert_of[0:1, 0:1], min_val=0, max_val=E_N - 1)
            load_expert(sp, e, we_gate_up, we_down, raw, expert_loaded, expert_loaded)
            sp.wait_ge(expert_loaded, 48)

        @block.gpsimd
        def _(pool):
            pool.memset(before[:], 1.0).then_inc(consts, 1)
            pool.memset(ones[:], 1.0).then_inc(consts, 1)
            pool.memset(w_hi[:].bitcast(F32), 0.0).then_inc(consts, 1)
            pool.memset(w_lo[:].bitcast(F32), 0.0).then_inc(consts, 1)
            pool.memset(keep[:], 1.0).then_inc(consts, 1)
            pool.memset(unit[:], 1.0).then_inc(consts, 1)
            pool.wait_ge(var_done, 1)
            pool.tensor_tensor(ln.rstd[:], ln.var[:], ln.power[:], ALU.pow).then_inc(rstd_done, 1)
            pool.wait_ge(consts, 6)
            pool.affine_select(out=before[:], in_=before[:], compare_op=ALU.is_gt, fill=0.0, base=0,
                               pattern=[[1, P]], channel_multiplier=-1).then_inc(consts, 1)
            pool.memset(keep[:, :, 0:1], 0.0).then_inc(consts, 1)
            n = 0
            for out, pattern, start, mult in (
                (rank8[:], [[0, NT], [-1, E_N]], E_N, 0),
                (col128[:], [[1, P]], 0, 0),
                (col_nb[:], [[1, NB]], 0, 0),
                (token[:], [[P, NT]], 0, 1),
                (tile_no[:], [[1, E_TILES], [0, E_N]], 0, 0),
            ):
                size = 1
                for _, k in pattern:
                    size *= k
                if n:
                    pool.wait_ge(iotas, n)
                pool.iota(int_a[:, 0:size], pattern=pattern, base=start, channel_multiplier=mult).then_inc(iotas, 1)
                pool.wait_ge(iotas, n + 1)
                flat = out if len(out.shape) == 2 else out.rearrange("p a b -> p (a b)")
                pool.tensor_copy(flat, int_a[:, 0:size]).then_inc(iotas, 1)
                n += 2
            for k, (hi, lo, n, cols, _) in enumerate(parts):
                pool.wait_ge(part_hi_done, k + 1)
                pool.tensor_tensor(lo, w_part[0:n, k % 2, 0:cols], hi.bitcast(F32), ALU.subtract).then_inc(part_lo_done, 1)

        @block.scalar
        def _(act):
            act.preload_act_table_set("exp_and_others")
            act.wait_ge(w_loaded, 16)
            act.wait_ge(consts, CONSTS)
            act.activation(w_hi[:, :, 0:E_N], w_raw[:], ACT.Copy).then_inc(w_hi_done, 1)
            for g in range(GROUPS):
                if g:
                    act.wait_ge(lg_ready, g)
                for c in range(DC):
                    shared.x_round(act, g, c)
                for k in range(2 * g, min(2 * g + 2, S_PARTS)):
                    hi, _, n, cols, _ = parts[k]
                    act.wait_ge(part_loaded[k % 2], 16 * (k // 2) + 16)
                    act.activation(hi, w_part[0:n, k % 2, 0:cols], ACT.Copy).then_inc(part_hi_done, 1)
                act.wait_ge(lg_ready, g + 1)
                act.activation(lg_t[:, g * GT:(g + 1) * GT], ps_l[0:E_N], ACT.Copy).then_inc(lg_read, 1)
            act.wait_ge(sub_done, 1)
            act.activation(pr[:], lg[:], ACT.Exp).then_inc(exp_done, 1)
            for u in range(Shared.U):
                shared.gate(act, 0, u)

        @block.vector
        def _(dve):
            steps = [0]

            def link(ins):
                steps[0] += 1
                ins.then_inc(step, 1)
                dve.wait_ge(step, steps[0])

            dve.memset(raw[1][E_UNITS[2]:P, 2], 0.0).then_inc(padded, 1)
            moments(dve, sums, ln, ln_step, 0, var_done)
            dve.wait_ge(rstd_done, 1)
            for t in range(TILES):
                dve.tensor_scalar(kept[:, t], sums[:, t], ln.mean[:, t:t + 1], ln.rstd[:, t:t + 1],
                                  ALU.subtract, ALU.mult).then_inc(x2_ready, 1)
            shared.begin(dve)
            dve.wait_ge(w_hi_done, 1)
            dve.tensor_tensor(w_lo[:, :, 0:E_N], w_raw[:], w_hi[:, :, 0:E_N].bitcast(F32), ALU.subtract)\
                .then_inc(w_lo_done, 1)
            with dve.Fori(0, GROUPS) as g:
                for c in range(DC):
                    shared.x_rest(dve, g, c)

            def each(row):
                return row.rearrange("p (t o) -> p t o", o=1).broadcast_to([P, NT, E_N])

            dve.wait_ge(iotas, 10)
            dve.wait_ge(turned, 1)
            logits = ps_logits.rearrange("p (t e) -> p t e", e=E_N)
            link(dve.tensor_reduce(top[:], logits, AX_X, ALU.max))
            dve.tensor_tensor(lg[:], logits, each(top[:]), ALU.subtract).then_inc(sub_done, 1)
            dve.wait_ge(exp_done, 1)
            link(dve.tensor_reduce(rsum[:], pr[:], AX_X, ALU.add))
            link(dve.reciprocal(rsum[:], rsum[:]))
            link(dve.tensor_tensor(pr[:], pr[:], each(rsum[:]), ALU.mult))
            shared.up(dve, 0, 0)
            for k in range(2):
                w = rt.weight[:, k]
                link(dve.tensor_reduce(w, pr[:], AX_X, ALU.max))
                link(dve.tensor_tensor(cand[:], pr[:], each(w), ALU.is_equal))
                link(dve.tensor_tensor(cand[:], cand[:], rank8[:], ALU.mult))
                link(dve.tensor_reduce(best[:], cand[:], AX_X, ALU.max))
                link(dve.tensor_tensor(pick[:, k], cand[:], each(best[:]), ALU.is_equal))
                if k == 0:
                    link(dve.scalar_tensor_tensor(pr[:], pick[:, 0], -4.0, pr[:], ALU.mult, ALU.add))
                    shared.up(dve, 0, 1)
            dve.tensor_tensor(both[:], pick[:, 0], pick[:, 1], ALU.add).then_inc(both_done, 1)
            shared.up(dve, 0, 2)
            dve.wait_ge(counted, 1)
            prior = ps_prior.rearrange("p (t e) -> p t e", e=E_N)
            total = ps_total.rearrange("p (t e) -> p e t", e=E_N)
            link(dve.tensor_copy(tot[:], total))
            link(dve.tensor_tensor_scan(run[:].rearrange("p e t -> p (e t)"), keep[:].rearrange("p e t -> p (e t)"),
                                        tot[:].rearrange("p e t -> p (e t)"), 0.0, ALU.mult, ALU.add))
            link(dve.tensor_scalar(tiles_i[:], run[:, :, NT - 1], float(SLOTS - 1), None, ALU.add))
            link(dve.tensor_scalar(tiles_i[:], tiles_i[:], SLOTS.bit_length() - 1, None, ALU.logical_shift_right))
            link(dve.tensor_copy(tiles_f[:], tiles_i[:]))
            link(dve.tensor_tensor_scan(ends[:], unit[:], tiles_f[:], 0.0, ALU.mult, ALU.add))
            shared.up(dve, 0, 3)
            link(dve.tensor_tensor(base[:], ends[:], tiles_f[:], ALU.subtract))
            link(dve.tensor_scalar(base[:], base[:], float(SLOTS), None, ALU.mult))
            link(dve.tensor_tensor(cmp[:], tile_no[:],
                                   ends[:].rearrange("p (o e) -> p o e", o=1).broadcast_to([P, E_TILES, E_N]), ALU.is_ge))
            link(dve.tensor_reduce(ex_f[:], cmp[:], AX_X, ALU.add))
            dve.tensor_scalar(rt.expert_of[:], ex_f[:], float(E_N - 1), None, ALU.min).then_inc(expert_known, 1)
            link(dve.tensor_tensor(tot[:], run[:], tot[:], ALU.subtract))
            link(dve.tensor_tensor(tot[:], tot[:], base[:].rearrange("p (e o) -> p e o", o=1).broadcast_to([P, E_N, NT]),
                                   ALU.add))
            link(dve.tensor_tensor(pos[:], prior, tot[:].rearrange("p e t -> p t e"), ALU.add))
            for k in range(2):
                link(dve.tensor_tensor(cand[:], pos[:], pick[:, k], ALU.mult))
                link(dve.tensor_reduce(slot_f[:, k], cand[:], AX_X, ALU.add))
            shared.up(dve, 0, 4)
            link(dve.tensor_copy(rt.slot[:], slot_f[:]))
            link(dve.tensor_scalar(part_i[:, 0], rt.slot[:], P.bit_length() - 1, None, ALU.logical_shift_right))
            link(dve.tensor_scalar(part_i[:, 1], rt.slot[:], P - 1, None, ALU.bitwise_and))
            link(dve.tensor_copy(part_f[:], part_i[:]))
            def spread(x, n):
                return x.rearrange("p k t -> p (k t)").rearrange("p (a o) -> p a o", o=1).broadcast_to([P, 2 * NT, n])

            def repeat(x, n):
                return x.rearrange("p (o n) -> p o n", o=1).broadcast_to([P, 2 * NT, n])

            link(dve.tensor_tensor(hot_lo[:], repeat(col128[:], P), spread(part_f[:, 1], P), ALU.is_equal))
            shared.up(dve, 0, 5)
            link(dve.tensor_tensor(hot_hi[:], repeat(col_nb[:], NB), spread(part_f[:, 0], NB), ALU.is_equal))
            for k in range(2):
                rows = hot_hi[:, k * NT:(k + 1) * NT]
                ins = dve.tensor_tensor(rows, rows, token[:].rearrange("p (t o) -> p t o", o=1).broadcast_to([P, NT, NB]),
                                        ALU.mult).then_inc(hot_done, 1)
            dve.wait_ge(x2_stored, 16)
            for t in range(TILES - 1):
                shared.add(dve, kept, 0, t)
            dve.wait_ge(placed, 1)
            link(dve.tensor_copy(rt.token_of[:], ps_token))
            shared.add(dve, kept, 0, TILES - 1)

        @block.tensor
        def _(pe):
            pe.wait_ge(consts, CONSTS)
            pe.wait_ge(w_lo_done, 1)
            with pe.Fori(0, GROUPS // 2) as h:
                for b in range(2):
                    g = 2 * h + b
                    pe.wait_ge(loaded[b], 16 * h + 16)
                    for c in range(DC):
                        shared.turn(pe, xt[:, b], ident, g, c)
                    pe.wait_ge(shared.x_lo_done, Shared.BANKS + DC * g + DC)
                    pe.wait_ge(lg_read, g)
                    for c in range(DC):
                        mm = three_pass(pe, ps_l, w_hi[:, c], w_lo[:, c], shared.x_hi[:, c], shared.x_lo[:, c],
                                        c == 0, c == DC - 1)
                    mm.then_inc(lg_ready, 1)
            pe.wait_ge(lg_read, GROUPS)
            for t in range(NT):
                mm = pe.transpose(ps_logits[:, t * E_N:(t + 1) * E_N], lg_t[:, t * P:(t + 1) * P], ident[0:E_N, 0:E_N])
            mm.then_inc(turned, 1)
            pe.wait_ge(part_lo_done, S_PARTS)
            for u in range(Shared.U):
                shared.hidden(pe, 0, u)
                if u == 3:
                    pe.wait_ge(both_done, 1)
                    rows = both[:].rearrange("p t e -> p (t e)")
                    pe.matmul(ps_prior, before[:], rows, start=True, stop=True)
                    pe.matmul(ps_total, ones[:], rows, start=True, stop=True).then_inc(counted, 1)
            for t in range(TILES):
                if t == TILES - 1:
                    pe.wait_ge(hot_done, 2)
                    for n in range(2 * NT):
                        mm = pe.matmul(ps_token, hot_lo[:, n], hot_hi[:, n], start=n == 0, stop=n == 2 * NT - 1)
                    mm.then_inc(placed, 1)
                shared.down(pe, 0, t)


def load_expert(sp, e, w_gate_up, w_down, raw, gu_loaded, dn_loaded):
    sp.dma_start(raw[0], w_gate_up[bass.ds(e, 1)].rearrange("o p c n -> p (o c) n")).then_inc(gu_loaded, 16)
    load_down(sp, e, w_down, raw, dn_loaded)


def load_down(sp, e, w_down, raw, dn_loaded):
    rows = w_down[bass.ds(e, 1)].rearrange("o h n -> (o h) n")
    sp.dma_start(raw[1][:, 0:2], rows[0:2 * P].rearrange("(u p) n -> p u n", p=P)).then_inc(dn_loaded, 16)
    sp.dma_start(raw[1][0:E_UNITS[2], 2], rows[2 * P:DE]).then_inc(dn_loaded, 16)


def experts(nc, x2_rows, w_gate_up, w_down, y_dram, ident, raw, rt):
    with ExitStack() as ctx:
        def sb(name, shape, dt=F32):
            return ctx.enter_context(nc.sbuf_tensor("e_" + name, shape, dt))

        def sem(name):
            return ctx.enter_context(nc.semaphore("e_" + name))

        U = len(E_UNITS)
        gu_raw, dn_raw = raw
        gu_hi = sb("gu_hi", [P, DC, 2 * DE], F32R)
        gu_lo = sb("gu_lo", [P, DC, 2 * DE], F32R)
        dn_hi = sb("dn_hi", [P, U, D], F32R)
        dn_lo = sb("dn_lo", [P, U, D], F32R)
        xg = sb("xg", [P, BLOCKS, D])
        index = sb("index", [P, BLOCKS], I32)
        carrier = sb("carrier", [P, 1])
        x_hi = sb("x_hi", [P, DC, SLOTS], F32R)
        x_lo = sb("x_lo", [P, DC, SLOTS], F32R)
        sg = sb("sg", [P, 2, SLOTS])
        hf = sb("hf", [P, 2, SLOTS])
        h_hi = sb("h_hi", [P, U, SLOTS], F32R)
        h_lo = sb("h_lo", [P, U, SLOTS], F32R)
        y = sb("y", [P, BLOCKS, D])
        ps_h = ctx.enter_context(nc.psum_tensor("e_ps_h", [P, 2, 2, SLOTS], F32))
        ps_x = ctx.enter_context(nc.psum_tensor("e_ps_x", [P, 2, 512], F32))
        ps_y = ctx.enter_context(nc.psum_tensor("e_ps_y", [P, 2, D], F32))

        gu_loaded = sem("gu_loaded")
        dn_loaded = sem("dn_loaded")
        gu_hi_done = sem("gu_hi_done")
        gu_lo_done = sem("gu_lo_done")
        dn_hi_done = sem("dn_hi_done")
        dn_lo_done = sem("dn_lo_done")
        indexed = sem("indexed")
        carried = sem("carried")
        x_gathered = sem("x_gathered")
        x_ready = sem("x_ready")
        x_hi_done = sem("x_hi_done")
        x_lo_done = sem("x_lo_done")
        h_ready = sem("h_ready")
        silu_done = sem("silu_done")
        h_done = sem("h_done")
        h_hi_done = sem("h_hi_done")
        h_lo_done = sem("h_lo_done")
        y_ready = sem("y_ready")
        y_read = sem("y_read")
        y_stored = sem("y_stored")

        BANKS = 2
        LAST = E_TILES - 1
        y_tiles = y_dram.rearrange("(i b p) d -> i p b d", b=BLOCKS, p=P)

        block = ctx.enter_context(nc.Block())

        @block.sync
        def _(sp):
            def load(i):
                e = sp.value_load(rt.expert_of[0:1, bass.ds(i, 1)], min_val=0, max_val=E_N - 1)
                sp.wait_ge(gu_lo_done, DC * i)
                sp.dma_start(gu_raw, w_gate_up[bass.ds(e, 1)].rearrange("o p c n -> p (o c) n")).then_inc(gu_loaded, 16)
                sp.wait_ge(dn_lo_done, i)
                load_down(sp, e, w_down, raw, dn_loaded)

            with sp.Fori(0, LAST) as i:
                load(i + 1)
                sp.wait_ge(y_read, BANKS + BLOCKS * i + BLOCKS)
                sp.dma_start(y_tiles[bass.ds(i, 1)].rearrange("o p b d -> p (o b) d"), y[:]).then_inc(y_stored, 16)
            sp.wait_ge(y_read, BANKS + BLOCKS * E_TILES)
            sp.dma_start(y_tiles[LAST], y[:]).then_inc(y_stored, 16)
            sp.wait_ge(y_stored, 16 * E_TILES)

        @block.gpsimd
        def _(pool):

            pool.memset(carrier[:], 0.0).then_inc(carried, 1)

            def gather(i):
                pool.wait_ge(x_ready, DC * i)
                pool.wait_ge(carried, 1 + i)
                pool.tensor_copy(index[:], rt.token_of[:, bass.ds(BLOCKS * i, BLOCKS)]).then_inc(indexed, 1)
                pool.wait_ge(indexed, i + 1)
                pool.tensor_tensor(carrier[:], carrier[:], carrier[:], ALU.add).then_inc(carried, 1)
                for b in range(BLOCKS):
                    pool.indirect_dma_start(xg[:, b], None, x2_rows,
                                            bass.IndirectOffsetOnAxis(ap=index[:, b:b + 1], axis=0)).then_inc(x_gathered, 16)

            def split_down(i):
                pool.wait_ge(dn_hi_done, i + 1)
                pool.tensor_tensor(dn_lo[:], dn_raw, dn_hi[:].bitcast(F32), ALU.subtract).then_inc(dn_lo_done, 1)

            gather(0)
            with pool.Fori(0, LAST) as i:
                gather(i + 1)
                split_down(i)
            split_down(LAST)

        @block.scalar
        def _(act):
            act.preload_act_table_set("silu_and_others")

            def split_x(i, c):
                act.wait_ge(x_ready, DC * i + c + 1)
                act.activation(x_hi[:, c], ps_x[:, c % 2], ACT.Copy).then_inc(x_hi_done, 1)

            def split_gate_up(i, c):
                if c == 0:
                    act.wait_ge(gu_loaded, 16 * i)
                    act.wait_ge(h_ready, U * i)
                act.activation(gu_hi[:, c], gu_raw[:, c], ACT.Copy).then_inc(gu_hi_done, 1)

            def split_x_and_gate_up(i):
                split_x(i, 0)
                split_x(i, 1)
                split_gate_up(i, 0)
                split_x(i, 2)
                split_gate_up(i, 1)
                split_x(i, 3)
                split_gate_up(i, 2)
                split_gate_up(i, 3)

            def split_down(i):
                act.wait_ge(dn_loaded, 32 * i)
                act.wait_ge(y_ready, BLOCKS * i)
                act.activation(dn_hi[:], dn_raw, ACT.Copy).then_inc(dn_hi_done, 1)

            def hidden(i):
                for u, n in enumerate(E_UNITS):
                    act.wait_ge(h_ready, U * i + u + 1)
                    act.activation(sg[0:n, u % 2], ps_h[0:n, u % 2, 0], ACT.Silu).then_inc(silu_done, 1)
                    if u == 0:
                        split_down(i)
                    act.wait_ge(h_done, U * i + u + 1)
                    act.activation(h_hi[0:n, u], hf[0:n, u % 2], ACT.Copy).then_inc(h_hi_done, 1)

            split_x_and_gate_up(0)
            with act.Fori(0, LAST) as i:
                hidden(i)
                split_x_and_gate_up(i + 1)
            hidden(LAST)

        @block.vector
        def _(dve):
            dve.sem_inc(x_lo_done, BANKS)
            dve.sem_inc(y_read, BANKS)

            def split_x(i, c):
                dve.wait_ge(x_hi_done, DC * i + c + 1)
                dve.tensor_tensor(x_lo[:, c], ps_x[:, c % 2], x_hi[:, c].bitcast(F32), ALU.subtract)\
                    .then_inc(x_lo_done, 1)

            def split_gate_up(i, c):
                dve.wait_ge(gu_hi_done, DC * i + c + 1)
                dve.tensor_tensor(gu_lo[:, c], gu_raw[:, c], gu_hi[:, c].bitcast(F32), ALU.subtract)\
                    .then_inc(gu_lo_done, 1)

            def hidden(i):
                for u, n in enumerate(E_UNITS):
                    dve.wait_ge(silu_done, U * i + u + 1)
                    dve.wait_ge(h_lo_done, U * i + max(0, u - 1))
                    dve.tensor_tensor(hf[0:n, u % 2], ps_h[0:n, u % 2, 1], sg[0:n, u % 2], ALU.mult).then_inc(h_done, 1)
                    dve.wait_ge(h_hi_done, U * i + u + 1)
                    dve.tensor_tensor(h_lo[0:n, u], hf[0:n, u % 2], h_hi[0:n, u].bitcast(F32), ALU.subtract)\
                        .then_inc(h_lo_done, 1)

            def output(i, b):
                dve.wait_ge(y_ready, BLOCKS * i + b + 1)
                if b == 0:
                    dve.wait_ge(y_stored, 16 * i)
                dve.tensor_copy(y[:, b], ps_y[:, b % 2]).then_inc(y_read, 1)

            for c in range(DC):
                split_x(0, c)
            for c in range(DC):
                split_gate_up(0, c)
            with dve.Fori(0, LAST) as i:
                hidden(i)
                split_x(i + 1, 0)
                split_x(i + 1, 1)
                output(i, 0)
                output(i, 1)
                split_gate_up(i + 1, 0)
                split_x(i + 1, 2)
                split_gate_up(i + 1, 1)
                output(i, 2)
                split_x(i + 1, 3)
                split_gate_up(i + 1, 2)
                split_gate_up(i + 1, 3)
                output(i, 3)
            hidden(LAST)
            for b in range(BLOCKS):
                output(LAST, b)

        @block.tensor
        def _(pe):
            def turn(i, c):
                if c == 0:
                    pe.wait_ge(x_gathered, 16 * BLOCKS * i + 16 * BLOCKS)
                pe.wait_ge(x_lo_done, DC * i + c + 1)
                for b in range(BLOCKS):
                    mm = pe.transpose(ps_x[:, c % 2, b * P:(b + 1) * P], xg[:, b, c * P:(c + 1) * P], ident[:])
                mm.then_inc(x_ready, 1)

            def hidden(i, u):
                n = E_UNITS[u]
                pe.wait_ge(h_done, U * i + max(0, u - 1))
                for s in range(2):
                    at = slice(s * DE + u * P, s * DE + u * P + n)
                    for c in range(DC):
                        if u == 0 and s == 0:
                            pe.wait_ge(x_lo_done, BANKS + DC * i + c + 1)
                            pe.wait_ge(gu_lo_done, DC * i + c + 1)
                        mm = three_pass(pe, ps_h[0:n, u % 2, s], gu_hi[:, c, at], gu_lo[:, c, at], x_hi[:, c], x_lo[:, c],
                                        c == 0, c == DC - 1)
                mm.then_inc(h_ready, 1)

            def down(i, b, units):
                for u in units:
                    n = E_UNITS[u]
                    if b == 0:
                        if u == 0:
                            pe.wait_ge(dn_lo_done, i + 1)
                        pe.wait_ge(h_lo_done, U * i + u + 1)
                    if u == 0:
                        pe.wait_ge(y_read, BLOCKS * i + b + 1)
                    mm = three_pass(pe, ps_y[:, b % 2], h_hi[0:n, u, b * P:(b + 1) * P], h_lo[0:n, u, b * P:(b + 1) * P],
                                    dn_hi[0:n, u], dn_lo[0:n, u], u == 0, u == U - 1)
                    if u == U - 1:
                        mm.then_inc(y_ready, 1)

            def tile(i, more):
                hidden(i, 0)
                hidden(i, 1)
                if more:
                    turn(i + 1, 0)
                    turn(i + 1, 1)
                hidden(i, 2)
                down(i, 0, (0, 1))
                down(i, 1, (0, 1))
                down(i, 0, (2,))
                down(i, 1, (2,))
                if more:
                    turn(i + 1, 2)
                down(i, 2, range(U))
                if more:
                    turn(i + 1, 3)
                down(i, 3, range(U))

            for c in range(DC):
                turn(0, c)
            with pe.Fori(0, LAST) as i:
                tile(i, True)
            tile(LAST, False)


def combine(nc, x2_tiles, y_dram, out_tiles, ident, shared, kept, rt):
    with ExitStack() as ctx:
        def sb(name, shape, dt=F32):
            return ctx.enter_context(nc.sbuf_tensor("c_" + name, shape, dt))

        def sem(name):
            return ctx.enter_context(nc.semaphore("c_" + name))

        xt = sb("xt", [P, TILES, D])
        res = sb("res", [P, TILES, D])
        y = sb("y", [P, 2, TILES, D])
        y_kept = sb("y_kept", [P, 2, TILES, D])
        index = sb("index", [P, 2, TILES], I32)
        carrier = sb("carrier", [P, 1])
        ln = Moments(sb, "ln", TILES)
        ln_kept = Moments(sb, "kept", TILES)
        shared.block(sb, sem, lambda name, shape, dt: ctx.enter_context(nc.psum_tensor("c_" + name, shape, dt)))

        ln_const = sem("ln_const")
        xt_loaded = sem("xt_loaded")
        res_loaded = sem("res_loaded")
        indexed = sem("indexed")
        carried = sem("carried")
        y_gathered = sem("y_gathered")
        y_kept_gathered = sem("y_kept_gathered")
        add_step = sem("add_step")
        y_read = sem("y_read")
        kept_step = sem("kept_step")
        ln_step = sem("ln_step")
        var_done = sem("var_done")
        rstd_done = sem("rstd_done")
        out_ready = sem("out_ready")
        out_stored = sem("out_stored")
        kept_ln_step = sem("kept_ln_step")
        kept_var_done = sem("kept_var_done")
        kept_rstd_done = sem("kept_rstd_done")
        kept_ready = sem("kept_ready")
        kept_stored = sem("kept_stored")

        KEPT = GROUPS - 1
        LAST = KEPT - 1

        block = ctx.enter_context(nc.Block())

        @block.sync
        def _(sp):
            def tiles(dram, g):
                return dram[g] if isinstance(g, int) else dram[bass.ds(g, 1)].rearrange("o p t d -> p (o t) d")

            sp.dma_start(xt[:], x2_tiles[0]).then_inc(xt_loaded, 16)
            with sp.Fori(0, LAST) as g:
                sp.wait_ge(out_stored, 16 * g)
                sp.dma_start(res[:], tiles(x2_tiles, g)).then_inc(res_loaded, 16)
                sp.wait_ge(shared.x_ready, DC * g + DC)
                sp.dma_start(xt[:], tiles(x2_tiles, g + 1)).then_inc(xt_loaded, 16)
                sp.wait_ge(out_ready, TILES * g + TILES)
                sp.dma_start(tiles(out_tiles, g), res[:]).then_inc(out_stored, 16)
            sp.wait_ge(out_stored, 16 * LAST)
            sp.dma_start(res[:], x2_tiles[LAST]).then_inc(res_loaded, 16)
            sp.wait_ge(kept_ready, TILES)
            sp.dma_start(out_tiles[KEPT], kept[:]).then_inc(kept_stored, 16)
            for t in range(TILES):
                sp.wait_ge(out_ready, TILES * LAST + t + 1)
                sp.dma_start(out_tiles[LAST][:, t], res[:, t]).then_inc(out_stored, 16)
            sp.wait_ge(kept_stored, 16)
            sp.wait_ge(out_stored, 16 * (LAST + TILES))

        @block.gpsimd
        def _(pool):
            def gather(n, into, done):
                if isinstance(n, int):
                    first = (KEPT if n == 0 else 0) * TILES
                    slots = rt.slot[:, :, first:first + TILES]
                else:
                    slots = rt.slot[:, :, bass.ds(TILES * (n - 1), TILES)]
                    pool.wait_ge(y_read, TILES * (n - 1))
                pool.wait_ge(carried, n + 1)
                pool.tensor_copy(index[:], slots).then_inc(indexed, 1)
                pool.wait_ge(indexed, n + 1)
                pool.tensor_tensor(carrier[:], carrier[:], carrier[:], ALU.add).then_inc(carried, 1)
                for t in range(TILES):
                    for k in range(2):
                        pool.indirect_dma_start(into[:, k, t], None, y_dram,
                                                bass.IndirectOffsetOnAxis(ap=index[:, k, t:t + 1], axis=0)).then_inc(done, 16)

            pool.memset(ln.power[:], -0.5).then_inc(ln_const, 1)
            pool.memset(ln_kept.power[:], -0.5).then_inc(ln_const, 1)
            pool.memset(carrier[:], 0.0).then_inc(carried, 1)
            pool.wait_ge(ln_const, 2)
            gather(0, y_kept, y_kept_gathered)
            pool.wait_ge(y_kept_gathered, 2 * TILES * 16)

            def root(g):
                pool.wait_ge(var_done, g + 1)
                pool.tensor_tensor(ln.rstd[:], ln.var[:], ln.power[:], ALU.pow).then_inc(rstd_done, 1)

            gather(1, y, y_gathered)
            with pool.Fori(0, LAST) as g:
                root(g)
                gather(g + 2, y, y_gathered)
            pool.wait_ge(kept_var_done, 1)
            pool.tensor_tensor(ln_kept.rstd[:], ln_kept.var[:], ln_kept.power[:], ALU.pow).then_inc(kept_rstd_done, 1)
            root(LAST)

        @block.scalar
        def _(act):
            act.preload_act_table_set("silu_and_others")
            for c in range(DC):
                shared.x_round(act, 0, c)
            with act.Fori(0, LAST) as g:
                for u in range(Shared.U):
                    shared.gate(act, g, u)
                for c in range(DC):
                    shared.x_round(act, g + 1, c)
            for u in range(Shared.U):
                shared.gate(act, LAST, u)

        @block.vector
        def _(dve):
            def weigh(res, y, w, done):
                for t in range(TILES):
                    dve.scalar_tensor_tensor(res[:, t], y[:, t], w(t), res[:, t], ALU.mult, ALU.add).then_inc(done, 1)

            def weigh_group(g):
                def w(k):
                    if isinstance(g, int):
                        return lambda t: rt.weight[:, k, TILES * g + t:TILES * g + t + 1]
                    return lambda t: rt.weight[:, k, bass.ds(TILES * g + t, 1)]

                dve.wait_ge(res_loaded, 16 * g + 16)
                dve.wait_ge(y_gathered, 2 * TILES * 16 * (g + 1))
                weigh(res, y[:, 0], w(0), add_step)
                dve.wait_ge(add_step, TILES * g + TILES)
                weigh(res, y[:, 1], w(1), y_read)
                dve.wait_ge(y_read, TILES * g + TILES)

            def finish(g):
                dve.wait_ge(shared.out_free, Shared.BANKS + TILES * g + TILES)
                moments(dve, res, ln, ln_step, (TILES + 6) * g, var_done)
                dve.wait_ge(rstd_done, g + 1)
                for t in range(TILES):
                    dve.tensor_scalar(res[:, t], res[:, t], ln.mean[:, t:t + 1], ln.rstd[:, t:t + 1],
                                      ALU.subtract, ALU.mult).then_inc(out_ready, 1)

            def weight_kept(k):
                return lambda t: rt.weight[:, k, TILES * KEPT + t:TILES * KEPT + t + 1]

            shared.begin(dve)
            for c in range(DC):
                shared.x_rest(dve, 0, c)
            with dve.Fori(0, LAST) as g:
                for u in range(Shared.U):
                    shared.up(dve, g, u)
                shared.x_rest(dve, g + 1, 0)
                shared.x_rest(dve, g + 1, 1)
                weigh_group(g)
                shared.add(dve, res, g, 0)
                shared.x_rest(dve, g + 1, 2)
                shared.add(dve, res, g, 1)
                shared.x_rest(dve, g + 1, 3)
                shared.add(dve, res, g, 2)
                shared.add(dve, res, g, 3)
                finish(g)
            for u in range(Shared.U):
                shared.up(dve, LAST, u)
                if u == 0:
                    dve.wait_ge(y_kept_gathered, 2 * TILES * 16)
                    weigh(kept, y_kept[:, 0], weight_kept(0), kept_step)
                if u == 1:
                    dve.wait_ge(kept_step, TILES)
                    weigh(kept, y_kept[:, 1], weight_kept(1), kept_step)
                if u == 2:
                    dve.wait_ge(kept_step, 2 * TILES)
                    moments(dve, kept, ln_kept, kept_ln_step, 0, kept_var_done)
                if u == 3:
                    dve.wait_ge(kept_rstd_done, 1)
                    for t in range(TILES):
                        dve.tensor_scalar(kept[:, t], kept[:, t], ln_kept.mean[:, t:t + 1], ln_kept.rstd[:, t:t + 1],
                                          ALU.subtract, ALU.mult).then_inc(kept_ready, 1)
            weigh_group(LAST)
            for t in range(TILES):
                shared.add(dve, res, LAST, t)
            finish(LAST)

        @block.tensor
        def _(pe):
            def turn(n, c):
                if c == 0:
                    pe.wait_ge(xt_loaded, 16 * n + 16)
                shared.turn(pe, xt, ident, n, c)

            def hidden(n):
                pe.wait_ge(shared.x_lo_done, Shared.BANKS + DC * n + DC)
                for u in range(Shared.U):
                    shared.hidden(pe, n, u)

            for c in range(DC):
                turn(0, c)
            with pe.Fori(0, LAST) as g:
                hidden(g)
                turn(g + 1, 0)
                turn(g + 1, 1)
                shared.down(pe, g, 0)
                turn(g + 1, 2)
                shared.down(pe, g, 1)
                turn(g + 1, 3)
                shared.down(pe, g, 2)
                shared.down(pe, g, 3)
            hidden(LAST)
            for t in range(TILES):
                shared.down(pe, LAST, t)


def program(nc, x_t, x_tok, w_in, w_out, conv_w, conv_b, gain, ctx_t, w_q, w_kv, w_o, w_router, we_gate_up, we_down,
            ws_gate_up, ws_down, out):
    x1 = nc.dram_tensor("x1", (GROUPS, P, TILES, D), F32, kind="Internal").ap()
    x2 = nc.dram_tensor("x2", (T, D), F32, kind="Internal").ap()
    y = nc.dram_tensor("y_slots", (E_TILES * SLOTS, D), F32, kind="Internal").ap()
    x2_tiles = x2.rearrange("(g t p) d -> g p t d", p=P, t=TILES)
    out_tiles = out.rearrange("(g b) (s p) d -> g p (b s) d", b=GB, p=P)
    with ExitStack() as ctx:
        def sb(name, shape, dt=F32):
            return ctx.enter_context(nc.sbuf_tensor("f_" + name, shape, dt))

        ident = sb("ident", [P, P])
        sums = sb("sums", [P, TILES, D])
        ln = Moments(sb, "attention", TILES)
        with nc.sbuf_tensor("arena", [P, 2 * JC * DC * 2 * P], F32R) as arena:
            cross = CrossWeights(arena[:], w_q, w_kv, w_o)
            gated_conv(nc, x_t, x_tok, w_in, w_out, conv_w, conv_b, gain, x1, arena[:], cross.units)
            cross_attention(nc, x1, ctx_t, cross, x2_tiles, ident, sums, ln)
        rt = Routing(sb)
        kept = sums
        shared = Shared(sb)
        raw = (sb("gate_up_raw", [P, DC, 2 * DE])[:], sb("down_raw", [P, len(E_UNITS), D])[:])
        route(nc, x2_tiles, w_router, sums, ln, ident, shared, ws_gate_up, ws_down, we_gate_up, we_down, raw, kept, rt)
        experts(nc, x2, we_gate_up, we_down, y, ident, raw, rt)
        combine(nc, x2_tiles, y, out_tiles, ident, shared, kept, rt)


def layouts(inputs):
    import numpy as np

    def get(name):
        return np.asarray(inputs["L0_" + name])

    def square(name):
        return get(name).T.reshape(2, 2, P, D).transpose(0, 2, 1, 3).reshape(2, P, 2 * D)

    def gate_up(gate, up, width):
        both = np.stack([get(gate), get(up)], axis=-2)
        lead = both.shape[:-3]
        both = both.reshape(*lead, DC, P, 2 * width)
        return np.swapaxes(both, -3, -2)

    x = np.asarray(inputs["x"])
    ctx = np.asarray(inputs["ctx_512"])
    out = {
        "x_t": x.reshape(GROUPS, GT, DC, P).transpose(0, 3, 2, 1),
        "x_tok": x.reshape(GROUPS, TILES, P, D).transpose(0, 2, 1, 3),
        "w_in": get("attn_w_in").reshape(2, JC, P, DC, P).transpose(1, 4, 3, 0, 2).reshape(JC, P, 1024),
        "w_out": get("attn_w_out").reshape(D, JC // 2, 2, P).transpose(1, 3, 2, 0).reshape(JC // 2, P, 1024),
        "conv_w": get("attn_conv_w").reshape(JC, P, TAPS).transpose(1, 0, 2),
        "conv_b": get("attn_conv_b").reshape(JC, P).T,
        "gain": get("attn_D").reshape(JC, P).T,
        "ctx_t": ctx.reshape(GROUPS, GT, L).transpose(0, 2, 1),
        "w_q": square("xattn_Wq"),
        "w_kv": get("xattn_Wkv_expand").T,
        "w_o": square("xattn_Wout"),
        "w_router": get("ffn_W_router").reshape(DC, P, E_N).transpose(1, 0, 2),
        "we_gate_up": gate_up("ffn_We_gate", "ffn_We_up", DE),
        "we_down": get("ffn_We_down"),
        "ws_gate_up": gate_up("ffn_Ws_gate", "ffn_Ws_up", DS),
        "ws_down": get("ffn_Ws_down"),
    }
    return {k: np.ascontiguousarray(v) for k, v in out.items()}


def kernel(**inputs):
    import concourse.bacc as bacc
    import numpy as np
    from concourse.bass_utils import run_bass_kernel_spmd

    nc = bacc.Bacc("TRN2", target_bir_lowering=False, num_devices=1)
    arrays = layouts(inputs)
    args = [nc.dram_tensor(name, a.shape, mybir.dt.from_np(a.dtype), kind="ExternalInput").ap()
            for name, a in arrays.items()]
    out = nc.dram_tensor("out", (B, S, D), F32, kind="ExternalOutput").ap()
    program(nc, *args, out)
    result = run_bass_kernel_spmd(nc, [arrays], core_ids=[0])
    return np.asarray(result.results[0]["out"])
```

```python
from contextlib import ExitStack

import concourse.bass as bass
from concourse import mybir

F32 = mybir.dt.float32
F32R = mybir.dt.float32r
BF16 = mybir.dt.bfloat16
I32 = mybir.dt.int32
U32 = mybir.dt.uint32
ALU = mybir.AluOpType
ACT = mybir.ActivationFunctionType
AX_X = mybir.AxisListType.X

P = 128
B, S, D = 8, 256, 512
T = B * S
GT = 512
GROUPS = T // GT
GB = GT // S
TILES = GT // P
DC = D // P
DI = 1024
JC = DI // P
TAPS = 4
EPS = 1e-5


def three_pass(pe, out, a_hi, a_lo, b_hi, b_lo, first, last):
    pe.matmul(out, a_hi, b_lo, start=first, stop=False)
    pe.matmul(out, a_lo, b_hi, start=False, stop=False)
    return pe.matmul(out, a_hi, b_hi, start=False, stop=last)


class Moments:

    def __init__(self, sb, name, n):
        self.n = n
        self.stats = sb(name + "_ln_stats", [P, n, 6])
        self.sum = sb(name + "_ln_sum", [P, n])
        self.diff = sb(name + "_ln_diff", [P, n])
        self.sq = sb(name + "_ln_sq", [P, n])
        self.mean = sb(name + "_ln_mean", [P, n])
        self.sq_eps = sb(name + "_ln_sq_eps", [P, n])
        self.diff_sq = sb(name + "_ln_diff_sq", [P, n])
        self.var = sb(name + "_ln_var", [P, n])
        self.power = sb(name + "_ln_power", [P, n])
        self.rstd = sb(name + "_ln_rstd", [P, n])


def moments(dve, x, ln, step, base, var_done):
    for k in range(ln.n + 3):
        moments_step(dve, x, ln, k, step, base, var_done)


def moments_step(dve, x, ln, k, step, base, var_done):
    n, s = ln.n, ln.stats
    if 0 <= k < n:
        dve.bn_stats(s[:, k], x[:, k]).then_inc(step, 1)
    if k == n:
        dve.wait_ge(step, base + n)
        dve.tensor_tensor(ln.sum[:], s[:, :, 1], s[:, :, 4], ALU.add).then_inc(step, 1)
        dve.tensor_tensor(ln.diff[:], s[:, :, 1], s[:, :, 4], ALU.subtract).then_inc(step, 1)
        dve.tensor_tensor(ln.sq[:], s[:, :, 2], s[:, :, 5], ALU.add).then_inc(step, 1)
    if k == n + 1:
        dve.wait_ge(step, base + n + 3)
        dve.tensor_scalar(ln.mean[:], ln.sum[:], 0.5, None, ALU.mult).then_inc(step, 1)
        dve.tensor_scalar(ln.sq_eps[:], ln.sq[:], 1.0 / D, EPS, ALU.mult, ALU.add).then_inc(step, 1)
        dve.scalar_tensor_tensor(ln.diff_sq[:], ln.diff[:], 0.25, ln.diff[:], ALU.mult, ALU.mult).then_inc(step, 1)
    if k == n + 2:
        dve.wait_ge(step, base + n + 6)
        dve.tensor_tensor(ln.var[:], ln.sq_eps[:], ln.diff_sq[:], ALU.add).then_inc(var_done, 1)


def gated_conv(nc, x_t, x_tok, w_in, w_out, conv_w, conv_b, gain, x1_dram, arena, following, x1, ln, ident,
               xt_next, ctx_t, ctx_next):
    with ExitStack() as ctx:
        def sb(name, shape, dt=F32):
            return ctx.enter_context(nc.sbuf_tensor(name, shape, dt))

        def sem(name):
            return ctx.enter_context(nc.semaphore(name))

        w_raw = sb("a_w_raw", [P, 2, 1024])
        half = JC * DC * 2 * P
        wi_hi = arena[:, 0:half].rearrange("p (j c s m) -> p j c s m", j=JC, c=DC, s=2)
        wi_lo = arena[:, half:2 * half].rearrange("p (j c s m) -> p j c s m", j=JC, c=DC, s=2)
        wo_hi = sb("a_wo_hi", [P, JC, D], F32R)
        wo_lo = sb("a_wo_lo", [P, JC, D], F32R)
        taps = sb("a_taps", [P, JC, TAPS])
        bias = sb("a_bias", [P, JC])
        dgain = sb("a_dgain", [P, JC])
        x_raw = sb("a_x_raw", [P, DC, GT])
        x_hi = sb("a_x_hi", [P, DC, GT], F32R)
        x_lo = sb("a_x_lo", [P, DC, GT], F32R)
        xc = sb("a_xc", [P, 2, GB, S])
        sg = sb("a_sg", [P, 2, GT])
        hf = sb("a_hf", [P, 2, GT])
        h_hi = sb("a_h_hi", [P, JC, GT], F32R)
        h_lo = sb("a_h_lo", [P, JC, GT], F32R)
        xt = sb("a_xt", [P, TILES, D])
        ps_proj = ctx.enter_context(nc.psum_tensor("a_ps_proj", [P, 2, 2, GT], F32))
        ps_out = ctx.enter_context(nc.psum_tensor("a_ps_out", [P, TILES, D], F32))

        w_loaded = [sem("a_w_loaded_even"), sem("a_w_loaded_odd")]
        w_hi_done = sem("a_w_hi_done")
        w_lo_done = sem("a_w_lo_done")
        consts_loaded = sem("a_consts_loaded")
        x_loaded = sem("a_x_loaded")
        xt_loaded = sem("a_xt_loaded")
        x_hi_done = sem("a_x_hi_done")
        x_lo_done = sem("a_x_lo_done")
        first_lo_done = sem("a_first_lo_done")
        chunk_loaded = [sem("a_chunk_loaded_%d" % c) for c in range(DC)]
        proj_done = sem("a_proj_done")
        gate_free = sem("a_gate_free")
        tap_last = sem("a_tap_last")
        tap_step = sem("a_tap_step")
        conv_done = sem("a_conv_done")
        silu_done = sem("a_silu_done")
        h_done = sem("a_h_done")
        h_hi_done = sem("a_h_hi_done")
        h_lo_done = sem("a_h_lo_done")
        out_done = sem("a_out_done")
        out_free = sem("a_out_free")
        ln_step = sem("a_ln_step")
        ln_const = sem("a_ln_const")
        var_done = sem("a_var_done")
        rstd_done = sem("a_rstd_done")
        x1_ready = sem("a_x1_ready")
        x1_stored = sem("a_x1_stored")

        BANKS = 2
        W_UNITS = JC + JC // 2
        W_AHEAD = 3
        ALL_UNITS = W_UNITS + len(following)

        def w_unit(u, hi):
            if u >= W_UNITS:
                return following[u - W_UNITS][1 if hi else 2]
            if u < JC:
                return (wi_hi if hi else wi_lo)[:, u].rearrange("p c s m -> p (c s m)")
            c = 2 * (u - JC)
            return (wo_hi if hi else wo_lo)[:, c:c + 2].rearrange("p c n -> p (c n)")

        block = ctx.enter_context(nc.Block())

        @block.sync
        def _(sp):
            for c in range(DC):
                sp.dma_start(x_raw[:, c], x_t[0][:, c]).then_inc(chunk_loaded[c], 16)
                if c == 0:
                    sp.dma_start(w_raw[:, 0], w_in[0]).then_inc(w_loaded[0], 16)
            sp.dma_start(taps[:], conv_w).then_inc(consts_loaded, 16)
            sp.dma_start(bias[:], conv_b).then_inc(consts_loaded, 16)
            sp.dma_start(dgain[:], gain).then_inc(consts_loaded, 16)
            for u in range(1, W_UNITS):
                if u >= 2:
                    sp.wait_ge(w_lo_done, u - 1)
                src = w_in[u] if u < JC else w_out[u - JC]
                sp.dma_start(w_raw[:, u % 2], src).then_inc(w_loaded[u % 2], 16)
            sp.wait_ge(first_lo_done, DC)
            with sp.Fori(0, GROUPS - 1) as g:
                sp.wait_ge(x1_ready, TILES * g)
                sp.dma_start(xt[:], x_tok[bass.ds(g, 1)].rearrange("o p t d -> p (o t) d")).then_inc(xt_loaded, 16)
                sp.wait_ge(x_lo_done, g)
                sp.dma_start(x_raw[:], x_t[bass.ds(g + 1, 1)].rearrange("o p c t -> p (o c) t")).then_inc(x_loaded, 16)
            sp.wait_ge(x1_ready, TILES * (GROUPS - 1))
            sp.dma_start(xt[:], x_tok[GROUPS - 1]).then_inc(xt_loaded, 16)
            for u in range(W_UNITS, ALL_UNITS):
                sp.wait_ge(w_lo_done, u - 1)
                sp.dma_start(w_raw[:, u % 2], following[u - W_UNITS][0]).then_inc(w_loaded[u % 2], 16)
            sp.wait_ge(x1_stored, 16)
            sp.dma_start(xt_next[:], x1_dram[0]).then_inc(xt_loaded, 16)
            sp.dma_start(ctx_next[:], ctx_t[0]).then_inc(xt_loaded, 16)
            sp.wait_ge(xt_loaded, 16 * (GROUPS + 2))

        @block.gpsimd
        def _(pool):
            def split_x(g):
                pool.wait_ge(x_hi_done, DC + g)
                pool.tensor_tensor(x_lo[:], x_raw[:], x_hi[:].bitcast(F32), ALU.subtract).then_inc(x_lo_done, 1)

            def root(g):
                pool.wait_ge(ln_const, 1)
                pool.wait_ge(var_done, g + 1)
                pool.tensor_tensor(ln.rstd[:], ln.var[:], ln.power[:], ALU.pow).then_inc(rstd_done, 1)

            pool.memset(ln.power[:], -0.5).then_inc(ln_const, 1)
            def split_w(u):
                pool.wait_ge(w_hi_done, u + 1)
                pool.tensor_tensor(w_unit(u, False), w_raw[:, u % 2], w_unit(u, True).bitcast(F32),
                                   ALU.subtract).then_inc(w_lo_done, 1)

            for u in range(W_UNITS):
                split_w(u)
            pool.memset(ident[:], 0.0).then_inc(ln_const, 1)
            pool.wait_ge(ln_const, 2)
            pool.affine_select(out=ident[:], in_=ident[:], compare_op=ALU.not_equal, fill=1.0, base=0,
                               pattern=[[-1, P]], channel_multiplier=1).then_inc(ln_const, 1)
            with pool.Fori(0, GROUPS - 1) as g:
                split_x(g + 1)
                root(g)
                pool.wait_ge(x1_ready, TILES * g + TILES)
                pool.dma_start(x1_dram[bass.ds(g, 1)].rearrange("o p t d -> p (o t) d"), x1[:]).then_inc(x1_stored, 16)
            for u in range(W_UNITS, ALL_UNITS):
                split_w(u)
            pool.wait_ge(x1_stored, 16 * (GROUPS - 1))

        @block.scalar
        def _(act):
            act.preload_act_table_set("silu_and_others")

            def split_x(g):
                act.wait_ge(x_loaded, 16 * g)
                act.wait_ge(proj_done, JC * g)
                act.activation(x_hi[:], x_raw[:], ACT.Copy).then_inc(x_hi_done, 1)

            def h_round(g, j):
                act.wait_ge(h_done, JC * g + j + 1)
                if j == 0:
                    act.wait_ge(out_done, TILES * g)
                act.activation(h_hi[:, j], hf[:, j % 2], ACT.Copy).then_inc(h_hi_done, 1)

            def split_w(u):
                act.wait_ge(w_loaded[u % 2], 16 * (u // 2) + 16)
                act.activation(w_unit(u, True), w_raw[:, u % 2], ACT.Copy).then_inc(w_hi_done, 1)

            for c in range(DC):
                act.wait_ge(chunk_loaded[c], 16)
                act.activation(x_hi[:, c], x_raw[:, c], ACT.Copy).then_inc(x_hi_done, 1)
                if c == 0:
                    split_w(0)
            act.sem_inc(gate_free, BANKS)
            for u in range(1, W_AHEAD):
                split_w(u)
            act.wait_ge(consts_loaded, 48)

            def group(g):
                for j in range(JC):
                    xcj = xc[:, j % 2].rearrange("p b s -> p (b s)")
                    act.wait_ge(proj_done, JC * g + j + 1)
                    act.activation(xcj, ps_proj[:, j % 2, 0], ACT.Identity,
                                   scale=taps[:, j, TAPS - 1:TAPS], bias=bias[:, j:j + 1]).then_inc(tap_last, 1)
                    act.activation(sg[:, j % 2], ps_proj[:, j % 2, 1], ACT.Silu).then_inc(gate_free, 1)
                    if isinstance(g, int) and g == 0:
                        for u in range(W_AHEAD + 2 * j, min(W_AHEAD + 2 * j + 2, W_UNITS)):
                            split_w(u)
                    if j:
                        h_round(g, j - 1)
                    act.wait_ge(conv_done, BANKS + JC * g + j + 1)
                    act.activation(xcj, xcj, ACT.Silu).then_inc(silu_done, 1)
                h_round(g, JC - 1)

            group(0)
            split_x(1)
            with act.Fori(1, GROUPS - 1) as g:
                group(g)
                split_x(g + 1)
            group(GROUPS - 1)
            for u in range(W_UNITS, ALL_UNITS):
                split_w(u)

        @block.vector
        def _(dve):
            dve.sem_inc(conv_done, BANKS)
            for c in range(DC):
                dve.wait_ge(x_hi_done, c + 1)
                dve.tensor_tensor(x_lo[:, c], x_raw[:, c], x_hi[:, c].bitcast(F32), ALU.subtract).then_inc(first_lo_done, 1)
            dve.wait_ge(consts_loaded, 48)

            def h_rest(g, j):
                dve.wait_ge(h_hi_done, JC * g + j + 1)
                dve.tensor_tensor(h_lo[:, j], hf[:, j % 2], h_hi[:, j].bitcast(F32), ALU.subtract).then_inc(h_lo_done, 1)

            def conv(g):
                for j in range(JC):
                    dve.wait_ge(tap_last, JC * g + j + 1)
                    xi = ps_proj[:, j % 2, 0].rearrange("p (b s) -> p b s", b=GB)
                    for s in range(1, TAPS):
                        if s > 1:
                            dve.wait_ge(tap_step, (TAPS - 2) * (JC * g + j) + s - 1)
                        ins = dve.scalar_tensor_tensor(xc[:, j % 2, :, s:S], xi[:, :, 0:S - s],
                                                       taps[:, j, TAPS - 1 - s:TAPS - s], xc[:, j % 2, :, s:S],
                                                       ALU.mult, ALU.add)
                        ins.then_inc(tap_step if s < TAPS - 1 else conv_done, 1)
                    if j:
                        h_rest(g, j - 1)
                    dve.wait_ge(silu_done, JC * g + j + 1)
                    dve.scalar_tensor_tensor(hf[:, j % 2], xc[:, j % 2].rearrange("p b s -> p (b s)"),
                                             dgain[:, j:j + 1], sg[:, j % 2], ALU.mult, ALU.mult).then_inc(h_done, 1)
                h_rest(g, JC - 1)

            def add_x(g, into):
                dve.wait_ge(xt_loaded, 16 * g + 16)
                for t in range(TILES):
                    dve.wait_ge(out_done, TILES * g + t + 1)
                    dve.tensor_tensor(into[:, t], ps_out[:, t], xt[:, t], ALU.add).then_inc(out_free, 1)

            with dve.Fori(0, GROUPS - 1) as g:
                conv(g)
                add_x(g, xt)
                dve.wait_ge(out_free, TILES * g + TILES)
                moments(dve, xt, ln, ln_step, (TILES + 6) * g, var_done)
                dve.wait_ge(rstd_done, g + 1)
                dve.wait_ge(x1_stored, 16 * g)
                for t in range(TILES):
                    dve.tensor_scalar(x1[:, t], xt[:, t], ln.mean[:, t:t + 1], ln.rstd[:, t:t + 1],
                                      ALU.subtract, ALU.mult).then_inc(x1_ready, 1)
            conv(GROUPS - 1)
            dve.wait_ge(x1_stored, 16 * (GROUPS - 1))
            add_x(GROUPS - 1, x1)

        @block.tensor
        def _(pe):
            pe.wait_ge(first_lo_done, DC)
            with pe.Fori(0, GROUPS) as g:
                pe.wait_ge(x_lo_done, g)
                for j in range(JC):
                    pe.wait_ge(w_lo_done, j + 1)
                    for side, free in ((0, conv_done), (1, gate_free)):
                        pe.wait_ge(free, JC * g + j + 1)
                        for c in range(DC):
                            mm = three_pass(pe, ps_proj[:, j % 2, side], wi_hi[:, j, c, side], wi_lo[:, j, c, side],
                                            x_hi[:, c], x_lo[:, c], c == 0, c == DC - 1)
                    mm.then_inc(proj_done, 1)
                pe.wait_ge(w_lo_done, W_UNITS)
                pe.wait_ge(out_free, TILES * g)
                for j in range(JC):
                    pe.wait_ge(h_lo_done, JC * g + j + 1)
                    for t in range(TILES):
                        mm = three_pass(pe, ps_out[:, t], h_hi[:, j, t * P:(t + 1) * P], h_lo[:, j, t * P:(t + 1) * P],
                                        wo_hi[:, j], wo_lo[:, j], j == 0, j == JC - 1)
                        if j == JC - 1:
                            mm.then_inc(out_done, 1)


HEADS = 16
HD = D // HEADS
HC = P // HD
L = 128
SCALE = 1.0 / float(HD) ** 0.5
MASKED = -1e30


class CrossWeights:

    def __init__(self, arena, w_q, w_kv, w_o):
        n = DC * D
        h = n // 2
        at = [arena[:, k:k + size] for k, size in ((0, n), (n, n), (2 * n, n), (3 * n, n), (4 * n, h), (4 * n + h, h))]
        self.q_hi, self.q_lo, self.o_hi, self.o_lo, self.kv_hi, self.kv_lo = (
            w.rearrange("p (c n) -> p c n", n=D) for w in at)
        self.units = [(w_q[0], at[0][:, 0:h], at[1][:, 0:h]), (w_q[1], at[0][:, h:n], at[1][:, h:n]),
                      (w_kv, at[4], at[5]),
                      (w_o[0], at[2][:, 0:h], at[3][:, 0:h]), (w_o[1], at[2][:, h:n], at[3][:, h:n])]


def cross_attention(nc, x1_dram, ctx_t, weights, x2_dram, left_ln, ident, xt, c_raw, res, ln):
    with ExitStack() as ctx:
        def sb(name, shape, dt=F32):
            return ctx.enter_context(nc.sbuf_tensor("b_" + name, shape, dt))

        def sem(name):
            return ctx.enter_context(nc.semaphore("b_" + name))

        GH = GB * HEADS
        AHEAD = 4
        HB = AHEAD + 1
        wq_hi, wq_lo, wkv_hi, wkv_lo = weights.q_hi, weights.q_lo, weights.kv_hi, weights.kv_lo
        wo_hi, wo_lo = weights.o_hi, weights.o_lo
        mask = sb("mask", [P, 3 * P])
        x_hi = sb("x_hi", [P, DC, GT], F32R)
        x_lo = sb("x_lo", [P, DC, GT], F32R)
        c_hi = sb("c_hi", [P, GT], F32R)
        c_lo = sb("c_lo", [P, GT], F32R)
        q = sb("q", [P, DC, GT])
        k = sb("k", [P, DC, HC, GT])
        v = sb("v", [P, TILES, DC, HC, P])
        carrier = sb("carrier", [P, GH])
        pr = sb("pr", [P, HB, 3 * P])
        bmax = sb("bmax", [P, HB, 2])
        rsum = sb("rsum", [P, HB, 2])
        rinv = sb("rinv", [P, HB, 2])
        pt = sb("pt", [P, 2, 3 * P])
        a_hi = sb("a_hi", [P, DC, GT], F32R)
        a_lo = sb("a_lo", [P, DC, GT], F32R)
        ps_pj = ctx.enter_context(nc.psum_tensor("b_ps_pj", [P, 2, 512], F32))
        ps_s = ctx.enter_context(nc.psum_tensor("b_ps_s", [P, 2, 512], F32))
        ps_t = ctx.enter_context(nc.psum_tensor("b_ps_t", [P, 2, 512], F32))
        ps_o = ctx.enter_context(nc.psum_tensor("b_ps_o", [P, 2, 512], F32))

        consts = sem("consts")
        zeros = sem("zeros")
        xt_loaded = sem("xt_loaded")
        c_loaded = sem("c_loaded")
        res_loaded = sem("res_loaded")
        c_hi_done = sem("c_hi_done")
        c_lo_done = sem("c_lo_done")
        x_ready = sem("x_ready")
        x_hi_done = sem("x_hi_done")
        x_lo_done = sem("x_lo_done")
        q_ready = sem("q_ready")
        q_done = sem("q_done")
        k_ready = sem("k_ready")
        k_done = sem("k_done")
        v_ready = sem("v_ready")
        v_done = sem("v_done")
        out_ready = sem("out_ready")
        out_added = sem("out_added")
        left_step = sem("left_step")
        left_var_done = sem("left_var_done")
        left_rstd_done = sem("left_rstd_done")
        left_ready = sem("left_ready")
        left_stored = sem("left_stored")
        s_ready = sem("s_ready")
        max_done = sem("max_done")
        exp_done = sem("exp_done")
        rinv_done = sem("rinv_done")
        norm_done = sem("norm_done")
        pt_ready = sem("pt_ready")
        pt_free = sem("pt_free")
        pv_done = sem("pv_done")
        o_hi_done = sem("o_hi_done")
        o_free = sem("o_free")
        ln_step = sem("ln_step")
        var_done = sem("var_done")
        rstd_done = sem("rstd_done")
        x2_ready = sem("x2_ready")
        x2_stored = sem("x2_stored")

        CONSTS = 6
        BANKS = 2
        LAST = GROUPS - 1
        ROOT = 10
        CONTEXT = 16
        GC = GB * DC
        STEPS = GH + AHEAD + 3

        def seq(n):
            return n // HEADS, n % HEADS // HC, n % HC

        block = ctx.enter_context(nc.Block())

        @block.sync
        def _(sp):
            sp.wait_ge(left_ready, TILES)
            sp.dma_start(x1_dram[LAST], res[:]).then_inc(left_stored, 16)
            sp.wait_ge(left_stored, 16)

            def load(dram, g, into, done):
                src = dram[g] if isinstance(g, int) else dram[bass.ds(g, 1)].rearrange("o p t d -> p (o t) d")
                sp.dma_start(into, src).then_inc(done, 16)

            def load_next(g):
                sp.wait_ge(x_ready, DC * g + DC)
                load(x1_dram, g + 1, xt[:], xt_loaded)
                sp.wait_ge(c_lo_done, g + 1)
                src = ctx_t[g + 1] if isinstance(g, int) else ctx_t[bass.ds(g + 1, 1)].rearrange("o p t -> p (o t)")
                sp.dma_start(c_raw[:], src).then_inc(c_loaded, 16)

            def store(g):
                sp.wait_ge(x2_ready, TILES * g + TILES)
                dst = x2_dram[g] if isinstance(g, int) else x2_dram[bass.ds(g, 1)].rearrange("o p t d -> p (o t) d")
                sp.dma_start(dst, res[:]).then_inc(x2_stored, 16)

            load_next(0)
            load(x1_dram, 0, res[:], res_loaded)
            with sp.Fori(1, LAST) as g:
                load_next(g)
                store(g - 1)
                sp.wait_ge(x2_stored, 16 * g)
                load(x1_dram, g, res[:], res_loaded)
            store(LAST - 1)
            sp.wait_ge(x2_stored, 16 * LAST)
            load(x1_dram, LAST, res[:], res_loaded)
            sp.wait_ge(x_ready, DC * GROUPS)
            load(x2_dram, 0, xt[:], xt_loaded)
            sp.wait_ge(xt_loaded, 16 * GROUPS)

        @block.gpsimd
        def _(pool):
            pool.memset(mask[:], 0.0).then_inc(consts, 1)
            pool.memset(ln.power[:], -0.5).then_inc(consts, 1)
            pool.wait_ge(consts, 2)
            for c in (0, 2):
                pool.affine_select(out=mask[:, c * P:(c + 1) * P], in_=mask[:, c * P:(c + 1) * P], compare_op=ALU.is_ge,
                                   fill=MASKED, base=0, pattern=[[-1, P]], channel_multiplier=1).then_inc(consts, 1)
            pool.memset(k[:], 0.0).then_inc(consts, 1)
            pool.memset(v[:, 2:TILES], 0.0).then_inc(consts, 1)

            def context(g):
                pool.wait_ge(c_hi_done, g + 1)
                pool.tensor_tensor(c_lo[:], c_raw[:], c_hi[:].bitcast(F32), ALU.subtract).then_inc(c_lo_done, 1)

            def attend(g, root, more):
                for n in range(GH):
                    pool.wait_ge(rinv_done, GH * g + n + 1)
                    for a, b, r in ((0, P, 0), (P, 3 * P, 1)):
                        ins = pool.tensor_tensor(pr[:, n % HB, a:b], pr[:, n % HB, a:b],
                                                 rinv[:, n % HB, r:r + 1].broadcast_to([P, b - a]), ALU.mult)
                    ins.then_inc(norm_done, 1)
                    if root and n == ROOT:
                        pool.wait_ge(var_done, g)
                        pool.tensor_tensor(ln.rstd[:], ln.var[:], ln.power[:], ALU.pow).then_inc(rstd_done, 1)
                    if more and n == CONTEXT:
                        context(g + 1)

            context(0)
            pool.wait_ge(left_var_done, 1)
            pool.tensor_tensor(left_ln.rstd[:], left_ln.var[:], left_ln.power[:], ALU.pow).then_inc(left_rstd_done, 1)
            attend(0, False, True)
            with pool.Fori(1, LAST) as g:
                attend(g, True, True)
            attend(LAST, True, False)

        @block.scalar
        def _(act):
            act.preload_act_table_set("exp_and_others")
            def context(g):
                act.wait_ge(c_loaded, 16 * g)
                act.wait_ge(v_ready, DC * g)
                act.activation(c_hi[:], c_raw[:], ACT.Copy).then_inc(c_hi_done, 1)

            def turned(g, c):
                act.wait_ge(x_ready, DC * g + c + 1)
                act.activation(x_hi[:, c], ps_pj[:, c % 2], ACT.Copy).then_inc(x_hi_done, 1)

            def keys(g):
                for c in range(DC):
                    act.wait_ge(k_ready, DC * g + c + 1)
                    for h in range(HC):
                        rows = slice(h * HD, (h + 1) * HD)
                        ins = act.activation(k[rows, c, h], ps_s[rows, c % 2], ACT.Copy)
                    ins.then_inc(k_done, 1)

            def attend(g, more):
                for n in range(STEPS):
                    if n < GH:
                        act.wait_ge(max_done, BANKS + GH * g + n + 1)
                        for a, b, r in ((0, P, 0), (P, 3 * P, 1)):
                            ins = act.activation(pr[:, n % HB, a:b], pr[:, n % HB, a:b], ACT.Exp, scale=-1.0,
                                                 bias=bmax[:, n % HB, r:r + 1], accum_out=rsum[:, n % HB, r:r + 1])
                        ins.then_inc(exp_done, 1)
                    m = n - AHEAD - 2
                    if 0 <= m < GH and m % HC == HC - 1:
                        b, c, _ = seq(m)
                        act.wait_ge(pv_done, BANKS + GH * g + m + 1)
                        act.activation(a_hi[:, c, b * S:(b + 1) * S], ps_o[:, m // HC % 2, 0:S], ACT.Copy)\
                            .then_inc(o_hi_done, 1)
                    if more and 0 <= n - GH < DC:
                        turned(g + 1, n - GH)
                    if more and n == CONTEXT:
                        context(g + 1)

            context(0)
            for c in range(DC):
                turned(0, c)
            act.wait_ge(consts, CONSTS - 1)
            keys(0)
            with act.Fori(0, LAST) as g:
                attend(g, True)
                keys(g + 1)
            attend(LAST, False)

        @block.vector
        def _(dve):
            dve.sem_inc(out_added, DC)
            dve.sem_inc(max_done, BANKS)
            dve.sem_inc(pt_free, BANKS)
            dve.sem_inc(o_free, BANKS)

            def turned(g, c):
                dve.wait_ge(x_hi_done, DC * g + c + 1)
                dve.tensor_tensor(x_lo[:, c], ps_pj[:, c % 2], x_hi[:, c].bitcast(F32), ALU.subtract).then_inc(x_lo_done, 1)

            def queries(g):
                for c in range(DC):
                    dve.wait_ge(q_ready, DC * g + c + 1)
                    dve.tensor_copy(q[:, c], ps_pj[:, c % 2]).then_inc(q_done, 1)

            def values(g, c):
                dve.wait_ge(v_ready, DC * g + c + 1)
                vs = ps_t[:, c % 2].rearrange("p (c h d) -> p c h d", c=DC, h=HC)
                for h in range(HC):
                    ins = dve.tensor_copy(v[:, c, :, h, h * HD:(h + 1) * HD], vs[:, :, h])
                ins.then_inc(v_done, 1)

            def attend(g, before, more):
                for n in range(STEPS):
                    if before:
                        moments_step(dve, res, ln, n - 1, ln_step, (TILES + 6) * (g - 1), var_done)
                        if n == ROOT + 2:
                            dve.wait_ge(rstd_done, g)
                        if 0 <= n - ROOT - 2 < TILES:
                            t = n - ROOT - 2
                            dve.tensor_scalar(res[:, t], res[:, t], ln.mean[:, t:t + 1], ln.rstd[:, t:t + 1],
                                              ALU.subtract, ALU.mult).then_inc(x2_ready, 1)
                    if n < GH:
                        dve.wait_ge(s_ready, GH * g + n + 1)
                        dve.memset(carrier[:, n:n + 1], 0.0)
                        for a, b, r in ((0, P, 0), (P, 3 * P, 1)):
                            ins = dve.tensor_tensor_reduce(pr[:, n % HB, a:b], ps_s[:, n % 2, a:b], mask[:, a:b], -SCALE, 3e38,
                                                           ALU.add, ALU.min, bmax[:, n % HB, r:r + 1])
                        ins.then_inc(max_done, 1)
                    m = n - 1
                    if 0 <= m < GH:
                        dve.wait_ge(exp_done, GH * g + m + 1)
                        dve.reciprocal(rinv[:, m % HB], rsum[:, m % HB]).then_inc(rinv_done, 1)
                    m = n - AHEAD
                    if 0 <= m < GH:
                        dve.wait_ge(pv_done, GH * g + m + 1)
                        dve.wait_ge(pt_ready, GH * g + m + 1)
                        dve.tensor_copy(pt[:, m % 2], ps_t[:, m % 2, 0:3 * P]).then_inc(pt_free, 1)
                    m = n - AHEAD - 2
                    if 0 <= m < GH and m % HC == HC - 1:
                        b, c, _ = seq(m)
                        dve.wait_ge(o_hi_done, GC * g + m // HC + 1)
                        dve.tensor_tensor(a_lo[:, c, b * S:(b + 1) * S], ps_o[:, m // HC % 2, 0:S],
                                          a_hi[:, c, b * S:(b + 1) * S].bitcast(F32), ALU.subtract).then_inc(o_free, 1)
                    if more and 0 <= n - GH < DC:
                        turned(g + 1, n - GH)
                if more:
                    queries(g + 1)
                dve.wait_ge(res_loaded, 16 * g + 16)
                for t in range(TILES):
                    if more:
                        values(g + 1, t)
                    dve.wait_ge(out_ready, DC * g + t + 1)
                    dve.tensor_tensor(res[:, t], ps_pj[:, t % 2], res[:, t], ALU.add).then_inc(out_added, 1)
                dve.wait_ge(out_added, DC + DC * g + DC)

            for c in range(DC):
                turned(0, c)
            dve.memset(v[:, 0:2], 0.0).then_inc(zeros, 1)
            queries(0)
            moments(dve, res, left_ln, left_step, 0, left_var_done)
            dve.wait_ge(left_rstd_done, 1)
            for t in range(TILES):
                dve.tensor_scalar(res[:, t], res[:, t], left_ln.mean[:, t:t + 1], left_ln.rstd[:, t:t + 1],
                                  ALU.subtract, ALU.mult).then_inc(left_ready, 1)
            dve.wait_ge(zeros, 1)
            dve.wait_ge(consts, CONSTS)
            for c in range(DC):
                values(0, c)
            attend(0, False, True)
            with dve.Fori(1, LAST) as g:
                attend(g, True, True)
            attend(LAST, True, False)

        @block.tensor
        def _(pe):
            pe.sem_inc(pv_done, BANKS)

            def turn(g, c):
                if c == 0:
                    pe.wait_ge(xt_loaded, 16 * g)
                if c >= BANKS:
                    pe.wait_ge(x_lo_done, DC * g + c - BANKS + 1)
                elif not (isinstance(g, int) and g == 0):
                    pe.wait_ge(out_added, DC * (g - 1) + c + BANKS + 1)
                for t in range(TILES):
                    mm = pe.transpose(ps_pj[:, c % 2, t * P:(t + 1) * P], xt[:, t, c * P:(c + 1) * P], ident[:])
                mm.then_inc(x_ready, 1)

            def query(g, c):
                pe.wait_ge(x_lo_done, DC * g + DC)
                if c >= BANKS:
                    pe.wait_ge(q_done, DC * g + c - BANKS + 1)
                for j in range(DC):
                    mm = three_pass(pe, ps_pj[:, c % 2], wq_hi[:, j, c * P:(c + 1) * P], wq_lo[:, j, c * P:(c + 1) * P],
                                    x_hi[:, j], x_lo[:, j], j == 0, j == DC - 1)
                mm.then_inc(q_ready, 1)

            def key(g, c):
                pe.wait_ge(c_lo_done, g + 1)
                if c >= BANKS:
                    pe.wait_ge(k_done, DC * g + c - BANKS + 1)
                else:
                    pe.wait_ge(max_done, GH * g + c + 1)
                three_pass(pe, ps_s[:, c % 2], wkv_hi[:, 0, c * P:(c + 1) * P], wkv_lo[:, 0, c * P:(c + 1) * P],
                           c_hi[:], c_lo[:], True, True).then_inc(k_ready, 1)

            def value(g, c):
                if c >= BANKS:
                    pe.wait_ge(v_done, DC * g + c - BANKS + 1)
                else:
                    pe.wait_ge(pt_free, GH * g + c + 1)
                three_pass(pe, ps_t[:, c % 2], c_hi[:, c * P:(c + 1) * P], c_lo[:, c * P:(c + 1) * P],
                           wkv_hi[:, 1], wkv_lo[:, 1], True, True).then_inc(v_ready, 1)

            def group(g, more):
                pe.wait_ge(q_done, DC * g + DC)
                pe.wait_ge(k_done, DC * g + DC)
                pe.wait_ge(v_done, DC * g + DC)
                for n in range(STEPS):
                    if n < GH:
                        b, c, h = seq(n)
                        pe.wait_ge(max_done, GH * g + n + 1)
                        for u in range(2):
                            qs = slice(b * S + u * P, b * S + (u + 1) * P)
                            ks = slice(b * S, b * S + (u + 1) * P)
                            mm = pe.matmul(ps_s[:, n % 2, u * P:(1 + 2 * u) * P], q[:, c, qs], k[:, c, h, ks],
                                           start=True, stop=True)
                        mm.then_inc(s_ready, 1)
                    m = n - AHEAD
                    if 0 <= m < GH:
                        pe.wait_ge(norm_done, GH * g + m + 1)
                        pe.wait_ge(pt_free, GH * g + m + 1)
                        for u in range(3):
                            mm = pe.transpose(ps_t[:, m % 2, u * P:(u + 1) * P], pr[:, m % HB, u * P:(u + 1) * P], ident[:])
                        mm.then_inc(pt_ready, 1)
                    m = n - AHEAD - 1
                    if 0 <= m < GH:
                        b, c, h = seq(m)
                        pe.wait_ge(pt_free, BANKS + GH * g + m + 1)
                        if h == 0:
                            pe.wait_ge(o_free, GC * g + m // HC + 1)
                        o = ps_o[:, m // HC % 2]
                        for u, out, keys in ((0, o[:, 0:S], slice(0, S)), (1, o[:, P:S], slice(S, 3 * P))):
                            mm = pe.matmul(out, v[:, b * GB + u, c, h], pt[:, m % 2, keys],
                                           start=h == 0 and u == 0, stop=h == HC - 1 and u == 1)
                        mm.then_inc(pv_done, 1)
                    if more and n >= GH:
                        if n - GH < DC:
                            turn(g + 1, n - GH)
                        else:
                            query(g + 1, n - GH - DC)
                if more:
                    for c in range(STEPS - GH - DC, DC):
                        query(g + 1, c)
                pe.wait_ge(o_free, BANKS + GC * g + GC)
                for t in range(TILES):
                    if t >= BANKS:
                        pe.wait_ge(out_added, DC + DC * g + t - BANKS + 1)
                    elif more:
                        pe.wait_ge(q_done, DC * (g + 1) + t + BANKS + 1)
                    for c in range(DC):
                        mm = three_pass(pe, ps_pj[:, t % 2], a_hi[:, c, t * P:(t + 1) * P], a_lo[:, c, t * P:(t + 1) * P],
                                        wo_hi[:, c], wo_lo[:, c], c == 0, c == DC - 1)
                    mm.then_inc(out_ready, 1)
                    if more:
                        key(g + 1, t)
                        value(g + 1, t)

            for c in range(DC):
                turn(0, c)
            for c in range(DC):
                query(0, c)
            for c in range(DC):
                key(0, c)
                value(0, c)
            with pe.Fori(0, LAST) as g:
                group(g, True)
            group(LAST, False)


E_N = 8
DE = 352
DS = 704
E_UNITS = (P, P, DE - 2 * P)
S_UNITS = DS // P + 1
HALF = DS - (S_UNITS - 1) * P
S_ROWS = [slice(0, P)] * (S_UNITS - 1) + [slice(P - HALF, P)]
SLOTS = 512
E_TILES = (2 * T + E_N * (SLOTS - 1)) // SLOTS
BLOCKS = SLOTS // P
NB = E_TILES * BLOCKS
NT = T // P
F16 = mybir.dt.float16


class Routing:

    def __init__(self, sb):
        self.token_of = sb("token_of", [P, NB], I32)
        self.slot = sb("slot", [P, 2, NT], I32)
        self.weight = sb("weight", [P, 2, NT])
        self.expert_of = sb("expert_of", [P, E_TILES], I32)


S_PARTS = DC + 4


class Shared:

    def __init__(self, sb, sem):
        U = S_UNITS
        self.gu_hi = sb("s_gu_hi", [P, DC, 2 * DS], F32R)
        self.gu_lo = sb("s_gu_lo", [P, DC, 2 * DS], F32R)
        self.dn_hi = sb("s_dn_hi", [P, U, D], F32R)
        self.dn_lo = sb("s_dn_lo", [P, U, D], F32R)
        self.x_ready = sem("s_x_ready")
        self.x_hi_done = sem("s_x_hi_done")
        self.x_lo_done = sem("s_x_lo_done")
        self.h_ready = sem("s_h_ready")
        self.silu_done = sem("s_silu_done")
        self.h_done = sem("s_h_done")
        self.h_hi_done = sem("s_h_hi_done")
        self.h_lo_done = sem("s_h_lo_done")
        self.out_done = sem("s_out_done")
        self.out_free = sem("s_out_free")

    def parts(self, w_gate_up, w_down):
        every = slice(0, P)
        out = [(self.gu_hi[:, c], self.gu_lo[:, c], every, 2 * DS, w_gate_up[:, c]) for c in range(DC)]
        for u in (0, 2):
            hi, lo = (w[:, u:u + 2].rearrange("p u n -> p (u n)") for w in (self.dn_hi, self.dn_lo))
            out.append((hi, lo, every, 2 * D, w_down[u * P:(u + 2) * P].rearrange("(u p) n -> p u n", u=2)))
        for u in (4, 5):
            rows = S_ROWS[u]
            out.append((self.dn_hi[rows, u], self.dn_lo[rows, u], rows, D, w_down[u * P:min((u + 1) * P, DS)]))
        return out

    def block(self, sb, psum):
        U = S_UNITS
        self.x_hi = sb("s_x_hi", [P, DC, GT], F32R)
        self.x_lo = sb("s_x_lo", [P, DC, GT], F32R)
        self.sg = sb("s_sg", [P, 2, GT])
        self.hf = sb("s_hf", [P, 2, GT])
        self.h_hi = sb("s_h_hi", [P, U, GT], F32R)
        self.h_lo = sb("s_h_lo", [P, U, GT], F32R)
        self.ps_x = psum("s_ps_x", [P, 2, GT], F32)
        self.ps_h = psum("s_ps_h", [P, 2, 2, GT], F32)
        self.ps_out = psum("s_ps_out", [P, 2, D], F32)

    BANKS = 2
    U = S_UNITS

    def begin(self, dve):
        dve.sem_inc(self.x_lo_done, self.BANKS)
        dve.sem_inc(self.out_free, self.BANKS)

    def turn(self, pe, xt, ident, n, c):
        pe.wait_ge(self.x_lo_done, DC * n + c + 1)
        for t in range(TILES):
            mm = pe.transpose(self.ps_x[:, c % 2, t * P:(t + 1) * P], xt[:, t, c * P:(c + 1) * P], ident[:])
        mm.then_inc(self.x_ready, 1)

    def x_round(self, act, n, c):
        act.wait_ge(self.x_ready, DC * n + c + 1)
        act.activation(self.x_hi[:, c], self.ps_x[:, c % 2], ACT.Copy).then_inc(self.x_hi_done, 1)

    def x_rest(self, dve, n, c):
        dve.wait_ge(self.x_hi_done, DC * n + c + 1)
        dve.tensor_tensor(self.x_lo[:, c], self.ps_x[:, c % 2], self.x_hi[:, c].bitcast(F32), ALU.subtract)\
            .then_inc(self.x_lo_done, 1)

    def hidden(self, pe, n, u, x_done=None):
        pe.wait_ge(self.h_done, self.U * n + max(0, u - 1))
        for s, column in ((0, u * P), (1, DS + HALF + u * P)):
            if s == 1 and u == self.U - 1:
                break
            at = slice(column, column + P)
            for c in range(DC):
                if x_done is not None and s == 0:
                    pe.wait_ge(self.x_lo_done, self.BANKS + DC * x_done + c + 1)
                mm = three_pass(pe, self.ps_h[:, u % 2, s], self.gu_hi[:, c, at], self.gu_lo[:, c, at],
                                self.x_hi[:, c], self.x_lo[:, c], c == 0, c == DC - 1)
        mm.then_inc(self.h_ready, 1)

    def gate(self, act, n, u):
        rows = S_ROWS[u]
        act.wait_ge(self.h_ready, self.U * n + u + 1)
        act.activation(self.sg[rows, u % 2], self.ps_h[0:rows.stop - rows.start, u % 2, 0], ACT.Silu)\
            .then_inc(self.silu_done, 1)
        act.wait_ge(self.h_done, self.U * n + u + 1)
        if u == 0:
            act.wait_ge(self.out_done, TILES * n)
        act.activation(self.h_hi[rows, u], self.hf[rows, u % 2], ACT.Copy).then_inc(self.h_hi_done, 1)

    def up(self, dve, n, u):
        rows = S_ROWS[u]
        dve.wait_ge(self.silu_done, self.U * n + u + 1)
        dve.wait_ge(self.h_lo_done, self.U * n + max(0, u - 1))
        dve.tensor_tensor(self.hf[rows, u % 2], self.ps_h[rows, u % 2, 0 if u == self.U - 1 else 1], self.sg[rows, u % 2],
                          ALU.mult).then_inc(self.h_done, 1)
        dve.wait_ge(self.h_hi_done, self.U * n + u + 1)
        dve.tensor_tensor(self.h_lo[rows, u], self.hf[rows, u % 2], self.h_hi[rows, u].bitcast(F32), ALU.subtract)\
            .then_inc(self.h_lo_done, 1)

    def down(self, pe, n, t):
        pe.wait_ge(self.out_free, TILES * n + t + 1)
        for u, rows in enumerate(S_ROWS):
            pe.wait_ge(self.h_lo_done, self.U * n + u + 1)
            mm = three_pass(pe, self.ps_out[:, t % 2], self.h_hi[rows, u, t * P:(t + 1) * P],
                            self.h_lo[rows, u, t * P:(t + 1) * P], self.dn_hi[rows, u], self.dn_lo[rows, u],
                            u == 0, u == self.U - 1)
        mm.then_inc(self.out_done, 1)

    def add(self, dve, res, n, t):
        dve.wait_ge(self.out_done, TILES * n + t + 1)
        dve.tensor_tensor(res[:, t], self.ps_out[:, t % 2], res[:, t], ALU.add).then_inc(self.out_free, 1)


def route(nc, x2_dram, w_router, sums, ln, ident, shared, w_gate_up, w_down, we_gate_up, we_down, raw, xg, x2_rows,
          kept, x_next, rt):
    with ExitStack() as ctx:
        def sb(name, shape, dt=F32):
            return ctx.enter_context(nc.sbuf_tensor("r_" + name, shape, dt))

        def sem(name):
            return ctx.enter_context(nc.semaphore("r_" + name))

        xt = (x_next, sb("xt", [P, TILES, D]))
        before = sb("before", [P, P])
        ones = sb("ones", [P, P])
        w_raw = sb("w_raw", [P, DC, E_N])
        w_hi = sb("w_hi", [P, DC, P], F32R)
        w_lo = sb("w_lo", [P, DC, P], F32R)
        lg_t = sb("lg_t", [E_N, T])
        int_a = sb("int_a", [P, P], I32)
        rank8 = sb("rank8", [P, NT, E_N])
        col128 = sb("col128", [P, P])
        col_nb = sb("col_nb", [P, NB])
        token = sb("token", [P, NT])
        tile_no = sb("tile_no", [P, E_TILES, E_N])
        keep = sb("keep", [P, E_N, NT])
        unit = sb("unit", [P, E_N])
        lg = sb("lg", [P, NT, E_N])
        pr = sb("pr", [P, NT, E_N])
        top = sb("top", [P, NT])
        rsum = sb("rsum", [P, NT])
        cand = sb("cand", [P, NT, E_N])
        best = sb("best", [P, NT])
        pick = sb("pick", [P, 2, NT, E_N])
        both = sb("both", [P, NT, E_N])
        tot = sb("tot", [P, E_N, NT])
        run = sb("run", [P, E_N, NT])
        tiles_f = sb("tiles_f", [P, E_N])
        tiles_i = sb("tiles_i", [P, E_N], I32)
        ends = sb("ends", [P, E_N])
        base = sb("base", [P, E_N])
        pos = sb("pos", [P, NT, E_N])
        cmp = sb("cmp", [P, E_TILES, E_N])
        ex_f = sb("ex_f", [P, E_TILES])
        slot_f = sb("slot_f", [P, 2, NT])
        part_i = sb("part_i", [P, 2, 2, NT], I32)
        part_f = sb("part_f", [P, 2, 2, NT])
        hot_lo = sb("hot_lo", [P, 2 * NT, P], F16)
        hot_hi = sb("hot_hi", [P, 2 * NT, NB], F16)
        shared.block(sb, lambda name, shape, dt: ctx.enter_context(nc.psum_tensor("r_" + name, shape, dt)))
        ps_l = shared.ps_out
        ps_r = shared.ps_x[:, 1]
        each_e = NT * E_N
        ps_logits, ps_prior, ps_total = (ps_r[:, k * each_e:(k + 1) * each_e] for k in range(3))
        ps_token = ps_r[:, 3 * each_e:3 * each_e + NB]
        parts = shared.parts(w_gate_up, w_down)
        w_part = raw[0].rearrange("p c n -> p (c n)").rearrange("p (b n) -> p b n", b=2)

        consts = sem("consts")
        iotas = sem("iotas")
        loaded = [sem("loaded_even"), sem("loaded_odd")]
        w_loaded = sem("w_loaded")
        w_hi_done = sem("w_hi_done")
        w_lo_done = sem("w_lo_done")
        part_loaded = [sem("part_loaded_even"), sem("part_loaded_odd")]
        part_hi_done = sem("part_hi_done")
        part_lo_done = sem("part_lo_done")
        ln_step = sem("ln_step")
        var_done = sem("var_done")
        rstd_done = sem("rstd_done")
        x2_ready = sem("x2_ready")
        x2_stored = sem("x2_stored")
        padded = sem("padded")
        expert_known = sem("expert_known")
        expert_loaded = sem("expert_loaded")
        token_known = sem("token_known")
        x_gathered = sem("x_gathered")
        lg_chunk = sem("lg_chunk")
        lg_read = sem("lg_read")
        turned = sem("turned")
        sub_done = sem("sub_done")
        exp_done = sem("exp_done")
        both_done = sem("both_done")
        counted = sem("counted")
        hot_done = sem("hot_done")
        placed = sem("placed")
        step = sem("step")

        CONSTS = 8
        PARTS_AT = {(1, 1): 0, (1, 3): 1, (3, 0): 2, (3, 2): 3}
        LAST = GROUPS - 1

        block = ctx.enter_context(nc.Block())

        @block.sync
        def _(sp):
            def load(g):
                sp.dma_start(xt[g % 2][:], x2_dram[g]).then_inc(loaded[g % 2], 16)

            def load_part(k):
                if k >= 2:
                    sp.wait_ge(part_lo_done, k - 1)
                _, _, rows, cols, src = parts[k]
                dst = w_part[rows, k % 2, 0:cols]
                if cols == 2 * D:
                    dst = dst.rearrange("p (u n) -> p u n", u=2)
                sp.dma_start(dst, src).then_inc(part_loaded[k % 2], 16)

            sp.dma_start(w_raw[:], w_router).then_inc(w_loaded, 16)
            load(1)
            load_part(0)
            load_part(1)
            sp.wait_ge(x2_ready, TILES)
            sp.dma_start(x2_dram[LAST], kept[:]).then_inc(x2_stored, 16)
            for g in range(2, GROUPS):
                sp.wait_ge(shared.x_ready, DC * (g - 1))
                if g == LAST:
                    sp.wait_ge(x2_stored, 16)
                load(g)
            for k in range(2, S_PARTS):
                load_part(k)
            sp.wait_ge(part_lo_done, S_PARTS)
            sp.wait_ge(padded, 1)
            sp.wait_ge(expert_known, 1)
            e = sp.value_load(rt.expert_of[0:1, 0:1], min_val=0, max_val=E_N - 1)
            load_expert(sp, e, we_gate_up, we_down, raw, expert_loaded, expert_loaded)
            sp.wait_ge(expert_loaded, 48)

        @block.gpsimd
        def _(pool):
            pool.memset(before[:], 1.0).then_inc(consts, 1)
            pool.memset(ones[:], 1.0).then_inc(consts, 1)
            pool.memset(w_hi[:].bitcast(F32), 0.0).then_inc(consts, 1)
            pool.memset(w_lo[:].bitcast(F32), 0.0).then_inc(consts, 1)
            pool.memset(keep[:], 1.0).then_inc(consts, 1)
            pool.memset(unit[:], 1.0).then_inc(consts, 1)
            pool.wait_ge(var_done, 1)
            pool.tensor_tensor(ln.rstd[:], ln.var[:], ln.power[:], ALU.pow).then_inc(rstd_done, 1)
            pool.wait_ge(consts, 6)
            pool.affine_select(out=before[:], in_=before[:], compare_op=ALU.is_gt, fill=0.0, base=0,
                               pattern=[[1, P]], channel_multiplier=-1).then_inc(consts, 1)
            pool.memset(keep[:, :, 0:1], 0.0).then_inc(consts, 1)
            n = 0
            for out, pattern, start, mult in (
                (rank8[:], [[0, NT], [-1, E_N]], E_N, 0),
                (col128[:], [[1, P]], 0, 0),
                (col_nb[:], [[1, NB]], 0, 0),
                (token[:], [[P, NT]], 0, 1),
                (tile_no[:], [[1, E_TILES], [0, E_N]], 0, 0),
            ):
                size = 1
                for _, k in pattern:
                    size *= k
                if n:
                    pool.wait_ge(iotas, n)
                pool.iota(int_a[:, 0:size], pattern=pattern, base=start, channel_multiplier=mult).then_inc(iotas, 1)
                pool.wait_ge(iotas, n + 1)
                flat = out if len(out.shape) == 2 else out.rearrange("p a b -> p (a b)")
                pool.tensor_copy(flat, int_a[:, 0:size]).then_inc(iotas, 1)
                n += 2
            for k, (hi, lo, rows, cols, _) in enumerate(parts):
                pool.wait_ge(part_hi_done, k + 1)
                if rows.start:
                    pool.wait_ge(part_lo_done, k)
                pool.tensor_tensor(lo, w_part[rows, k % 2, 0:cols], hi.bitcast(F32), ALU.subtract).then_inc(part_lo_done, 1)
            pool.wait_ge(token_known, 1)
            for b in range(BLOCKS):
                pool.indirect_dma_start(xg[:, b], None, x2_rows,
                                        bass.IndirectOffsetOnAxis(ap=rt.token_of[:, b:b + 1], axis=0)).then_inc(x_gathered, 16)
            pool.wait_ge(x_gathered, 16 * BLOCKS)

        @block.scalar
        def _(act):
            act.preload_act_table_set("exp_and_others")

            def split_part(k):
                hi, _, rows, cols, _ = parts[k]
                act.wait_ge(part_loaded[k % 2], 16 * (k // 2) + 16)
                act.activation(hi, w_part[rows, k % 2, 0:cols], ACT.Copy).then_inc(part_hi_done, 1)

            for g in range(GROUPS):
                for c in range(DC):
                    if g:
                        act.wait_ge(lg_chunk, DC * (g - 1) + c + 1)
                    shared.x_round(act, g, c)
                    if g == 0 and c == 2:
                        act.wait_ge(w_loaded, 16)
                        act.wait_ge(consts, CONSTS)
                        act.activation(w_hi[:, :, 0:E_N], w_raw[:], ACT.Copy).then_inc(w_hi_done, 1)
                    if g and c == 1:
                        act.wait_ge(lg_chunk, DC * g)
                        act.activation(lg_t[:, (g - 1) * GT:g * GT], ps_l[0:E_N, (g - 1) % 2], ACT.Copy).then_inc(lg_read, 1)
                    if (g, c) in PARTS_AT:
                        split_part(PARTS_AT[g, c])
            act.wait_ge(lg_chunk, DC * GROUPS)
            act.activation(lg_t[:, LAST * GT:T], ps_l[0:E_N, LAST % 2], ACT.Copy).then_inc(lg_read, 1)
            act.wait_ge(sub_done, 1)
            act.activation(pr[:], lg[:], ACT.Exp).then_inc(exp_done, 1)
            for u in range(Shared.U):
                shared.gate(act, 0, u)
                if DC + u < S_PARTS:
                    split_part(DC + u)

        @block.vector
        def _(dve):
            steps = [0]

            def link(ins):
                steps[0] += 1
                ins.then_inc(step, 1)
                dve.wait_ge(step, steps[0])

            shared.begin(dve)
            for k in range(TILES):
                moments_step(dve, sums, ln, k, ln_step, 0, var_done)
            for k in range(TILES, TILES + 3):
                moments_step(dve, sums, ln, k, ln_step, 0, var_done)
                shared.x_rest(dve, 0, k - TILES)
            dve.wait_ge(rstd_done, 1)
            for t in range(TILES):
                dve.tensor_scalar(kept[:, t], sums[:, t], ln.mean[:, t:t + 1], ln.rstd[:, t:t + 1],
                                  ALU.subtract, ALU.mult).then_inc(x2_ready, 1)
            dve.wait_ge(w_hi_done, 1)
            dve.tensor_tensor(w_lo[:, :, 0:E_N], w_raw[:], w_hi[:, :, 0:E_N].bitcast(F32), ALU.subtract)\
                .then_inc(w_lo_done, 1)
            shared.x_rest(dve, 0, DC - 1)
            dve.memset(raw[1][E_UNITS[2]:P, 2], 0.0).then_inc(padded, 1)
            with dve.Fori(1, GROUPS) as g:
                for c in range(DC):
                    shared.x_rest(dve, g, c)

            def each(row):
                return row.rearrange("p (t o) -> p t o", o=1).broadcast_to([P, NT, E_N])

            dve.wait_ge(iotas, 10)
            dve.wait_ge(turned, 1)
            logits = ps_logits.rearrange("p (t e) -> p t e", e=E_N)
            link(dve.tensor_reduce(top[:], logits, AX_X, ALU.max))
            dve.tensor_tensor(lg[:], logits, each(top[:]), ALU.subtract).then_inc(sub_done, 1)
            dve.wait_ge(exp_done, 1)
            link(dve.tensor_reduce(rsum[:], pr[:], AX_X, ALU.add))
            link(dve.reciprocal(rsum[:], rsum[:]))
            link(dve.tensor_tensor(pr[:], pr[:], each(rsum[:]), ALU.mult))
            shared.up(dve, 0, 0)
            for k in range(2):
                w = rt.weight[:, k]
                link(dve.tensor_reduce(w, pr[:], AX_X, ALU.max))
                link(dve.tensor_tensor(cand[:], pr[:], each(w), ALU.is_equal))
                link(dve.tensor_tensor(cand[:], cand[:], rank8[:], ALU.mult))
                link(dve.tensor_reduce(best[:], cand[:], AX_X, ALU.max))
                link(dve.tensor_tensor(pick[:, k], cand[:], each(best[:]), ALU.is_equal))
                if k == 0:
                    link(dve.scalar_tensor_tensor(pr[:], pick[:, 0], -4.0, pr[:], ALU.mult, ALU.add))
            dve.tensor_tensor(both[:], pick[:, 0], pick[:, 1], ALU.add).then_inc(both_done, 1)
            shared.up(dve, 0, 1)
            shared.up(dve, 0, 2)
            dve.wait_ge(counted, 1)
            prior = ps_prior.rearrange("p (t e) -> p t e", e=E_N)
            total = ps_total.rearrange("p (t e) -> p e t", e=E_N)
            link(dve.tensor_copy(tot[:], total))
            link(dve.tensor_tensor_scan(run[:].rearrange("p e t -> p (e t)"), keep[:].rearrange("p e t -> p (e t)"),
                                        tot[:].rearrange("p e t -> p (e t)"), 0.0, ALU.mult, ALU.add))
            link(dve.tensor_scalar(tiles_i[:], run[:, :, NT - 1], float(SLOTS - 1), None, ALU.add))
            link(dve.tensor_scalar(tiles_i[:], tiles_i[:], SLOTS.bit_length() - 1, None, ALU.logical_shift_right))
            link(dve.tensor_copy(tiles_f[:], tiles_i[:]))
            link(dve.tensor_tensor_scan(ends[:], unit[:], tiles_f[:], 0.0, ALU.mult, ALU.add))
            link(dve.tensor_tensor(base[:], ends[:], tiles_f[:], ALU.subtract))
            link(dve.tensor_scalar(base[:], base[:], float(SLOTS), None, ALU.mult))
            link(dve.tensor_tensor(cmp[:], tile_no[:],
                                   ends[:].rearrange("p (o e) -> p o e", o=1).broadcast_to([P, E_TILES, E_N]), ALU.is_ge))
            link(dve.tensor_reduce(ex_f[:], cmp[:], AX_X, ALU.add))
            dve.tensor_scalar(rt.expert_of[:], ex_f[:], float(E_N - 1), None, ALU.min).then_inc(expert_known, 1)
            link(dve.tensor_tensor(tot[:], run[:], tot[:], ALU.subtract))
            link(dve.tensor_tensor(tot[:], tot[:], base[:].rearrange("p (e o) -> p e o", o=1).broadcast_to([P, E_N, NT]),
                                   ALU.add))
            link(dve.tensor_tensor(pos[:], prior, tot[:].rearrange("p e t -> p t e"), ALU.add))
            for k in range(2):
                link(dve.tensor_tensor(cand[:], pos[:], pick[:, k], ALU.mult))
                link(dve.tensor_reduce(slot_f[:, k], cand[:], AX_X, ALU.add))
            shared.up(dve, 0, 3)
            link(dve.tensor_copy(rt.slot[:], slot_f[:]))
            link(dve.tensor_scalar(part_i[:, 0], rt.slot[:], P.bit_length() - 1, None, ALU.logical_shift_right))
            link(dve.tensor_scalar(part_i[:, 1], rt.slot[:], P - 1, None, ALU.bitwise_and))
            link(dve.tensor_copy(part_f[:], part_i[:]))
            def spread(x, n):
                return x.rearrange("p k t -> p (k t)").rearrange("p (a o) -> p a o", o=1).broadcast_to([P, 2 * NT, n])

            def repeat(x, n):
                return x.rearrange("p (o n) -> p o n", o=1).broadcast_to([P, 2 * NT, n])

            link(dve.tensor_tensor(hot_lo[:], repeat(col128[:], P), spread(part_f[:, 1], P), ALU.is_equal))
            shared.up(dve, 0, 4)
            shared.up(dve, 0, 5)
            link(dve.tensor_tensor(hot_hi[:], repeat(col_nb[:], NB), spread(part_f[:, 0], NB), ALU.is_equal))
            for k in range(2):
                rows = hot_hi[:, k * NT:(k + 1) * NT]
                ins = dve.tensor_tensor(rows, rows, token[:].rearrange("p (t o) -> p t o", o=1).broadcast_to([P, NT, NB]),
                                        ALU.mult).then_inc(hot_done, 1)
            dve.wait_ge(x2_stored, 16)
            for t in range(TILES - 1):
                shared.add(dve, kept, 0, t)
            dve.wait_ge(placed, 1)
            dve.tensor_copy(rt.token_of[:], ps_token).then_inc(token_known, 1)
            shared.add(dve, kept, 0, TILES - 1)

        @block.tensor
        def _(pe):
            def turn(n):
                g, c = n // DC, n % DC
                if g and c == 0:
                    pe.wait_ge(loaded[g % 2], 16 * ((g + 1) // 2))
                shared.turn(pe, xt[g % 2], ident, g, c)

            turn(0)
            turn(1)
            for n in range(DC * GROUPS):
                g, c = n // DC, n % DC
                if n + 2 < DC * GROUPS:
                    turn(n + 2)
                pe.wait_ge(shared.x_lo_done, Shared.BANKS + n + 1)
                if n == 0:
                    pe.wait_ge(w_lo_done, 1)
                if c == 0 and g >= 2:
                    pe.wait_ge(lg_read, g - 1)
                three_pass(pe, ps_l[:, g % 2], w_hi[:, c], w_lo[:, c], shared.x_hi[:, c], shared.x_lo[:, c],
                           c == 0, c == DC - 1).then_inc(lg_chunk, 1)
            pe.wait_ge(lg_read, GROUPS)
            for t in range(NT):
                mm = pe.transpose(ps_logits[:, t * E_N:(t + 1) * E_N], lg_t[:, t * P:(t + 1) * P], ident[0:E_N, 0:E_N])
            mm.then_inc(turned, 1)
            pe.wait_ge(part_lo_done, DC)
            for u in range(Shared.U):
                shared.hidden(pe, 0, u)
                if u == 2:
                    pe.wait_ge(both_done, 1)
                    rows = both[:].rearrange("p t e -> p (t e)")
                    pe.wait_ge(consts, CONSTS)
                    pe.matmul(ps_prior, before[:], rows, start=True, stop=True)
                    pe.matmul(ps_total, ones[:], rows, start=True, stop=True).then_inc(counted, 1)
            pe.wait_ge(part_lo_done, S_PARTS)
            for t in range(TILES):
                if t == TILES - 1:
                    pe.wait_ge(hot_done, 2)
                    for n in range(2 * NT):
                        mm = pe.matmul(ps_token, hot_lo[:, n], hot_hi[:, n], start=n == 0, stop=n == 2 * NT - 1)
                    mm.then_inc(placed, 1)
                shared.down(pe, 0, t)


def load_expert(sp, e, w_gate_up, w_down, raw, gu_loaded, dn_loaded):
    sp.dma_start(raw[0], w_gate_up[bass.ds(e, 1)].rearrange("o p c n -> p (o c) n")).then_inc(gu_loaded, 16)
    load_down(sp, e, w_down, raw, dn_loaded)


def load_down(sp, e, w_down, raw, dn_loaded):
    rows = w_down[bass.ds(e, 1)].rearrange("o h n -> (o h) n")
    sp.dma_start(raw[1][:, 0:2], rows[0:2 * P].rearrange("(u p) n -> p u n", p=P)).then_inc(dn_loaded, 16)
    sp.dma_start(raw[1][0:E_UNITS[2], 2], rows[2 * P:DE]).then_inc(dn_loaded, 16)


def experts(nc, x2_rows, w_gate_up, w_down, y_dram, ident, raw, xg, x2_first, x2_next, y, y_stored, rt):
    with ExitStack() as ctx:
        def sb(name, shape, dt=F32):
            return ctx.enter_context(nc.sbuf_tensor("e_" + name, shape, dt))

        def sem(name):
            return ctx.enter_context(nc.semaphore("e_" + name))

        U = len(E_UNITS)
        gu_raw, dn_raw = raw
        gu_hi = sb("gu_hi", [P, DC, 2 * DE], F32R)
        gu_lo = sb("gu_lo", [P, DC, 2 * DE], F32R)
        dn_hi = sb("dn_hi", [P, U, D], F32R)
        dn_lo = sb("dn_lo", [P, U, D], F32R)
        index = sb("index", [P, BLOCKS], I32)
        carrier = sb("carrier", [P, 1])
        x_hi = sb("x_hi", [P, DC, SLOTS], F32R)
        x_lo = sb("x_lo", [P, DC, SLOTS], F32R)
        sg = sb("sg", [P, 2, SLOTS])
        hf = sb("hf", [P, 2, SLOTS])
        h_hi = sb("h_hi", [P, U, SLOTS], F32R)
        h_lo = sb("h_lo", [P, U, SLOTS], F32R)
        ps_h = ctx.enter_context(nc.psum_tensor("e_ps_h", [P, 2, 2, SLOTS], F32))
        ps_x = ctx.enter_context(nc.psum_tensor("e_ps_x", [P, 2, 512], F32))
        ps_y = ctx.enter_context(nc.psum_tensor("e_ps_y", [P, 2, D], F32))

        gu_loaded = sem("gu_loaded")
        dn_loaded = sem("dn_loaded")
        gu_hi_done = sem("gu_hi_done")
        gu_lo_done = sem("gu_lo_done")
        dn_hi_done = sem("dn_hi_done")
        dn_lo_done = sem("dn_lo_done")
        indexed = sem("indexed")
        carried = sem("carried")
        x_gathered = sem("x_gathered")
        x2_loaded = sem("x2_loaded")
        x_ready = sem("x_ready")
        x_hi_done = sem("x_hi_done")
        x_lo_done = sem("x_lo_done")
        h_ready = sem("h_ready")
        silu_done = sem("silu_done")
        h_done = sem("h_done")
        h_hi_done = sem("h_hi_done")
        h_lo_done = sem("h_lo_done")
        y_ready = sem("y_ready")
        y_read = sem("y_read")

        BANKS = 2
        LAST = E_TILES - 1
        y_tiles = y_dram.rearrange("(i b p) d -> i p b d", b=BLOCKS, p=P)

        block = ctx.enter_context(nc.Block())

        @block.sync
        def _(sp):
            def load(i):
                e = sp.value_load(rt.expert_of[0:1, bass.ds(i, 1)], min_val=0, max_val=E_N - 1)
                sp.wait_ge(gu_lo_done, DC * i)
                sp.dma_start(gu_raw, w_gate_up[bass.ds(e, 1)].rearrange("o p c n -> p (o c) n")).then_inc(gu_loaded, 16)
                sp.wait_ge(dn_lo_done, i)
                load_down(sp, e, w_down, raw, dn_loaded)

            sp.dma_start(x2_next, x2_first).then_inc(x2_loaded, 16)
            with sp.Fori(0, LAST) as i:
                load(i + 1)
                sp.wait_ge(y_read, BANKS + BLOCKS * i + BLOCKS)
                sp.dma_start(y_tiles[bass.ds(i, 1)].rearrange("o p b d -> p (o b) d"), y[:]).then_inc(y_stored, 16)
            sp.wait_ge(y_read, BANKS + BLOCKS * E_TILES)
            sp.dma_start(y_tiles[LAST], y[:]).then_inc(y_stored, 16)
            sp.wait_ge(x2_loaded, 16)

        @block.gpsimd
        def _(pool):

            pool.memset(carrier[:], 0.0).then_inc(carried, 1)

            def gather(i):
                pool.wait_ge(x_ready, DC * i)
                pool.wait_ge(carried, i)
                pool.tensor_copy(index[:], rt.token_of[:, bass.ds(BLOCKS * i, BLOCKS)]).then_inc(indexed, 1)
                pool.wait_ge(indexed, i)
                pool.tensor_tensor(carrier[:], carrier[:], carrier[:], ALU.add).then_inc(carried, 1)
                for b in range(BLOCKS):
                    pool.indirect_dma_start(xg[:, b], None, x2_rows,
                                            bass.IndirectOffsetOnAxis(ap=index[:, b:b + 1], axis=0)).then_inc(x_gathered, 16)

            def split_down(i):
                pool.wait_ge(dn_hi_done, i + 1)
                pool.tensor_tensor(dn_lo[:], dn_raw, dn_hi[:].bitcast(F32), ALU.subtract).then_inc(dn_lo_done, 1)

            with pool.Fori(0, LAST) as i:
                gather(i + 1)
                split_down(i)
            split_down(LAST)

        @block.scalar
        def _(act):
            act.preload_act_table_set("silu_and_others")

            def split_x(i, c):
                act.wait_ge(x_ready, DC * i + c + 1)
                act.activation(x_hi[:, c], ps_x[:, c % 2], ACT.Copy).then_inc(x_hi_done, 1)

            def split_gate_up(i, c):
                if c == 0:
                    act.wait_ge(gu_loaded, 16 * i)
                    act.wait_ge(h_ready, U * i)
                act.activation(gu_hi[:, c], gu_raw[:, c], ACT.Copy).then_inc(gu_hi_done, 1)

            def split_x_and_gate_up(i):
                split_x(i, 0)
                split_x(i, 1)
                split_gate_up(i, 0)
                split_x(i, 2)
                split_gate_up(i, 1)
                split_x(i, 3)
                split_gate_up(i, 2)
                split_gate_up(i, 3)

            def split_down(i):
                act.wait_ge(dn_loaded, 32 * i)
                act.wait_ge(y_ready, BLOCKS * i)
                act.activation(dn_hi[:], dn_raw, ACT.Copy).then_inc(dn_hi_done, 1)

            def hidden(i):
                for u, n in enumerate(E_UNITS):
                    act.wait_ge(h_ready, U * i + u + 1)
                    act.activation(sg[0:n, u % 2], ps_h[0:n, u % 2, 0], ACT.Silu).then_inc(silu_done, 1)
                    if u == 0:
                        split_down(i)
                    act.wait_ge(h_done, U * i + u + 1)
                    act.activation(h_hi[0:n, u], hf[0:n, u % 2], ACT.Copy).then_inc(h_hi_done, 1)

            split_x_and_gate_up(0)
            with act.Fori(0, LAST) as i:
                hidden(i)
                split_x_and_gate_up(i + 1)
            hidden(LAST)

        @block.vector
        def _(dve):
            dve.sem_inc(x_lo_done, BANKS)
            dve.sem_inc(y_read, BANKS)

            def split_x(i, c):
                dve.wait_ge(x_hi_done, DC * i + c + 1)
                dve.tensor_tensor(x_lo[:, c], ps_x[:, c % 2], x_hi[:, c].bitcast(F32), ALU.subtract)\
                    .then_inc(x_lo_done, 1)

            def split_gate_up(i, c):
                dve.wait_ge(gu_hi_done, DC * i + c + 1)
                dve.tensor_tensor(gu_lo[:, c], gu_raw[:, c], gu_hi[:, c].bitcast(F32), ALU.subtract)\
                    .then_inc(gu_lo_done, 1)

            def hidden(i):
                for u, n in enumerate(E_UNITS):
                    dve.wait_ge(silu_done, U * i + u + 1)
                    dve.wait_ge(h_lo_done, U * i + max(0, u - 1))
                    dve.tensor_tensor(hf[0:n, u % 2], ps_h[0:n, u % 2, 1], sg[0:n, u % 2], ALU.mult).then_inc(h_done, 1)
                    dve.wait_ge(h_hi_done, U * i + u + 1)
                    dve.tensor_tensor(h_lo[0:n, u], hf[0:n, u % 2], h_hi[0:n, u].bitcast(F32), ALU.subtract)\
                        .then_inc(h_lo_done, 1)

            def output(i, b):
                dve.wait_ge(y_ready, BLOCKS * i + b + 1)
                if b == 0:
                    dve.wait_ge(y_stored, 16 * i)
                dve.tensor_copy(y[:, b], ps_y[:, b % 2]).then_inc(y_read, 1)

            for c in range(DC):
                split_x(0, c)
            for c in range(DC):
                split_gate_up(0, c)
            with dve.Fori(0, LAST) as i:
                hidden(i)
                split_x(i + 1, 0)
                split_x(i + 1, 1)
                output(i, 0)
                output(i, 1)
                split_gate_up(i + 1, 0)
                split_x(i + 1, 2)
                split_gate_up(i + 1, 1)
                output(i, 2)
                split_x(i + 1, 3)
                split_gate_up(i + 1, 2)
                split_gate_up(i + 1, 3)
                output(i, 3)
            hidden(LAST)
            for b in range(BLOCKS):
                output(LAST, b)

        @block.tensor
        def _(pe):
            def turn(i, c):
                if c == 0:
                    pe.wait_ge(x_gathered, 16 * BLOCKS * i)
                pe.wait_ge(x_lo_done, DC * i + c + 1)
                for b in range(BLOCKS):
                    mm = pe.transpose(ps_x[:, c % 2, b * P:(b + 1) * P], xg[:, b, c * P:(c + 1) * P], ident[:])
                mm.then_inc(x_ready, 1)

            def hidden(i, u):
                n = E_UNITS[u]
                pe.wait_ge(h_done, U * i + max(0, u - 1))
                for s in range(2):
                    at = slice(s * DE + u * P, s * DE + u * P + n)
                    for c in range(DC):
                        if u == 0 and s == 0:
                            pe.wait_ge(x_lo_done, BANKS + DC * i + c + 1)
                            pe.wait_ge(gu_lo_done, DC * i + c + 1)
                        mm = three_pass(pe, ps_h[0:n, u % 2, s], gu_hi[:, c, at], gu_lo[:, c, at], x_hi[:, c], x_lo[:, c],
                                        c == 0, c == DC - 1)
                mm.then_inc(h_ready, 1)

            def down(i, b, units):
                for u in units:
                    n = E_UNITS[u]
                    if b == 0:
                        if u == 0:
                            pe.wait_ge(dn_lo_done, i + 1)
                        pe.wait_ge(h_lo_done, U * i + u + 1)
                    if u == 0:
                        pe.wait_ge(y_read, BLOCKS * i + b + 1)
                    mm = three_pass(pe, ps_y[:, b % 2], h_hi[0:n, u, b * P:(b + 1) * P], h_lo[0:n, u, b * P:(b + 1) * P],
                                    dn_hi[0:n, u], dn_lo[0:n, u], u == 0, u == U - 1)
                    if u == U - 1:
                        mm.then_inc(y_ready, 1)

            def tile(i, more):
                hidden(i, 0)
                hidden(i, 1)
                if more:
                    turn(i + 1, 0)
                    turn(i + 1, 1)
                hidden(i, 2)
                down(i, 0, (0, 1))
                down(i, 1, (0, 1))
                down(i, 0, (2,))
                down(i, 1, (2,))
                if more:
                    turn(i + 1, 2)
                down(i, 2, range(U))
                if more:
                    turn(i + 1, 3)
                down(i, 3, range(U))

            for c in range(DC):
                turn(0, c)
            with pe.Fori(0, LAST) as i:
                tile(i, True)
            tile(LAST, False)


def combine(nc, x2_tiles, y_dram, out_tiles, ident, shared, kept, xt, y_stored, rt):
    with ExitStack() as ctx:
        def sb(name, shape, dt=F32):
            return ctx.enter_context(nc.sbuf_tensor("c_" + name, shape, dt))

        def sem(name):
            return ctx.enter_context(nc.semaphore("c_" + name))

        res = sb("res", [P, TILES, D])
        y = sb("y", [P, 2, TILES, D])
        y_kept = sb("y_kept", [P, 2, TILES, D])
        index = sb("index", [P, 2, TILES], I32)
        carrier = sb("carrier", [P, 1])
        ln = Moments(sb, "ln", TILES)
        ln_kept = Moments(sb, "kept", TILES)
        shared.block(sb, lambda name, shape, dt: ctx.enter_context(nc.psum_tensor("c_" + name, shape, dt)))

        ln_const = sem("ln_const")
        xt_loaded = sem("xt_loaded")
        res_loaded = sem("res_loaded")
        indexed = sem("indexed")
        carried = sem("carried")
        y_gathered = sem("y_gathered")
        y_kept_gathered = sem("y_kept_gathered")
        add_step = sem("add_step")
        y_read = sem("y_read")
        kept_step = sem("kept_step")
        ln_step = sem("ln_step")
        var_done = sem("var_done")
        rstd_done = sem("rstd_done")
        out_ready = sem("out_ready")
        out_stored = sem("out_stored")
        kept_ln_step = sem("kept_ln_step")
        kept_var_done = sem("kept_var_done")
        kept_rstd_done = sem("kept_rstd_done")
        kept_ready = sem("kept_ready")
        kept_stored = sem("kept_stored")

        KEPT = GROUPS - 1
        TURNED = GROUPS
        DONE = 1
        LAST = KEPT - 1

        block = ctx.enter_context(nc.Block())

        @block.sync
        def _(sp):
            def tiles(dram, g):
                return dram[g] if isinstance(g, int) else dram[bass.ds(g, 1)].rearrange("o p t d -> p (o t) d")

            with sp.Fori(0, LAST) as g:
                sp.wait_ge(out_stored, 16 * g)
                sp.dma_start(res[:], tiles(x2_tiles, g)).then_inc(res_loaded, 16)
                sp.wait_ge(shared.x_ready, DC * (TURNED + g) + DC)
                sp.dma_start(xt[:], tiles(x2_tiles, g + 1)).then_inc(xt_loaded, 16)
                sp.wait_ge(out_ready, TILES * g + TILES)
                sp.dma_start(tiles(out_tiles, g), res[:]).then_inc(out_stored, 16)
            sp.wait_ge(out_stored, 16 * LAST)
            sp.dma_start(res[:], x2_tiles[LAST]).then_inc(res_loaded, 16)
            sp.wait_ge(kept_ready, TILES)
            sp.dma_start(out_tiles[KEPT], kept[:]).then_inc(kept_stored, 16)
            for t in range(TILES):
                sp.wait_ge(out_ready, TILES * LAST + t + 1)
                sp.dma_start(out_tiles[LAST][:, t], res[:, t]).then_inc(out_stored, 16)
            sp.wait_ge(kept_stored, 16)
            sp.wait_ge(out_stored, 16 * (LAST + TILES))

        @block.gpsimd
        def _(pool):
            def gather(n, into, done):
                if isinstance(n, int):
                    first = (KEPT if n == 0 else 0) * TILES
                    slots = rt.slot[:, :, first:first + TILES]
                else:
                    slots = rt.slot[:, :, bass.ds(TILES * (n - 1), TILES)]
                    pool.wait_ge(y_read, TILES * (n - 1))
                pool.wait_ge(carried, n + 1)
                pool.tensor_copy(index[:], slots).then_inc(indexed, 1)
                pool.wait_ge(indexed, n + 1)
                pool.tensor_tensor(carrier[:], carrier[:], carrier[:], ALU.add).then_inc(carried, 1)
                for t in range(TILES):
                    for k in range(2):
                        pool.indirect_dma_start(into[:, k, t], None, y_dram,
                                                bass.IndirectOffsetOnAxis(ap=index[:, k, t:t + 1], axis=0)).then_inc(done, 16)

            pool.memset(ln.power[:], -0.5).then_inc(ln_const, 1)
            pool.memset(ln_kept.power[:], -0.5).then_inc(ln_const, 1)
            pool.memset(carrier[:], 0.0).then_inc(carried, 1)
            pool.wait_ge(ln_const, 2)
            pool.wait_ge(y_stored, 16 * E_TILES)
            gather(0, y_kept, y_kept_gathered)
            pool.wait_ge(y_kept_gathered, 2 * TILES * 16)

            def root(g):
                pool.wait_ge(var_done, g + 1)
                pool.tensor_tensor(ln.rstd[:], ln.var[:], ln.power[:], ALU.pow).then_inc(rstd_done, 1)

            gather(1, y, y_gathered)
            with pool.Fori(0, LAST) as g:
                root(g)
                gather(g + 2, y, y_gathered)
            pool.wait_ge(kept_var_done, 1)
            pool.tensor_tensor(ln_kept.rstd[:], ln_kept.var[:], ln_kept.power[:], ALU.pow).then_inc(kept_rstd_done, 1)
            root(LAST)

        @block.scalar
        def _(act):
            act.preload_act_table_set("silu_and_others")
            for c in range(DC):
                shared.x_round(act, TURNED, c)
            with act.Fori(0, LAST) as g:
                for u in range(Shared.U):
                    shared.gate(act, DONE + g, u)
                for c in range(DC):
                    shared.x_round(act, TURNED + g + 1, c)
            for u in range(Shared.U):
                shared.gate(act, DONE + LAST, u)

        @block.vector
        def _(dve):
            def weigh(res, y, w, done):
                for t in range(TILES):
                    dve.scalar_tensor_tensor(res[:, t], y[:, t], w(t), res[:, t], ALU.mult, ALU.add).then_inc(done, 1)

            def weigh_group(g):
                def w(k):
                    if isinstance(g, int):
                        return lambda t: rt.weight[:, k, TILES * g + t:TILES * g + t + 1]
                    return lambda t: rt.weight[:, k, bass.ds(TILES * g + t, 1)]

                dve.wait_ge(res_loaded, 16 * g + 16)
                dve.wait_ge(y_gathered, 2 * TILES * 16 * (g + 1))
                weigh(res, y[:, 0], w(0), add_step)
                dve.wait_ge(add_step, TILES * g + TILES)
                weigh(res, y[:, 1], w(1), y_read)
                dve.wait_ge(y_read, TILES * g + TILES)

            def finish(g):
                dve.wait_ge(shared.out_free, Shared.BANKS + TILES * (DONE + g) + TILES)
                moments(dve, res, ln, ln_step, (TILES + 6) * g, var_done)
                normalize(g)

            def normalize(g):
                dve.wait_ge(rstd_done, g + 1)
                for t in range(TILES):
                    dve.tensor_scalar(res[:, t], res[:, t], ln.mean[:, t:t + 1], ln.rstd[:, t:t + 1],
                                      ALU.subtract, ALU.mult).then_inc(out_ready, 1)

            def weight_kept(k):
                return lambda t: rt.weight[:, k, TILES * KEPT + t:TILES * KEPT + t + 1]

            for c in range(DC):
                shared.x_rest(dve, TURNED, c)
            with dve.Fori(0, LAST) as g:
                for u in range(Shared.U):
                    shared.up(dve, DONE + g, u)
                shared.x_rest(dve, TURNED + g + 1, 0)
                shared.x_rest(dve, TURNED + g + 1, 1)
                weigh_group(g)
                shared.add(dve, res, DONE + g, 0)
                shared.x_rest(dve, TURNED + g + 1, 2)
                shared.add(dve, res, DONE + g, 1)
                shared.x_rest(dve, TURNED + g + 1, 3)
                shared.add(dve, res, DONE + g, 2)
                shared.add(dve, res, DONE + g, 3)
                finish(g)
            for u in range(Shared.U):
                shared.up(dve, DONE + LAST, u)
                if u == 0:
                    dve.wait_ge(y_kept_gathered, 2 * TILES * 16)
                    weigh(kept, y_kept[:, 0], weight_kept(0), kept_step)
                if u == 1:
                    dve.wait_ge(kept_step, TILES)
                    weigh(kept, y_kept[:, 1], weight_kept(1), kept_step)
                if u == 2:
                    dve.wait_ge(kept_step, 2 * TILES)
                    moments(dve, kept, ln_kept, kept_ln_step, 0, kept_var_done)
                if u == 3:
                    dve.wait_ge(kept_rstd_done, 1)
                    for t in range(TILES):
                        dve.tensor_scalar(kept[:, t], kept[:, t], ln_kept.mean[:, t:t + 1], ln_kept.rstd[:, t:t + 1],
                                          ALU.subtract, ALU.mult).then_inc(kept_ready, 1)
            weigh_group(LAST)
            base = (TILES + 6) * LAST
            for t in range(TILES):
                shared.add(dve, res, DONE + LAST, t)
                dve.wait_ge(shared.out_free, Shared.BANKS + TILES * (DONE + LAST) + t + 1)
                moments_step(dve, res, ln, t, ln_step, base, var_done)
            for k in range(TILES, TILES + 3):
                moments_step(dve, res, ln, k, ln_step, base, var_done)
            normalize(LAST)

        @block.tensor
        def _(pe):
            def turn(n, c):
                if c == 0:
                    pe.wait_ge(xt_loaded, 16 * n)
                shared.turn(pe, xt, ident, TURNED + n, c)

            def hidden(n):
                for u in range(Shared.U):
                    shared.hidden(pe, DONE + n, u, x_done=TURNED + n if u == 0 else None)

            for c in range(DC):
                turn(0, c)
            with pe.Fori(0, LAST) as g:
                hidden(g)
                turn(g + 1, 0)
                turn(g + 1, 1)
                shared.down(pe, DONE + g, 0)
                turn(g + 1, 2)
                shared.down(pe, DONE + g, 1)
                turn(g + 1, 3)
                shared.down(pe, DONE + g, 2)
                shared.down(pe, DONE + g, 3)
            hidden(LAST)
            for t in range(TILES):
                shared.down(pe, DONE + LAST, t)


def program(nc, x_t, x_tok, w_in, w_out, conv_w, conv_b, gain, ctx_t, w_q, w_kv, w_o, w_router, we_gate_up, we_down,
            ws_gate_up, ws_down, out):
    x1 = nc.dram_tensor("x1", (GROUPS, P, TILES, D), F32, kind="Internal").ap()
    x2 = nc.dram_tensor("x2", (T, D), F32, kind="Internal").ap()
    y = nc.dram_tensor("y_slots", (E_TILES * SLOTS, D), F32, kind="Internal").ap()
    x2_tiles = x2.rearrange("(g t p) d -> g p t d", p=P, t=TILES)
    out_tiles = out.rearrange("(g b) (s p) d -> g p (b s) d", b=GB, p=P)
    with ExitStack() as ctx:
        def sb(name, shape, dt=F32):
            return ctx.enter_context(nc.sbuf_tensor("f_" + name, shape, dt))

        ident = sb("ident", [P, P])
        sums = sb("sums", [P, TILES, D])
        ln = Moments(sb, "attention", TILES)
        conv_ln = Moments(sb, "conv", TILES)
        x_next = sb("x_next", [P, TILES, D])
        with nc.sbuf_tensor("arena", [P, 2 * JC * DC * 2 * P], F32R) as arena, \
                nc.sbuf_tensor("ctx_next", [P, GT], F32) as ctx_next:
            cross = CrossWeights(arena[:], w_q, w_kv, w_o)
            gated_conv(nc, x_t, x_tok, w_in, w_out, conv_w, conv_b, gain, x1, arena[:], cross.units, sums, conv_ln, ident,
                       x_next, ctx_t, ctx_next)
            cross_attention(nc, x1, ctx_t, cross, x2_tiles, conv_ln, ident, x_next, ctx_next, sums, ln)
        rt = Routing(sb)
        kept = sums
        shared = Shared(sb, lambda name: ctx.enter_context(nc.semaphore(name)))
        raw = (sb("gate_up_raw", [P, DC, 2 * DE])[:], sb("down_raw", [P, len(E_UNITS), D])[:])
        xg = sb("x_gathered", [P, BLOCKS, D])
        route(nc, x2_tiles, w_router, sums, ln, ident, shared, ws_gate_up, ws_down, we_gate_up, we_down, raw, xg, x2,
              kept, x_next, rt)
        y_tile = sb("y_tile", [P, BLOCKS, D])
        y_stored = ctx.enter_context(nc.semaphore("y_stored"))
        experts(nc, x2, we_gate_up, we_down, y, ident, raw, xg, x2_tiles[0], x_next[:], y_tile, y_stored, rt)
        combine(nc, x2_tiles, y, out_tiles, ident, shared, kept, x_next, y_stored, rt)


def layouts(inputs):
    import numpy as np

    def get(name):
        return np.asarray(inputs["L0_" + name])

    def square(name):
        return get(name).T.reshape(2, 2, P, D).transpose(0, 2, 1, 3).reshape(2, P, 2 * D)

    def gate_up(gate, up, width):
        both = np.stack([get(gate), get(up)], axis=-2)
        lead = both.shape[:-3]
        both = both.reshape(*lead, DC, P, 2 * width)
        return np.swapaxes(both, -3, -2)

    def shared_gate_up():
        gate, up = get("ffn_Ws_gate"), get("ffn_Ws_up")
        both = np.concatenate([gate, up[:, DS - HALF:], up[:, :DS - HALF]], axis=1)
        return both.reshape(DC, P, 2 * DS).transpose(1, 0, 2)

    x = np.asarray(inputs["x"])
    ctx = np.asarray(inputs["ctx_512"])
    out = {
        "x_t": x.reshape(GROUPS, GT, DC, P).transpose(0, 3, 2, 1),
        "x_tok": x.reshape(GROUPS, TILES, P, D).transpose(0, 2, 1, 3),
        "w_in": get("attn_w_in").reshape(2, JC, P, DC, P).transpose(1, 4, 3, 0, 2).reshape(JC, P, 1024),
        "w_out": get("attn_w_out").reshape(D, JC // 2, 2, P).transpose(1, 3, 2, 0).reshape(JC // 2, P, 1024),
        "conv_w": get("attn_conv_w").reshape(JC, P, TAPS).transpose(1, 0, 2),
        "conv_b": get("attn_conv_b").reshape(JC, P).T,
        "gain": get("attn_D").reshape(JC, P).T,
        "ctx_t": ctx.reshape(GROUPS, GT, L).transpose(0, 2, 1),
        "w_q": square("xattn_Wq"),
        "w_kv": get("xattn_Wkv_expand").T,
        "w_o": square("xattn_Wout"),
        "w_router": get("ffn_W_router").reshape(DC, P, E_N).transpose(1, 0, 2),
        "we_gate_up": gate_up("ffn_We_gate", "ffn_We_up", DE),
        "we_down": get("ffn_We_down"),
        "ws_gate_up": shared_gate_up(),
        "ws_down": get("ffn_Ws_down"),
    }
    return {k: np.ascontiguousarray(v) for k, v in out.items()}


def kernel(**inputs):
    import concourse.bacc as bacc
    import numpy as np
    from concourse.bass_utils import run_bass_kernel_spmd

    nc = bacc.Bacc("TRN2", target_bir_lowering=False, num_devices=1)
    arrays = layouts(inputs)
    args = [nc.dram_tensor(name, a.shape, mybir.dt.from_np(a.dtype), kind="ExternalInput").ap()
            for name, a in arrays.items()]
    out = nc.dram_tensor("out", (B, S, D), F32, kind="ExternalOutput").ap()
    program(nc, *args, out)
    result = run_bass_kernel_spmd(nc, [arrays], core_ids=[0])
    return np.asarray(result.results[0]["out"])
```
